# Optimizing a Trainium2 kernel written in Bass

```python
import numpy as np
import jax
import jax.numpy as jnp

def _softmax(x, axis=-1):
    return jax.nn.softmax(x, axis=axis)

def _gelu(x):
    return jax.nn.gelu(x, approximate=True)

def _silu(x):
    return jax.nn.silu(x)

def _sigmoid(x):
    return jax.nn.sigmoid(x)

def _layernorm(x, axis=-1, eps=1e-05):
    m = jnp.mean(x, axis=axis, keepdims=True)
    v = jnp.var(x, axis=axis, keepdims=True)
    return (x - m) / jnp.sqrt(v + eps)

def _scatter_add(tgt, idx, src, axis=0):
    return tgt.at[idx].add(src)

def _segment_sum(src, seg, n):
    return jax.ops.segment_sum(src, seg, n)
kernel_name = 'mk_xattn_ffn_d1_seqx_r4_1df6cb'

def setup_inputs(seed: int=0):
    np.random.seed(seed)
    _w = jnp.asarray

    def _rec_inputs():
        import jax
        import jax.numpy as jnp
        _rk = jax.random.key(seed)
        x = -0.0002928 + 1 * jax.random.normal(jax.random.fold_in(_rk, 1), (8, 256, 256), jnp.float32)
        _lenS = 256 - jax.random.randint(jax.random.fold_in(_rk, 7), (8,), 0, max(1, 256 // 4) + 1, jnp.int32)
        _lenS2 = 256 - jax.random.randint(jax.random.fold_in(_rk, 8), (8,), 0, max(1, 256 // 4) + 1, jnp.int32)
        _ctx_1024P = jax.random.normal(jax.random.fold_in(_rk, 11), (8, 16, 256), jnp.float32)
        _ctx_1024c = jax.random.dirichlet(jax.random.fold_in(_rk, 511), 0.3 * jnp.ones((16,), jnp.float32), (8, 256))
        _ctx_1024t = jnp.einsum('bsk,bkd->bsd', _ctx_1024c, _ctx_1024P)
        _ctx_1024t = _ctx_1024t * jax.lax.rsqrt(jnp.mean(jnp.square(_ctx_1024t)) + 1e-12) * 0.953939
        ctx_1024 = -1.39393e-06 + 0.999914 * (_ctx_1024t + 0.3 * jax.random.normal(jax.random.fold_in(_rk, 611), (8, 256, 256), jnp.float32))
        return (x, ctx_1024)
    x, ctx_1024 = _rec_inputs()

    def _L0_xattn_setup():
        import jax, jax.numpy as jnp
        import numpy as np
        B, T, N_EMBD, N_HEAD = (2, 512, 256, 16)
        HEAD = N_EMBD // N_HEAD
        WINDOW = 64
        key = jax.random.key(seed)
        kq, kk, kv, kw = jax.random.split(key, 4)
        q = jax.random.normal(kq, (B, T, N_EMBD), dtype=jnp.float32)
        k = jax.random.normal(kk, (B, T, N_EMBD), dtype=jnp.float32)
        v = jax.random.normal(kv, (B, T, N_EMBD), dtype=jnp.float32)
        W_proj = jax.random.normal(kw, (N_EMBD, N_EMBD), dtype=jnp.float32) * (1.0 / np.sqrt(N_EMBD))
        b_proj = jnp.zeros((N_EMBD,), dtype=jnp.float32)
        return {'q': q, 'k': k, 'v': v, 'W_proj': W_proj, 'b_proj': b_proj}
    _L0_xattn_all = _L0_xattn_setup()
    _L0_xattn_in = {k: v for k, v in _L0_xattn_all.items() if k in ('W_proj', 'b_proj')}
    del _L0_xattn_all

    def _L0_ffn_setup():
        import jax, jax.numpy as jnp
        import numpy as np
        B, T, D, F, E, TOP_K = (2, 512, 256, 1024, 8, 2)
        INIT = 0.02
        key = jax.random.key(seed)
        k0, k1, k2, k3, k4 = jax.random.split(key, 5)
        x = jax.random.normal(k0, (B, T, D), dtype=jnp.float32)
        Wg = jax.random.normal(k1, (D, E), dtype=jnp.float32) * INIT
        W1 = jax.random.normal(k2, (E, D, F), dtype=jnp.float32) * INIT
        W3 = jax.random.normal(k3, (E, D, F), dtype=jnp.float32) * INIT
        W2 = jax.random.normal(k4, (E, F, D), dtype=jnp.float32) * INIT
        return {'x': x, 'Wg': Wg, 'W1': W1, 'W3': W3, 'W2': W2}
    _L0_ffn_all = _L0_ffn_setup()
    _L0_ffn_in = {k: v for k, v in _L0_ffn_all.items() if k in ('Wg', 'W1', 'W3', 'W2')}
    del _L0_ffn_all
    return {'x': x, 'ctx_1024': ctx_1024, 'L0_xattn_W_proj': _L0_xattn_in['W_proj'], 'L0_xattn_b_proj': _L0_xattn_in['b_proj'], 'L0_ffn_Wg': _L0_ffn_in['Wg'], 'L0_ffn_W1': _L0_ffn_in['W1'], 'L0_ffn_W3': _L0_ffn_in['W3'], 'L0_ffn_W2': _L0_ffn_in['W2']}

def reference(x, ctx_1024, L0_xattn_W_proj, L0_xattn_b_proj, L0_ffn_Wg, L0_ffn_W1, L0_ffn_W3, L0_ffn_W2):
    import jax
    import jax.numpy as jnp

    def _L0_xattn_ref(q, k, v, W_proj, b_proj):
        import jax, jax.numpy as jnp
        import numpy as np
        B, T, N_EMBD, N_HEAD = (2, 512, 256, 16)
        HEAD = N_EMBD // N_HEAD
        WINDOW = 64
        Bsz, Tlen, _ = q.shape
        qh = q.reshape(Bsz, Tlen, N_HEAD, HEAD).transpose(0, 2, 1, 3)
        kh = k.reshape(Bsz, Tlen, N_HEAD, HEAD).transpose(0, 2, 1, 3)
        vh = v.reshape(Bsz, Tlen, N_HEAD, HEAD).transpose(0, 2, 1, 3)
        scale = 1.0 / np.sqrt(HEAD)
        scores = jnp.einsum('bhqd,bhkd->bhqk', qh, kh) * scale
        idx = jnp.arange(Tlen)
        dist = jnp.abs(idx[None, :] - idx[:, None])
        scores = jnp.where(dist[None, None] > WINDOW, -jnp.inf, scores)
        attn = jax.nn.softmax(scores, axis=-1)
        y = jnp.einsum('bhqk,bhkd->bhqd', attn, vh)
        y = y.transpose(0, 2, 1, 3).reshape(Bsz, Tlen, N_EMBD)
        return y @ W_proj.T + b_proj

    def _L0_ffn_ref(x, Wg, W1, W3, W2):
        import jax, jax.numpy as jnp
        import numpy as np
        B, T, D, F, E, TOP_K = (2, 512, 256, 1024, 8, 2)
        INIT = 0.02
        Bb, Tt, Dd = x.shape
        xf = x.reshape(-1, Dd)
        logits = xf @ Wg
        top_v, top_i = jax.lax.top_k(logits, TOP_K)
        top_w = jax.nn.softmax(top_v, axis=-1)
        h1 = jnp.einsum('nd,edf->enf', xf, W1)
        h3 = jnp.einsum('nd,edf->enf', xf, W3)
        y = jnp.einsum('enf,efd->end', jax.nn.silu(h1) * h3, W2)
        y = jnp.transpose(y, (1, 0, 2))
        sel = jnp.take_along_axis(y, top_i[:, :, None], axis=1)
        out = jnp.sum(sel * top_w[:, :, None], axis=1)
        return out.reshape(Bb, Tt, Dd)
    x = x + _L0_xattn_ref(_layernorm(x, axis=-1), ctx_1024, ctx_1024, L0_xattn_W_proj, L0_xattn_b_proj)
    x = x + _L0_ffn_ref(_layernorm(x, axis=-1), L0_ffn_Wg, L0_ffn_W1, L0_ffn_W3, L0_ffn_W2)
    return x

_drawn_inputs = setup_inputs


def setup_inputs(seed=0):
    import zlib

    import numpy as np

    out = dict(_drawn_inputs(seed))
    spreads = {'L0_xattn_b_proj': (0.0, 0.1)}
    factors = {'L0_ffn_Wg': 3.208, 'L0_ffn_W1': 2.768, 'L0_ffn_W3': 2.734, 'L0_ffn_W2': 2.737}
    for name, (base, spread) in spreads.items():
        noise = np.random.default_rng([zlib.crc32(name.encode()), seed]).standard_normal(out[name].shape)
        drawn = base * np.exp(spread * noise) if base else spread * noise
        out[name] = jnp.asarray(drawn.astype(out[name].dtype))
    for name, factor in factors.items():
        out[name] = (out[name] * factor).astype(out[name].dtype)
    return out
```

```python
from contextlib import ExitStack

import concourse.bass as bass
from concourse import mybir

B, T, D = 8, 256, 256
P = 128
N_TOK = B * T
N_TILE = N_TOK // P
H, HD = 16, 16
WIN = 64
NKB = T // WIN
SPAN = 3 * WIN
NC = D // P
NPAIR = H // 2
E, F_DIM = 8, 1024
N_ASSIGN = 2 * N_TOK
N_CHOICE = 2 * N_TILE
N_SLOT_TILE = (N_ASSIGN + E * P - 1) // P
SLOT_COLS = N_SLOT_TILE + 1
NF = F_DIM // P
HALF = F_DIM // 2
MAT = 2 * 2 * F_DIM
UNROLL = 3
PAD_ROWS = P
EPS = 1e-5
MASKED = -1e30
NIT = 4
SPT = 16
BASE = 64


def attention_and_experts(nc, x, ctx, w_proj, b_proj, wg, w1, w3, w2, out, xn_rows):
    F32, F32R, BF16, I32 = mybir.dt.float32, mybir.dt.float32r, mybir.dt.bfloat16, mybir.dt.int32
    ALU, ACT, AX = mybir.AluOpType, mybir.ActivationFunctionType, mybir.AxisListType

    x_t = x.rearrange("b (q p) d -> (b q) p d", p=P)
    ctx_t = ctx.rearrange("b (q p) d -> (b q) p d", p=P)
    ctx_v = ctx.rearrange("b (j p) d -> b p j d", p=WIN)
    out_t = out.rearrange("(t p) d -> t p d", p=P)
    xn_t = xn_rows.rearrange("(t p) d -> t p d", p=P)

    with ExitStack() as stack:
        sem_names = []

        def sem(name):
            s = stack.enter_context(nc.semaphore(name))
            return s

        place = {"at": (nc.sbuf_base + 63) // 64 * 64}

        def sb(name, shape, dt):
            size = 1
            for n in shape[1:]:
                size *= n
            size *= 2 if dt == BF16 else 4
            t = nc.alloc_sbuf_tensor_at(name, shape, dt, offset=place["at"])
            place["at"] += (size + 63) // 64 * 64
            return t

        def pb(name, shape, dt):
            return stack.enter_context(nc.psum_tensor(name, shape, dt))

        ident = sb("ident", [P, P], F32)
        ident_bf = sb("ident_bf", [P, P], BF16)
        mask = sb("mask", [P, 2, SPAN], BF16)
        head_sel = sb("head_sel", [H, NC, P], F32)
        ones_row = sb("ones_row", [1, P], F32)
        bias_row = sb("bias_row", [1, D], F32)
        neg_half = sb("neg_half", [P, 1], F32)
        w_nat = sb("w_nat", [P, NC, D], F32)
        w_T = sb("w_T", [P, NC, D], F32)
        wg_s = sb("wg_s", [P, NC, E], F32)
        logits = sb("logits", [P, N_TILE, E], F32)

        iota_e = sb("iota_e", [P, E], F32)
        iota_slot = sb("iota_slot", [P, P], F32)
        iota_tile = sb("iota_tile", [P, SLOT_COLS], F32)
        token_id = sb("token_id", [P, N_TILE], F32)
        part_id = sb("part_id", [P, 1], F32)
        before = sb("before", [P, P], F32)
        ones = sb("ones", [P, P], F32)

        slot_tok = sb("slot_tok", [P, SLOT_COLS], I32)
        slot_gate = sb("slot_gate", [P, SLOT_COLS], F32)
        tile_tab = sb("tile_tab", [P, 4, SLOT_COLS], I32)
        raw = [sb(f"raw{m}", [P, 2 * F_DIM], F32) for m in range(3)]
        wts = sb("wts", [P, 2, 3, MAT], F32R)
        behind_first = place["at"] - 3 * MAT * 4
        behind_wts = place["at"]

        place["at"] = behind_first
        k_in = [sb(f"k_in{q}", [P, D], F32) for q in range(2)]
        x_in = [sb(f"x_in{q}", [P, D], F32) for q in range(2)]
        v_in = sb("v_in", [P, NKB, D], F32)
        v_bd = [sb(f"v_bd{u}", [P, NKB, NPAIR, 2 * HD], F32) for u in range(2)]
        q_ln = [sb(f"q_ln{q}", [P, D], F32) for q in range(2)]
        k_parts = [sb(f"k_parts{q}", [P, H, 4, HD], F32) for q in range(2)]
        q_parts = [sb(f"q_parts{q}", [P, H, 4, HD], F32) for q in range(2)]
        kT = [sb(f"kT{u}", [P, NPAIR, T], F32R) for u in range(2)]
        qT = [sb(f"qT{u}", [P, NPAIR, T], F32R) for u in range(2)]
        neg_max = [sb(f"neg_max{g}", [P, 4], F32) for g in range(2)]
        probs = [sb(f"probs{g}", [P, 2, 3, 2, WIN], F32) for g in range(2)]
        probs_T = [sb(f"probs_T{g}", [P, 2, 3, P], F32) for g in range(2)]
        sums = [sb(f"sums{g}", [P, H], F32) for g in range(2)]
        rsum = sb("rsum", [P, H], F32)
        rsum_T = sb("rsum_T", [H, P], F32)
        y_raw = sb("y_raw", [P, NC, P], F32)
        y_norm = sb("y_norm", [P, NC, P], F32)
        x_res = [sb(f"x_res{q}", [P, D], F32) for q in range(2)]
        x2 = [sb(f"x2_{q}", [P, D], F32) for q in range(2)]
        xn = [sb(f"xn_{q}", [P, D], F32) for q in range(2)]
        xn_T = sb("xn_T", [P, NC, P], F32)
        zero_rows = sb("zero_rows", [P, D], F32)
        st1 = sb("st1", [P, 6], F32)
        mv1 = sb("mv1", [P, 2], F32)
        ve1 = sb("ve1", [P, 1], F32)
        rstd1 = sb("rstd1", [P, 1], F32)
        st2 = sb("st2", [P, 6], F32)
        mv2 = sb("mv2", [P, 2], F32)
        ve2 = sb("ve2", [P, 1], F32)
        rstd2 = sb("rstd2", [P, 1], F32)

        assert place["at"] <= nc.sbuf_usable_end

        place["at"] = behind_wts

        def table(name, *shape, dt=F32):
            return sb(name, [P, *shape], dt)

        best = table("best", 2, N_TILE)
        choice = table("choice", 2, N_TILE, E)
        same = table("same", N_TILE, E)
        cand = table("cand", N_TILE, E)
        first = table("first", N_TILE)
        rest = table("rest", N_TILE, E)
        chosen = table("chosen", N_TILE, E)
        total = table("total", N_TILE, E)
        upto = [table(f"upto{n}", N_TILE, E) for n in range(5)]
        earlier = table("earlier", N_TILE, E)
        place_e = table("place_e", N_TILE, E)
        picked = table("picked", 2, N_TILE, E)
        tiles_i = table("tiles_i", E, dt=I32)
        tiles_s = table("tiles_s", E, dt=I32)
        tiles_f = table("tiles_f", E)
        cum = [table(f"cum{n}", E) for n in range(4)]
        tile0 = table("tile0", E)
        pos = table("pos", N_CHOICE)
        pos_i = table("pos_i", N_CHOICE, dt=I32)
        row_i = table("row_i", N_CHOICE, dt=I32)
        til_i = table("til_i", N_CHOICE, dt=I32)
        row_f = table("row_f", N_CHOICE)
        til_f = table("til_f", N_CHOICE)
        tok_v = table("tok_v", N_CHOICE)
        diff = table("diff", N_TILE)
        ex = table("ex", N_TILE)
        gates = table("gates", N_CHOICE)
        gate_hi = table("gate_hi", N_CHOICE, dt=F32R)
        gate_lo = table("gate_lo", N_CHOICE)
        row_hot = table("row_hot", N_CHOICE, P, dt=F32R)
        til_hot = table("til_hot", N_CHOICE, SLOT_COLS)
        slot_vals = table("slot_vals", N_CHOICE, 3, SLOT_COLS, dt=F32R)
        ge_tile = table("ge_tile", SLOT_COLS, E - 1)
        tile_e = table("tile_e", SLOT_COLS + 1)
        tile_new = table("tile_new", SLOT_COLS)
        gate_part = table("gate_part", SLOT_COLS)
        tab_f = table("tab_f", 4, SLOT_COLS)
        assert place["at"] <= nc.sbuf_usable_end

        gather_row = [table(f"gather_row{n}", 1, dt=I32) for n in range(UNROLL)]
        add_row = [table(f"add_row{n}", 1, dt=I32) for n in range(UNROLL)]
        xg = [table(f"xg{n}", D) for n in range(UNROLL)]
        place["at"] = behind_wts
        xT = [table(f"xT{n}", 2, NC, P, dt=F32R) for n in range(UNROLL)]
        gated = table("gated", F_DIM)
        hidden = table("hidden", F_DIM)
        hT = [table(f"hT{n}", 2, NF, P, dt=F32R) for n in range(UNROLL)]
        y_small = table("y_small", D)
        y_out = [table(f"y_out{n}", D) for n in range(UNROLL)]

        ps = pb("ps", [P, 8, 512], F32)
        ps_s = ps[:, 0:4, :].rearrange("p (g e) c -> p g e c", g=2)
        ps_pt = ps[:, 4:6, :]
        ps_y = ps[:, 6, 0:D].rearrange("p (c t) -> p c t", c=NC)
        ps_m = ps[:, 7, :]
        ps_h = ps[:, 0:4, :].rearrange("p (m a) c -> p m a c", m=2)
        ps_hT = ps[:, 4:6, :]
        ps_out = ps[:, 6, :]
        ps_xT = ps[:, 7, :]

        PE_SEMS = ["scores_done", "ptrans_done", "pv_done", "parts_T_done", "rsum_T_done", "rbc_done",
                   "proj_done", "xn_T_ps_done", "logits_done", "w_T_ps_done",
                   "rank_done", "slots_done", "x_turned", "h1_done", "h3_done", "h_turned", "out_done"]
        DVE_SEMS = ["max_done", "pt0_copied", "partsT0_copied", "q_ln_done", "ln1_stats", "rsum_done",
                    "rsum_T_copied", "y_norm_done", "x2_done", "ln2_stats", "xn_done", "xn_T_copied", "logits_copied",
                    "w_T_copied", "route_link", "diff_done", "chosen_done", "hots_done", "tables_done",
                    "xT_lo_done", "hidden_done", "hT_lo_done", "y_done", "ln1_link", "ln2_link", "dve_waited"]
        ACT_SEMS = ["exp_done", "pt1_copied", "partsT1_copied", "hi_done", "v_bd_done", "y_raw_done", "ex_done",
                    "silu_done", "xT_hi_done", "hT_hi_done", "y_small_done", "w_hi_done"]
        POOL_SEMS = ["lo_done", "rstd1_done", "rstd2_done", "consts_done", "pool_link", "w_lo_done",
                     "rows_read", "adds_landed", "pool_waited"]
        S = {n: sem(n) for n in PE_SEMS + DVE_SEMS + ACT_SEMS + POOL_SEMS}
        DMA_SEMS = ["k_in0", "k_in1", "x_in0", "x_in1", "v_in", "x_res0", "x_res1", "weights_in",
                    "x2_out0", "x2_out1", "xn_out0", "xn_out1", "zero_out",
                    "raw0", "raw1", "raw2"]
        POOL_DMA_SEMS = ["xg0", "xg1", "xg2", "added"]
        L = {n: sem("dma_" + n) for n in DMA_SEMS + POOL_DMA_SEMS}

        def start(eng, names):
            for n in names:
                eng.sem_inc(S[n], BASE)

        def times(count):
            return count + BASE

        def landed(count):
            return count * 16 + BASE

        def within(value, low, high):
            return nc.s_assert_within(value, low, high, skip_runtime_bounds_check_because=
                                      "the If around it leaves the loop's register in this range")

        def lagged(eng, i, s, lag, task):
            if s >= lag:
                task(i, s - lag)
            else:
                with eng.If(i > 0):
                    task(within(i - 1, 0, NIT - 2), s - lag + SPT)

        def last_of_tile(s, lag):
            return (s - lag) % 4 == 3

        def tile_of(i, s):
            return i * 4 + s // 4

        def turns(eng, step, depth):
            with eng.Fori(0, NIT) as i:
                for s in range(SPT):
                    step(i, s)
            for s in range(SPT, SPT + depth):
                step(None, s)

        def lag_task(eng, i, s, lag, task):
            if i is None:
                if s - lag < SPT:
                    task(NIT - 1, s - lag)
            else:
                lagged(eng, i, s, lag, task)

        DEPTH = 8

        def prep(eng, i, s, task):
            if i is None:
                return
            u, k = s // 8, s % 8
            if u == 0 and k == 0:
                with eng.If(i > 0):
                    task(i * 2, 8, 0)
            elif k == 0:
                task(i * 2 + 1, 8, 1)
            elif u == 0:
                task(i * 2 + 1, k, 1)
            else:
                with eng.If(i < NIT - 1):
                    task(within(i * 2 + 2, 2, B - 2), k, 0)

        def prep0(eng, i, s, task):
            if i is None:
                return
            u, k = s // 8, s % 8
            if u == 0:
                task(i * 2 + 1, k, 1)
            else:
                with eng.If(i < NIT - 1):
                    task(within(i * 2 + 2, 2, B - 2), k, 0)

        block = stack.enter_context(nc.Block())

        @block.sync
        def _(sp):
            for n in DMA_SEMS:
                sp.sem_inc(L[n], BASE)

            def load_item(b, m):
                if m < 2:
                    sp.wait_ge(S["lo_done"], times((b - 1) * 4 + m + 1))
                    sp.dma_start(k_in[m][:, :], ctx_t[b * 2 + m, :, :]).then_inc(L[f"k_in{m}"], 16)
                else:
                    sp.wait_ge(S["q_ln_done"], times((b - 1) * 2 + m - 1))
                    sp.dma_start(x_in[m - 2][:, :], x_t[b * 2 + m - 2, :, :]).then_inc(L[f"x_in{m - 2}"], 16)

            def load_v(b):
                sp.wait_ge(S["v_bd_done"], times(b * 2))
                for half in range(2):
                    sp.dma_start(v_in[WIN * half:WIN * half + WIN, :, :], ctx_v[b, :, :, :])\
                        .then_inc(L["v_in"], 16)

            for m in range(4):
                load_item(0, m)
            load_v(0)
            sp.dma_start(w_nat[:, :, :], w_proj.rearrange("(c p) d -> p c d", p=P)).then_inc(L["weights_in"], 16)
            sp.dma_start(bias_row[:, :], b_proj.rearrange("(a n) -> a n", a=1)).then_inc(L["weights_in"], 16)
            sp.dma_start(wg_s[:, :, :], wg.rearrange("(c p) e -> p c e", p=P)).then_inc(L["weights_in"], 16)
            for m in range(3):
                load_item(1, m)
            w_dram = [w1.rearrange("e (c p) f -> e p c f", p=P), w3.rearrange("e (c p) f -> e p c f", p=P),
                      w2.rearrange("e (c p) n -> e p c n", p=P)]

            def load_expert(e, m):
                c = NC if m < 2 else NF
                sp.dma_start(raw[m][:, :].rearrange("p (c n) -> p c n", c=c), w_dram[m][e, :, :, :])\
                    .then_inc(L[f"raw{m}"], 16)

            for m in range(3):
                load_expert(0, m)
            sp.wait_ge(S["consts_done"], times(1))
            sp.dma_start(out_t[N_TILE, :, :], zero_rows[:, :]).then_inc(L["zero_out"], 16)
            sp.dma_start(xn_t[N_TILE, :, :], zero_rows[:, :]).then_inc(L["zero_out"], 16)

            def store_x2(i, s):
                t, q = tile_of(i, s), (s // 4) % 2
                sp.wait_ge(S["x2_done"], times(t + 1))
                sp.dma_start(out_t[t, :, :], x2[q][:, :]).then_inc(L[f"x2_out{q}"], 16)

            def store_xn(i, s):
                t, q = tile_of(i, s), (s // 4) % 2
                sp.wait_ge(S["xn_done"], times(t + 1))
                sp.dma_start(xn_t[t, :, :], xn[q][:, :]).then_inc(L[f"xn_out{q}"], 16)

            def step(i, s):
                if i is not None:
                    u, k = s // 8, s % 8
                    if k in (2, 4, 6):
                        with sp.If(i < NIT - 1):
                            load_item(within(i * 2 + (u + 2), u + 2, B - 2 + u), k // 2 - 1)
                    if k == 0:
                        if u == 0:
                            load_item(i * 2 + 1, 3)
                            load_v(i * 2 + 1)
                        else:
                            with sp.If(i < NIT - 1):
                                nxt = within(i * 2 + 2, 2, B - 2)
                                load_item(nxt, 3)
                                load_v(nxt)
                    if s % 4 == 3:
                        t, q = tile_of(i, s), (s // 4) % 2
                        sp.wait_ge(S["x2_done"], times(t - 1))
                        sp.dma_start(x_res[q][:, :], x_t[t, :, :]).then_inc(L[f"x_res{q}"], 16)
                if last_of_tile(s, 4):
                    lag_task(sp, i, s, 4, store_x2)
                if last_of_tile(s, 5):
                    lag_task(sp, i, s, 5, store_xn)

            turns(sp, step, DEPTH)
            with sp.Fori(1, E) as e:
                for m in range(3):
                    sp.wait_ge(S["w_hi_done"], times((e - 1) * 3 + m + 1))
                    sp.wait_ge(S["w_lo_done"], times((e - 1) * 3 + m + 1))
                    load_expert(e, m)
            for n in ("x2_out0", "x2_out1", "xn_out0", "xn_out1"):
                sp.wait_ge(L[n], landed(N_TILE // 2))
            sp.wait_ge(L["zero_out"], landed(2))
            sp.wait_ge(L["added"], N_SLOT_TILE * 16)

        @block.gpsimd
        def _(pool):
            start(pool, POOL_SEMS)
            pool.memset(ident[:, :], 0.0).then_inc(S["pool_link"], 1)
            pool.memset(ident_bf[:, :], 0.0).then_inc(S["pool_link"], 1)
            pool.memset(mask[:, :, :], 0.0).then_inc(S["pool_link"], 1)
            pool.memset(head_sel[:, :, :], 1.0).then_inc(S["pool_link"], 1)
            pool.memset(ones_row[:, :], 1.0).then_inc(S["pool_link"], 1)
            pool.memset(neg_half[:, :], -0.5).then_inc(S["pool_link"], 1)
            for u in range(2):
                pool.memset(v_bd[u][:, :, :, :], 0.0).then_inc(S["pool_link"], 1)
            pool.memset(zero_rows[:, :], 0.0).then_inc(S["pool_link"], 1)
            pool.wait_ge(S["pool_link"], times(9))
            for m in (ident, ident_bf):
                pool.affine_select(out=m[:, :], in_=m[:, :], compare_op=ALU.not_equal, fill=1.0, base=0,
                                   pattern=[[-1, P]], channel_multiplier=1).then_inc(S["pool_link"], 1)
            for q in range(2):
                pool.affine_select(out=mask[:, q, :], in_=mask[:, q, :], compare_op=ALU.is_ge, fill=MASKED,
                                   base=WIN + WIN * q, pattern=[[-1, SPAN]], channel_multiplier=1)\
                    .then_inc(S["pool_link"], 1)
            pool.wait_ge(S["pool_link"], times(13))
            for q in range(2):
                pool.affine_select(out=mask[:, q, :], in_=mask[:, q, :], compare_op=ALU.is_ge, fill=MASKED,
                                   base=WIN - WIN * q, pattern=[[1, SPAN]], channel_multiplier=-1)\
                    .then_inc(S["pool_link"], 1)
            pool.affine_select(out=head_sel[:, :, :], in_=head_sel[:, :, :], compare_op=ALU.is_ge, fill=0.0,
                               base=0, pattern=[[P, NC], [1, P]], channel_multiplier=-HD)\
                .then_inc(S["pool_link"], 1)
            pool.wait_ge(S["pool_link"], times(16))
            pool.affine_select(out=head_sel[:, :, :], in_=head_sel[:, :, :], compare_op=ALU.is_ge, fill=0.0,
                               base=HD - 1, pattern=[[-P, NC], [-1, P]], channel_multiplier=HD)\
                .then_inc(S["pool_link"], 1)
            pool.wait_ge(S["pool_link"], times(17))
            pool.nop().then_inc(S["consts_done"], 1)

            def count(out, pattern, base, per_partition):
                pool.iota(out, pattern, base=base, channel_multiplier=per_partition,
                          allow_small_or_imprecise_dtypes=True).then_inc(S["pool_link"], 1)

            count(iota_e[:, :], [[1, E]], 0, 0)
            count(iota_slot[:, :], [[1, P]], 0, 0)
            count(iota_tile[:, :], [[1, SLOT_COLS]], 0, 0)
            count(token_id[:, :], [[P, N_TILE]], 0, 1)
            count(part_id[:, :], [[1, 1]], N_TOK, 1)
            pool.memset(before[:, :], 1.0).then_inc(S["pool_link"], 1)
            pool.memset(ones[:, :], 1.0).then_inc(S["pool_link"], 1)
            pool.wait_ge(S["pool_link"], times(24))
            pool.affine_select(out=before[:, :], in_=before[:, :], compare_op=ALU.is_gt, fill=0.0, base=0,
                               pattern=[[1, P]], channel_multiplier=-1).then_inc(S["pool_link"], 1)
            pool.wait_ge(S["pool_link"], times(25))
            pool.nop().then_inc(S["consts_done"], 1)

            def lo_parts(b, m, u):
                q = m % 2
                pool.wait_ge(S["hi_done"], times(b * 4 + m + 1))
                if m < 2:
                    src, dst, sl, hi = k_in[q], k_parts[q], slice(1, 4, 2), 0
                else:
                    src, dst, sl, hi = q_ln[q], q_parts[q], slice(2, 4), 0
                for at in range(*sl.indices(4)):
                    ins = pool.tensor_tensor(dst[:, :, at, :].bitcast(F32R),
                                             src[:, :].rearrange("p (h d) -> p h d", h=H),
                                             dst[:, :, hi, :], ALU.subtract)
                ins.then_inc(S["lo_done"], 1)

            def rstd1_task(b, q):
                pool.wait_ge(S["ln1_stats"], times(b * 2 + q + 1))
                pool.tensor_tensor(rstd1[:, :], ve1[:, :], neg_half[:, :], ALU.pow).then_inc(S["rstd1_done"], 1)

            def rstd2_task(i, s):
                t = tile_of(i, s)
                pool.wait_ge(S["ln2_stats"], times(t + 1))
                pool.tensor_tensor(rstd2[:, :], ve2[:, :], neg_half[:, :], ALU.pow).then_inc(S["rstd2_done"], 1)

            lo_parts(0, 0, 0)
            lo_parts(0, 1, 0)
            rstd1_task(0, 0)
            lo_parts(0, 2, 0)
            rstd1_task(0, 1)
            lo_parts(0, 3, 0)
            def step(i, s):
                def task(b, k, u):
                    lo_parts(b, k // 2, u)
                    if k in (2, 4):
                        rstd1_task(b, k // 2 - 1)
                if s % 2 == 0:
                    prep0(pool, i, s, task)
                if last_of_tile(s, 4):
                    lag_task(pool, i, s, 4, rstd2_task)

            turns(pool, step, DEPTH)

            def w_lo(e, slot, m):
                pool.wait_ge(S["w_hi_done"], times(e * 3 + m + 1))
                pool.wait_ge(S["pool_link"], times(25))
                part = wts[:, slot, m, :]
                if m < 2:
                    hi, lo, src = part[:, 0:MAT // 2], part[:, MAT // 2:MAT], raw[m][:, :]
                else:
                    both = part.rearrange("p (c a n) -> p c a n", c=NF, a=2)
                    hi, lo = both[:, :, 0, :], both[:, :, 1, :]
                    src = raw[m][:, :].rearrange("p (c n) -> p c n", c=NF)
                pool.tensor_tensor(lo, src, hi.bitcast(F32), ALU.subtract).then_inc(S["w_lo_done"], 1)

            for m in range(3):
                w_lo(0, 0, m)
            pool.wait_ge(S["tables_done"], times(1))
            for n in range(2):
                pool.wait_ge(L[f"xn_out{n}"], landed(N_TILE // 2))
                pool.wait_ge(L[f"x2_out{n}"], landed(N_TILE // 2))
            pool.wait_ge(L["zero_out"], landed(2))

            def gather(t, n):
                pool.tensor_copy(gather_row[n][:, :], slot_tok[:, bass.ds(t, 1)]).then_inc(S["rows_read"], 1)
                pool.wait_ge(S["rows_read"], times(t + 1))
                pool.wait_ge(S["x_turned"], times(t - 2))
                pool.nop().then_inc(S["pool_waited"], 1)
                pool.indirect_dma_start(xg[n][:, :], None, xn_rows, bass.IndirectOffsetOnAxis(gather_row[n][:, :], 0),
                                        bounds_check=N_TOK + PAD_ROWS - 1).then_inc(L[f"xg{n}"], 16)

            def add(t, n):
                pool.wait_ge(S["y_done"], times(t + 1))
                pool.nop().then_inc(S["adds_landed"], 1)
                pool.tensor_copy(add_row[n][:, :], slot_tok[:, bass.ds(t, 1)]).then_inc(S["pool_link"], 1)
                pool.wait_ge(S["pool_link"], times(t + 26))
                pool.nop().then_inc(S["pool_waited"], 1)
                pool.indirect_dma_start(out, bass.IndirectOffsetOnAxis(add_row[n][:, :], 0), y_out[n][:, :], None,
                                        bounds_check=N_TOK + PAD_ROWS - 1, compute_op=ALU.add)\
                    .then_inc(L["added"], 16)

            def convert(t):
                is_first = pool.value_load(tile_tab[0:1, 2, bass.ds(t, 1)], min_val=0, max_val=1)
                with pool.If(is_first > 0):
                    expert = pool.value_load(tile_tab[0:1, 0, bass.ds(t, 1)], min_val=0, max_val=E - 2)
                    to = pool.value_load(tile_tab[0:1, 3, bass.ds(t, 1)], min_val=0, max_val=1)
                    for m in range(3):
                        w_lo(expert + 1, to, m)

            for n in range(UNROLL):
                gather(n, n)
            convert(0)
            with pool.Fori(0, N_SLOT_TILE // UNROLL) as i:
                for n in range(UNROLL):
                    t = i * UNROLL + n
                    with pool.If(i < N_SLOT_TILE // UNROLL - 1):
                        gather(within(t + UNROLL, UNROLL, N_SLOT_TILE - 1), n)
                    if n < UNROLL - 1:
                        convert(t + 1)
                    else:
                        with pool.If(i < N_SLOT_TILE // UNROLL - 1):
                            convert(within(t + 1, UNROLL, N_SLOT_TILE - 1))
                    pool.wait_ge(L["added"], i * (UNROLL * 16) + 16 * n)
                    add(t, n)

        @block.scalar
        def _(act):
            start(act, ACT_SEMS)

            def hi_parts(b, m):
                q = m % 2
                act.wait_ge(S["parts_T_done"], times((b - 1) * 8 + 2 * m + 2))
                if m < 2:
                    act.wait_ge(L[f"k_in{q}"], landed(b + 1))
                    src, dst = k_in[q], k_parts[q][:, :, 0:4:2, :]
                else:
                    act.wait_ge(S["q_ln_done"], times(b * 2 + q + 1))
                    src, dst = q_ln[q], q_parts[q][:, :, 0:2, :]
                src = src[:, :].rearrange("p (h d) -> p h d", h=H).unsqueeze(2).broadcast_to([P, H, 2, HD])
                act.activation(dst.bitcast(F32R), src, ACT.Copy).then_inc(S["hi_done"], 1)

            def copy_parts_T(b, k, u):
                m, q = k // 2 - 1, (k // 2 - 1) % 2
                act.wait_ge(S["parts_T_done"], times(b * 8 + k))
                dst = (kT if m < 2 else qT)[u]
                act.activation(dst[:, 4:8, P * q:P * q + P], ps_m[:, :].rearrange("p (r t) -> p r t", r=4),
                               ACT.Copy).then_inc(S["partsT1_copied"], 1)

            def spread_v(b, u):
                act.wait_ge(L["v_in"], landed((b + 1) * 2))
                act.wait_ge(S["consts_done"], times(1))
                act.wait_ge(S["pv_done"], times((b - 1) * 8))
                for par in range(2):
                    lo = WIN * par
                    src = v_in[lo:lo + WIN, :, :].rearrange("p j (r e d) -> p j r e d", e=2, d=HD)
                    act.activation(v_bd[u][lo:lo + WIN, :, :, HD * par:HD * par + HD], src[:, :, :, par, :], ACT.Copy)\
                        .then_inc(S["v_bd_done"], 1)

            def exps(i, s):
                g, w = s % 2, (s // 4) % 2
                n = i * SPT + s
                act.wait_ge(S["max_done"], times(n + 1))
                act.wait_ge(S["ptrans_done"], times(n - 1))
                if s % 4 == 0:
                    act.wait_ge(S["rsum_done"], times(tile_of(i, s) - 1))
                for par in range(2):
                    for r in range(2):
                        h = 2 * (2 * (s % 4) + r) + par
                        ins = act.activation(
                            probs[g][:, r, :, par, :],
                            ps_s[:, g, par, SPAN * r:SPAN * r + SPAN].rearrange("p (j c) -> p j c", j=3),
                            ACT.Exp, bias=neg_max[g][:, 2 * par + r:2 * par + r + 1],
                            accum_out=sums[w][:, h:h + 1])
                ins.then_inc(S["exp_done"], 1)

            def copy_pt1(i, s):
                g, n = s % 2, i * SPT + s
                act.wait_ge(S["ptrans_done"], times(n + 1))
                act.wait_ge(S["pv_done"], times(n - 1))
                act.activation(probs_T[g][:, 1, :, :], ps_pt[:, 1, 0:3 * P].rearrange("p (j q) -> p j q", j=3),
                               ACT.Copy).then_inc(S["pt1_copied"], 1)

            def copy_y(i, s):
                t = tile_of(i, s)
                act.wait_ge(S["pv_done"], times(i * SPT + s + 1))
                act.wait_ge(S["y_norm_done"], times(t))
                act.activation(y_raw[:, :, :], ps_y[:, :, :], ACT.Copy).then_inc(S["y_raw_done"], 1)

            for m in range(4):
                hi_parts(0, m)
                copy_parts_T(0, 2 * m + 2, 0)
            spread_v(0, 0)

            def step(i, s):
                if s % 2 == 0:
                    prep(act, i, s, copy_parts_T)
                    prep0(act, i, s, lambda b, k, u: hi_parts(b, k // 2))
                if i is not None:
                    exps(i, s)
                lag_task(act, i, s, 1, copy_pt1)
                if last_of_tile(s, 2):
                    lag_task(act, i, s, 2, copy_y)
                if s % 8 == 7:
                    prep0(act, i, s, lambda b, k, u: spread_v(b, u))

            turns(act, step, DEPTH)

            def w_hi(e, slot, m):
                act.wait_ge(L[f"raw{m}"], landed(e + 1))
                part = wts[:, slot, m, :]
                if m < 2:
                    act.copy(part[:, 0:MAT // 2], raw[m][:, :]).then_inc(S["w_hi_done"], 1)
                else:
                    act.copy(part.rearrange("p (c a n) -> p c a n", c=NF, a=2)[:, :, 0, :],
                             raw[m][:, :].rearrange("p (c n) -> p c n", c=NF)).then_inc(S["w_hi_done"], 1)

            for m in range(3):
                w_hi(0, 0, m)
            act.wait_ge(S["diff_done"], times(1))
            act.activation(ex[:, :], diff[:, :], ACT.Exp).then_inc(S["ex_done"], 1)

            def x_hi(t, n):
                act.wait_ge(S["x_turned"], times(t + 1))
                act.wait_ge(S["h3_done"], times((t - 2) * 2))
                act.activation(xT[n][:, 0, :, :], ps_xT[:, 0:D].rearrange("p (c t) -> p c t", c=NC),
                               ACT.Copy).then_inc(S["xT_hi_done"], 1)

            def y_low(t):
                act.wait_ge(S["out_done"], times(t + 1))
                act.wait_ge(S["y_done"], times(t))
                act.activation(y_small[:, :], ps_out[:, D:2 * D], ACT.Copy, scale=slot_gate[:, bass.ds(t, 1)])\
                    .then_inc(S["y_small_done"], 1)

            def convert(t, m):
                is_first = act.value_load(tile_tab[0:1, 2, bass.ds(t, 1)], min_val=0, max_val=1)
                with act.If(is_first > 0):
                    expert = act.value_load(tile_tab[0:1, 0, bass.ds(t, 1)], min_val=0, max_val=E - 2)
                    to = act.value_load(tile_tab[0:1, 3, bass.ds(t, 1)], min_val=0, max_val=1)
                    if m < 2:
                        act.wait_ge(S["h3_done"], times(t * 2))
                    else:
                        act.wait_ge(S["out_done"], times(t))
                    w_hi(expert + 1, to, m)

            act.wait_ge(S["tables_done"], times(1))
            x_hi(0, 0)
            with act.Fori(0, N_SLOT_TILE // UNROLL) as i:
                for n in range(UNROLL):
                    t = i * UNROLL + n
                    for a in range(2):
                        act.wait_ge(S["h1_done"], times(t * 2 + a + 1))
                        act.wait_ge(S["hidden_done"], times((t - 1) * 2 + a + 1))
                        act.activation(gated[:, HALF * a:HALF * a + HALF], ps_h[:, 0, a, :], ACT.Silu)\
                            .then_inc(S["silu_done"], 1)
                        if a == 0:
                            convert(t, 0)
                    if n < UNROLL - 1:
                        x_hi(t + 1, n + 1)
                    else:
                        with act.If(i < N_SLOT_TILE // UNROLL - 1):
                            x_hi(t + 1, 0)
                    convert(t, 1)
                    if n == 0:
                        with act.If(i > 0):
                            y_low(within(t - 1, 2, N_SLOT_TILE - 2))
                    else:
                        y_low(t - 1)
                    for a in range(2):
                        act.wait_ge(S["h_turned"], times(t * 2 + a + 1))
                        act.wait_ge(S["out_done"], times(t - 2))
                        act.activation(hT[n][:, 0, 4 * a:4 * a + 4, :], ps_hT[:, a, :].rearrange("p (c t) -> p c t", c=4),
                                       ACT.Copy).then_inc(S["hT_hi_done"], 1)
                    convert(t, 2)
            y_low(N_SLOT_TILE - 1)

        @block.vector
        def _(dve):
            start(dve, DVE_SEMS)
            links = {"ln1": 0, "ln2": 0}

            def stats1(b, q):
                dve.wait_ge(L[f"x_in{q}"], landed(b + 1))
                dve.wait_ge(S["q_ln_done"], times(b * 2 + q))
                n = (b * 2 + q) * 2
                dve.bn_stats(st1[:, :], x_in[q][:, :]).then_inc(S["ln1_link"], 1)
                dve.wait_ge(S["ln1_link"], times(n + 1))
                dve.nop().then_inc(S["dve_waited"], 1)
                dve.bn_aggr(mv1[:, :], st1[:, :]).then_inc(S["ln1_link"], 1)
                dve.wait_ge(S["ln1_link"], times(n + 2))
                dve.tensor_scalar(ve1[:, :], mv1[:, 1:2], EPS, float(HD), ALU.add, ALU.mult)\
                    .then_inc(S["ln1_stats"], 1)

            def normalise(b, q):
                dve.wait_ge(S["rstd1_done"], times(b * 2 + q + 1))
                dve.wait_ge(S["lo_done"], times((b - 1) * 4 + 3 + q))
                dve.tensor_scalar(q_ln[q][:, :], x_in[q][:, :], mv1[:, 0:1], rstd1[:, 0:1],
                                  ALU.subtract, ALU.mult).then_inc(S["q_ln_done"], 1)

            def copy_parts_T(b, k, u):
                m, q = k // 2, (k // 2) % 2
                dve.wait_ge(S["parts_T_done"], times(b * 8 + k))
                dst = (kT if m < 2 else qT)[u]
                dve.tensor_copy(dst[:, 0:4, P * q:P * q + P], ps_m[:, :].rearrange("p (r t) -> p r t", r=4))\
                    .then_inc(S["partsT0_copied"], 1)

            def maxes(i, s):
                g, n = s % 2, i * SPT + s
                dve.wait_ge(S["scores_done"], times(n + 1))
                dve.wait_ge(S["exp_done"], times(n - 1))
                dve.tensor_reduce(neg_max[g][:, :].rearrange("p (e r) -> p e r", e=2),
                                  ps_s[:, g, :, 0:2 * SPAN].rearrange("p e (r c) -> p e r c", r=2),
                                  AX.X, ALU.max, negate=True).then_inc(S["max_done"], 1)

            def copy_pt0(i, s):
                g, n = s % 2, i * SPT + s
                dve.wait_ge(S["ptrans_done"], times(n + 1))
                dve.wait_ge(S["pv_done"], times(n - 1))
                dve.tensor_copy(probs_T[g][:, 0, :, :], ps_pt[:, 0, 0:3 * P].rearrange("p (j q) -> p j q", j=3))\
                    .then_inc(S["pt0_copied"], 1)

            def invert_sums(i, s):
                t, w = tile_of(i, s), (s // 4) % 2
                dve.wait_ge(S["exp_done"], times(i * SPT + s + 1))
                dve.wait_ge(S["rsum_T_done"], times(t))
                dve.reciprocal(rsum[:, :], sums[w][:, :]).then_inc(S["rsum_done"], 1)

            def copy_rsum_T(i, s):
                t = tile_of(i, s)
                dve.wait_ge(S["rsum_T_done"], times(t + 1))
                dve.wait_ge(S["rbc_done"], times(t))
                dve.tensor_copy(rsum_T[:, :], ps_m[0:H, D:D + P]).then_inc(S["rsum_T_copied"], 1)

            def copy_xn_T(i, s):
                t = tile_of(i, s)
                dve.wait_ge(S["xn_T_ps_done"], times(t + 1))
                dve.wait_ge(S["logits_done"], times(t))
                dve.tensor_copy(xn_T[:, :, :], ps_m[:, 0:D].rearrange("p (c t) -> p c t", c=NC))\
                    .then_inc(S["xn_T_copied"], 1)

            def norm_y(i, s):
                t = tile_of(i, s)
                dve.wait_ge(S["rbc_done"], times(t + 1))
                dve.wait_ge(S["y_raw_done"], times(t + 1))
                dve.wait_ge(S["proj_done"], times(t))
                dve.tensor_tensor(y_norm[:, :, :], ps_m[:, 0:D].rearrange("p (c t) -> p c t", c=NC),
                                  y_raw[:, :, :], ALU.mult).then_inc(S["y_norm_done"], 1)

            def residual(i, s):
                t, q = tile_of(i, s), (s // 4) % 2
                dve.wait_ge(S["proj_done"], times(t + 1))
                dve.wait_ge(L[f"x_res{q}"], (i * 2 + s // 8 + 1) * 16 + BASE)
                dve.wait_ge(L[f"x2_out{q}"], (i * 2 + s // 8) * 16 + BASE)
                dve.wait_ge(S["xn_done"], times(t))
                dve.tensor_tensor(x2[q][:, :], ps_m[:, 0:D], x_res[q][:, :], ALU.add).then_inc(S["x2_done"], 1)

            def stats2(i, s):
                t, q = tile_of(i, s), (s // 4) % 2
                dve.wait_ge(S["x2_done"], times(t + 1))
                dve.bn_stats(st2[:, :], x2[q][:, :]).then_inc(S["ln2_link"], 1)
                dve.wait_ge(S["ln2_link"], times(t * 2 + 1))
                dve.nop().then_inc(S["dve_waited"], 1)
                dve.bn_aggr(mv2[:, :], st2[:, :]).then_inc(S["ln2_link"], 1)
                dve.wait_ge(S["ln2_link"], times(t * 2 + 2))
                dve.tensor_scalar(ve2[:, :], mv2[:, 1:2], EPS, None, ALU.add).then_inc(S["ln2_stats"], 1)

            def norm_x2(i, s):
                t, q = tile_of(i, s), (s // 4) % 2
                dve.wait_ge(S["rstd2_done"], times(t + 1))
                dve.wait_ge(L[f"xn_out{q}"], (i * 2 + s // 8) * 16 + BASE)
                dve.wait_ge(S["xn_T_ps_done"], times(t - 1))
                dve.tensor_scalar(xn[q][:, :], x2[q][:, :], mv2[:, 0:1], rstd2[:, 0:1],
                                  ALU.subtract, ALU.mult).then_inc(S["xn_done"], 1)

            def copy_logits(i, s):
                t = tile_of(i, s)
                dve.wait_ge(S["logits_done"], times(t + 1))
                dve.tensor_copy(logits[:, t, :], ps_m[:, D:D + E]).then_inc(S["logits_copied"], 1)

            dve.wait_ge(S["w_T_ps_done"], times(1))
            dve.tensor_copy(w_T[:, :, :].rearrange("p c n -> p (c n)"), ps_m[:, :]).then_inc(S["w_T_copied"], 1)
            copy_parts_T(0, 1, 0)
            copy_parts_T(0, 3, 0)
            stats1(0, 0)
            normalise(0, 0)
            copy_parts_T(0, 5, 0)
            stats1(0, 1)
            normalise(0, 1)
            copy_parts_T(0, 7, 0)

            def step(i, s):
                if s % 2 == 1:
                    prep0(dve, i, s, copy_parts_T)
                if i is not None:
                    maxes(i, s)
                for lag, task in ((2, copy_rsum_T), (6, copy_xn_T), (3, norm_y), (7, copy_logits), (4, residual)):
                    if last_of_tile(s, lag):
                        lag_task(dve, i, s, lag, task)
                lag_task(dve, i, s, 1, copy_pt0)
                if last_of_tile(s, 1):
                    lag_task(dve, i, s, 1, invert_sums)
                if last_of_tile(s, 4):
                    lag_task(dve, i, s, 4, stats2)
                if last_of_tile(s, 5):
                    lag_task(dve, i, s, 5, norm_x2)
                if s % 8 in (2, 4):
                    prep0(dve, i, s, lambda b, k, u: stats1(b, k // 2 - 1))
                if s % 8 in (3, 5):
                    prep0(dve, i, s, lambda b, k, u: normalise(b, k // 2 - 1))

            turns(dve, step, DEPTH)

            links["route"] = 0

            def link(ins):
                links["route"] += 1
                ins.then_inc(S["route_link"], 1)
                dve.wait_ge(S["route_link"], times(links["route"]))

            def over(ap, *shape):
                return ap.broadcast_to([P, *shape])

            dve.wait_ge(S["logits_copied"], times(N_TILE))
            dve.wait_ge(S["consts_done"], times(2))
            for k in range(2):
                lg = logits if k == 0 else rest
                if k == 1:
                    link(dve.scalar_tensor_tensor(out=rest[:, :, :], in0=choice[:, 0, :, :], scalar=-3e38,
                                                  in1=logits[:, :, :], op0=ALU.mult, op1=ALU.add))
                link(dve.tensor_reduce(best[:, k, :], lg[:, :, :], AX.X, ALU.max))
                link(dve.tensor_tensor(same[:, :, :], lg[:, :, :], over(best[:, k, :].unsqueeze(2), N_TILE, E),
                                       ALU.is_equal))
                link(dve.scalar_tensor_tensor(out=cand[:, :, :], in0=same[:, :, :], scalar=-float(E),
                                              in1=over(iota_e[:, :].unsqueeze(1), N_TILE, E),
                                              op0=ALU.mult, op1=ALU.add))
                link(dve.tensor_reduce(first[:, :], cand[:, :, :], AX.X, ALU.min))
                link(dve.tensor_tensor(choice[:, k, :, :], cand[:, :, :], over(first[:, :].unsqueeze(2), N_TILE, E),
                                       ALU.is_equal))
            dve.tensor_tensor(diff[:, :], best[:, 1, :], best[:, 0, :], ALU.subtract).then_inc(S["diff_done"], 1)
            dve.tensor_tensor(chosen[:, :, :], choice[:, 0, :, :], choice[:, 1, :, :], ALU.add)\
                .then_inc(S["chosen_done"], 1)
            dve.wait_ge(S["ex_done"], times(1))
            link(dve.tensor_scalar(gates[:, N_TILE:], ex[:, :], 1.0, None, ALU.add))
            link(dve.reciprocal(gates[:, 0:N_TILE], gates[:, N_TILE:]))
            link(dve.tensor_tensor(gates[:, N_TILE:], gates[:, 0:N_TILE], ex[:, :], ALU.mult))
            link(dve.tensor_copy(gate_hi[:, :], gates[:, :]))
            link(dve.tensor_tensor(gate_lo[:, :], gates[:, :], gate_hi[:, :].bitcast(F32), ALU.subtract))
            dve.wait_ge(S["rank_done"], times(1))
            flat = "p t e -> p (t e)"
            link(dve.tensor_copy(total[:, :, :].rearrange(flat), ps[:, 1, 0:P]))
            src = total
            for n, sh in enumerate((1, 2, 4, 8)):
                link(dve.tensor_copy(upto[n][:, 0:sh, :], src[:, 0:sh, :]))
                link(dve.tensor_tensor(upto[n][:, sh:, :], src[:, sh:, :], src[:, :N_TILE - sh, :], ALU.add))
                src = upto[n]
            link(dve.tensor_tensor(upto[4][:, :, :], src[:, :, :], total[:, :, :], ALU.subtract))
            link(dve.tensor_tensor(earlier[:, :, :].rearrange(flat), ps[:, 0, 0:P], upto[4][:, :, :].rearrange(flat),
                                   ALU.add))
            link(dve.tensor_scalar(tiles_i[:, :], src[:, N_TILE - 1, :], float(P - 1), None, ALU.add))
            link(dve.tensor_scalar(tiles_s[:, :], tiles_i[:, :], 7, None, ALU.arith_shift_right))
            link(dve.tensor_scalar(tiles_f[:, :], tiles_s[:, :], 1.0, None, ALU.max))
            src = tiles_f
            for n, sh in enumerate((1, 2, 4)):
                link(dve.tensor_copy(cum[n][:, 0:sh], src[:, 0:sh]))
                link(dve.tensor_tensor(cum[n][:, sh:], src[:, sh:], src[:, :E - sh], ALU.add))
                src = cum[n]
            link(dve.tensor_tensor(tile0[:, :], src[:, :], tiles_f[:, :], ALU.subtract))
            link(dve.scalar_tensor_tensor(out=place_e[:, :, :], in0=over(tile0[:, :].unsqueeze(1), N_TILE, E),
                                          scalar=float(P), in1=earlier[:, :, :], op0=ALU.mult, op1=ALU.add))
            for k in range(2):
                link(dve.tensor_tensor(picked[:, k, :, :], choice[:, k, :, :], place_e[:, :, :], ALU.mult))
            link(dve.tensor_reduce(pos[:, :], picked[:, :, :, :].rearrange("p k t e -> p (k t) e"), AX.X, ALU.add))
            link(dve.tensor_copy(pos_i[:, :], pos[:, :]))
            link(dve.tensor_scalar(row_i[:, :], pos_i[:, :], P - 1, None, ALU.bitwise_and))
            link(dve.tensor_scalar(til_i[:, :], pos_i[:, :], 7, None, ALU.arith_shift_right))
            link(dve.tensor_copy(row_f[:, :], row_i[:, :]))
            link(dve.tensor_copy(til_f[:, :], til_i[:, :]))
            for k in range(2):
                link(dve.scalar_tensor_tensor(out=tok_v[:, N_TILE * k:N_TILE * k + N_TILE], in0=token_id[:, :],
                                              scalar=float(N_TOK), in1=row_f[:, N_TILE * k:N_TILE * k + N_TILE],
                                              op0=ALU.subtract, op1=ALU.subtract))
            for n in range(2):
                dve.wait_ge(L[f"x2_out{n}"], landed(N_TILE // 2))
                dve.wait_ge(L[f"xn_out{n}"], landed(N_TILE // 2))
            link(dve.tensor_tensor(row_hot[:, :, :], over(iota_slot[:, :].unsqueeze(1), N_CHOICE, P),
                                   over(row_f[:, :].unsqueeze(2), N_CHOICE, P), ALU.is_equal))
            link(dve.tensor_tensor(til_hot[:, :, :], over(iota_tile[:, :].unsqueeze(1), N_CHOICE, SLOT_COLS),
                                   over(til_f[:, :].unsqueeze(2), N_CHOICE, SLOT_COLS), ALU.is_equal))
            for n, v in enumerate((tok_v[:, :], gate_hi[:, :].bitcast(F32), gate_lo[:, :])):
                link(dve.tensor_tensor(slot_vals[:, :, n, :], til_hot[:, :, :],
                                       over(v.unsqueeze(2), N_CHOICE, SLOT_COLS), ALU.mult))
            dve.nop().then_inc(S["hots_done"], 1)
            link(dve.tensor_tensor(ge_tile[:, :, :], over(iota_tile[:, :].unsqueeze(2), SLOT_COLS, E - 1),
                                   over(tile0[:, 1:].unsqueeze(1), SLOT_COLS, E - 1), ALU.is_ge))
            link(dve.memset(tile_e[:, 0:1], -1.0))
            link(dve.tensor_reduce(tile_e[:, 1:], ge_tile[:, :, :], AX.X, ALU.add))
            link(dve.tensor_copy(tab_f[:, 0, :], tile_e[:, 1:]))
            link(dve.tensor_tensor(tile_new[:, :], tile_e[:, 1:], tile_e[:, 0:SLOT_COLS], ALU.subtract))
            link(dve.scalar_tensor_tensor(out=tab_f[:, 2, :], in0=tile_e[:, 1:], scalar=float(E - 1),
                                          in1=tile_new[:, :], op0=ALU.is_lt, op1=ALU.mult))
            link(dve.tensor_copy(tile_tab[:, 0, :], tab_f[:, 0, :]))
            link(dve.tensor_copy(tile_tab[:, 2, :], tab_f[:, 2, :]))
            link(dve.tensor_scalar(tile_tab[:, 1, :], tile_tab[:, 0, :], 1, None, ALU.bitwise_and))
            link(dve.tensor_scalar(tile_tab[:, 3, :], tile_tab[:, 1, :], 1, None, ALU.bitwise_xor))
            dve.wait_ge(S["slots_done"], times(1))
            link(dve.tensor_scalar(slot_tok[:, :], ps[:, 2, 0:SLOT_COLS], part_id[:, 0:1], None, ALU.add))
            link(dve.tensor_copy(gate_part[:, :], ps[:, 2, SLOT_COLS:2 * SLOT_COLS]))
            link(dve.tensor_tensor(slot_gate[:, :], ps[:, 2, 2 * SLOT_COLS:3 * SLOT_COLS], gate_part[:, :], ALU.add))
            dve.nop().then_inc(S["tables_done"], 1)

            def x_lo(t, n):
                dve.wait_ge(S["xT_hi_done"], times(t + 1))
                dve.wait_ge(S["h3_done"], times((t - 2) * 2))
                dve.tensor_tensor(xT[n][:, 1, :, :], ps_xT[:, 0:D].rearrange("p (c t) -> p c t", c=NC),
                                  xT[n][:, 0, :, :].bitcast(F32), ALU.subtract).then_inc(S["xT_lo_done"], 1)

            def y_final(t, n, earlier_adds):
                dve.wait_ge(S["y_small_done"], times(t + 1))
                dve.wait_ge(S["adds_landed"], times(t - 1))
                dve.scalar_tensor_tensor(out=y_out[n][:, :], in0=ps_out[:, 0:D], scalar=slot_gate[:, bass.ds(t, 1)],
                                         in1=y_small[:, :], op0=ALU.mult, op1=ALU.add).then_inc(S["y_done"], 1)

            x_lo(0, 0)
            with dve.Fori(0, N_SLOT_TILE // UNROLL) as i:
                for n in range(UNROLL):
                    t = i * UNROLL + n
                    for a in range(2):
                        dve.wait_ge(S["h3_done"], times(t * 2 + a + 1))
                        dve.wait_ge(S["silu_done"], times(t * 2 + a + 1))
                        dve.wait_ge(S["h_turned"], times((t - 1) * 2 + a + 1))
                        dve.tensor_tensor(hidden[:, HALF * a:HALF * a + HALF], ps_h[:, 1, a, :],
                                          gated[:, HALF * a:HALF * a + HALF], ALU.mult).then_inc(S["hidden_done"], 1)
                    if n < UNROLL - 1:
                        x_lo(t + 1, n + 1)
                    else:
                        with dve.If(i < N_SLOT_TILE // UNROLL - 1):
                            x_lo(t + 1, 0)
                    if n == 0:
                        with dve.If(i > 0):
                            y_final(within(t - 1, 2, N_SLOT_TILE - 2), UNROLL - 1, i)
                    else:
                        y_final(t - 1, n - 1, i)
                    for a in range(2):
                        dve.wait_ge(S["hT_hi_done"], times(t * 2 + a + 1))
                        dve.wait_ge(S["out_done"], times(t - 2))
                        dve.tensor_tensor(hT[n][:, 1, 4 * a:4 * a + 4, :],
                                          ps_hT[:, a, :].rearrange("p (c t) -> p c t", c=4),
                                          hT[n][:, 0, 4 * a:4 * a + 4, :].bitcast(F32), ALU.subtract)\
                            .then_inc(S["hT_lo_done"], 1)
            y_final(N_SLOT_TILE - 1, UNROLL - 1, 0)

        @block.tensor
        def _(pe):
            start(pe, PE_SEMS)

            def parts_round(b, k, u, misc_free):
                m, half = (k - 1) // 2, (k - 1) % 2
                q = m % 2
                pe.wait_ge(S["lo_done"], times(b * 4 + m + 1))
                misc_free()
                src = (k_parts if m < 2 else q_parts)[q]
                for r in range(4):
                    pair = 4 * half + r
                    ins = pe.transpose(ps_m[:, P * r:P * r + P],
                                       src[:, 2 * pair:2 * pair + 2, :, :].rearrange("p h a d -> p (h a d)"),
                                       ident[:, :])
                ins.then_inc(S["parts_T_done"], 1)

            def parts_copied(b, k):
                pe.wait_ge(S["partsT0_copied"], times(b * 4 + (k + 1) // 2))
                pe.wait_ge(S["partsT1_copied"], times(b * 4 + k // 2))

            def scores(i, s):
                n, g, u, q = i * SPT + s, s % 2, s // 8, (s // 4) % 2
                b = i * 2 + u
                pe.wait_ge(S["exp_done"], times(n - 1))
                if s % 8 == 0:
                    parts_copied(b, 6)
                if s % 8 == 4:
                    parts_copied(b, 8)
                for par in range(2):
                    pe.matmul(ps_s[:, g, par, 0:2 * SPAN], ident_bf[:, :],
                              mask[:, q, :].unsqueeze(1).broadcast_to([P, 2, SPAN]), start=True, stop=False)
                    for r in range(2):
                        pair = 2 * (s % 4) + r
                        rows = slice(64 * par, 64 * par + 64)
                        ins = pe.matmul(ps_s[:, g, par, SPAN * r:SPAN * r + SPAN],
                                        qT[u][rows, pair, P * q:P * q + P],
                                        kT[u][rows, pair, WIN * q:WIN * q + SPAN], start=False, stop=(r == 1))
                ins.then_inc(S["scores_done"], 1)

            def prob_transposes(i, s):
                n, g = i * SPT + s, s % 2
                pe.wait_ge(S["exp_done"], times(n + 1))
                pe.wait_ge(S["pt0_copied"], times(n))
                pe.wait_ge(S["pt1_copied"], times(n))
                for r in range(2):
                    for j in range(3):
                        ins = pe.transpose(ps_pt[:, r, P * j:P * j + P],
                                           probs[g][:, r, j, :, :].rearrange("p e c -> p (e c)"), ident[:, :])
                ins.then_inc(S["ptrans_done"], 1)

            def values(i, s):
                n, g, u, q = i * SPT + s, s % 2, s // 8, (s // 4) % 2
                pe.wait_ge(S["pt0_copied"], times(n + 1))
                pe.wait_ge(S["pt1_copied"], times(n + 1))
                if s % 4 == 0:
                    pe.wait_ge(S["y_raw_done"], times(tile_of(i, s)))
                if s % 8 == 0:
                    pe.wait_ge(S["v_bd_done"], times((i * 2 + u) * 2 + 2))
                for r in range(2):
                    pair = 2 * (s % 4) + r
                    c, row = pair // 4, 32 * (pair % 4)
                    for j in range(3):
                        ins = pe.matmul(ps_y[row:row + 32, c, :], v_bd[u][:, q + j, pair, :],
                                        probs_T[g][:, r, j, :], start=(j == 0), stop=(j == 2))
                ins.then_inc(S["pv_done"], 1)

            def tail_sums(i, s):
                t = tile_of(i, s)
                pe.wait_ge(S["rsum_done"], times(t + 1))
                pe.transpose(ps_m[0:H, D:D + P], rsum[:, :], ident[:, :]).then_inc(S["rsum_T_done"], 1)

            def tail_broadcast(i, s):
                t = tile_of(i, s)
                pe.wait_ge(S["rsum_T_copied"], times(t + 1))
                for c in range(NC):
                    ins = pe.matmul(ps_m[:, P * c:P * c + P], head_sel[:, c, :], rsum_T[:, :],
                                    start=True, stop=True)
                ins.then_inc(S["rbc_done"], 1)

            def tail_project(i, s):
                t = tile_of(i, s)
                pe.wait_ge(S["y_norm_done"], times(t + 1))
                pe.matmul(ps_m[:, 0:D], ones_row[:, :], bias_row[:, :], start=True, stop=False)
                for c in range(NC):
                    ins = pe.matmul(ps_m[:, 0:D], y_norm[:, c, :], w_T[:, c, :], start=False, stop=(c == NC - 1))
                ins.then_inc(S["proj_done"], 1)

            def tail_turn(i, s):
                t, q = tile_of(i, s), (s // 4) % 2
                pe.wait_ge(S["xn_done"], times(t + 1))
                for c in range(NC):
                    ins = pe.transpose(ps_m[:, P * c:P * c + P], xn[q][:, P * c:P * c + P], ident[:, :])
                ins.then_inc(S["xn_T_ps_done"], 1)

            def tail_logits(i, s):
                t = tile_of(i, s)
                pe.wait_ge(S["xn_T_copied"], times(t + 1))
                for c in range(NC):
                    ins = pe.matmul(ps_m[:, D:D + E], xn_T[:, c, :], wg_s[:, c, :], start=(c == 0), stop=(c == NC - 1))
                ins.then_inc(S["logits_done"], 1)

            TAIL = {1: ((6, tail_turn, "xn_T_copied"), (2, tail_sums, "rsum_T_copied")),
                    2: ((7, tail_logits, "logits_copied"), (3, tail_broadcast, "y_norm_done")),
                    3: ((4, tail_project, "x2_done"),)}

            def tail_emptied(i, s):
                for lag, _, copied in TAIL[s % 4]:
                    if i is None:
                        pe.wait_ge(S[copied], times(min((NIT - 1) * 4 + (s - lag) // 4 + 1, N_TILE)))
                    else:
                        pe.wait_ge(S[copied], times(i * 4 + ((s - lag) // 4 + 1)))

            pe.wait_ge(S["consts_done"], times(1))
            pe.wait_ge(L["weights_in"], landed(3))
            for c in range(NC):
                for r in range(NC):
                    ins = pe.transpose(ps_m[:, D * c + P * r:D * c + P * r + P], w_nat[:, r, P * c:P * c + P],
                                       ident[:, :])
            ins.then_inc(S["w_T_ps_done"], 1)
            pe.wait_ge(S["w_T_copied"], times(1))
            for k in range(1, 9):
                parts_round(0, k, 0, lambda: parts_copied(0, k - 1))

            def step(i, s):
                def round_copied(b, k, u):
                    parts_copied(b, k)

                def bank_free(b, k):
                    if s % 4 != 1:
                        tail_emptied(i, s - 1)
                    if s % 4 == 1 or s <= 4:
                        parts_copied(b, k - 1)

                prep(pe, i, s, lambda b, k, u: parts_round(b, k, u, lambda: bank_free(b, k)))
                if i is not None:
                    scores(i, s)
                if s % 4 in TAIL and (i is not None or any(s - lag < SPT for lag, _, _ in TAIL[s % 4])):
                    if i is not None and s % 8 == 1:
                        parts_copied(i * 2 + s // 8, 8)
                    prep(pe, i, s, round_copied)
                    tail_emptied(i, s - 2 if s % 4 == 1 else s - 1)
                    for lag, task, _ in TAIL[s % 4]:
                        lag_task(pe, i, s, lag, task)
                lag_task(pe, i, s, 2, values)
                lag_task(pe, i, s, 1, prob_transposes)

            turns(pe, step, DEPTH)

            pe.wait_ge(S["chosen_done"], times(1))
            flat = chosen[:, :, :].rearrange("p t e -> p (t e)")
            pe.matmul(ps[:, 0, 0:P], before[:, :], flat, start=True, stop=True)
            pe.matmul(ps[:, 1, 0:P], ones[:, :], flat, start=True, stop=True).then_inc(S["rank_done"], 1)
            pe.wait_ge(S["hots_done"], times(1))
            for a in range(N_CHOICE):
                ins = pe.matmul(ps[:, 2, 0:3 * SLOT_COLS], row_hot[:, a, :],
                                slot_vals[:, a, :, :].rearrange("p v c -> p (v c)"),
                                start=(a == 0), stop=(a == N_CHOICE - 1))
            ins.then_inc(S["slots_done"], 1)
            pe.wait_ge(S["tables_done"], times(1))

            def turn_x(t, n, landed):
                pe.wait_ge(L[f"xg{n}"], landed * 16)
                pe.wait_ge(S["xT_lo_done"], times(t))
                for c in range(NC):
                    ins = pe.transpose(ps_xT[:, P * c:P * c + P], xg[n][:, P * c:P * c + P], ident[:, :])
                ins.then_inc(S["x_turned"], 1)

            def down(t, n, slot):
                pe.wait_ge(S["hT_lo_done"], times(t * 2 + 2))
                pe.wait_ge(S["y_done"], times(t))
                w = wts[:, slot, 2, :].rearrange("p (c a n) -> p c a n", c=NF, a=2)
                for c in range(NF):
                    pe.matmul(ps_out[:, :], hT[n][:, 0, c, :], w[:, c, :, :].rearrange("p a n -> p (a n)"),
                              start=(c == 0), stop=False)
                    ins = pe.matmul(ps_out[:, 0:D], hT[n][:, 1, c, :], w[:, c, 0, :],
                                    start=False, stop=(c == NF - 1))
                ins.then_inc(S["out_done"], 1)

            turn_x(0, 0, 1)
            with pe.Fori(0, N_SLOT_TILE // UNROLL) as i:
                for n in range(UNROLL):
                    t = i * UNROLL + n
                    expert = pe.value_load(tile_tab[0:1, 0, bass.ds(t, 1)], min_val=0, max_val=E - 1)
                    slot = pe.value_load(tile_tab[0:1, 1, bass.ds(t, 1)], min_val=0, max_val=1)
                    pe.wait_ge(S["xT_lo_done"], times(t + 1))
                    pe.wait_ge(S["w_lo_done"], times(expert * 3 + 3))
                    for a in range(2):
                        for m in range(2):
                            pe.wait_ge(S["silu_done" if m == 0 else "hidden_done"], times((t - 1) * 2 + a + 1))
                            w = wts[:, slot, m, :].rearrange("p (a c f) -> p a c f", a=2, c=NC)
                            for c in range(NC):
                                for part, x_part in ((0, 0), (1, 0), (0, 1)):
                                    ins = pe.matmul(ps_h[:, m, a, :], xT[n][:, x_part, c, :],
                                                    w[:, part, c, HALF * a:HALF * a + HALF],
                                                    start=(c == 0 and part + x_part == 0),
                                                    stop=(c == NC - 1 and x_part == 1))
                            ins.then_inc(S["h1_done" if m == 0 else "h3_done"], 1)
                    if n < UNROLL - 1:
                        turn_x(t + 1, n + 1, i + 1)
                    else:
                        with pe.If(i < N_SLOT_TILE // UNROLL - 1):
                            turn_x(t + 1, 0, i + 2)
                    if n == 0:
                        with pe.If(i > 0):
                            down(t - 1, UNROLL - 1, pe.value_load(
                                tile_tab[0:1, 1, bass.ds(within(t - 1, 2, N_SLOT_TILE - 2), 1)], min_val=0, max_val=1))
                    else:
                        down(t - 1, n - 1, pe.value_load(tile_tab[0:1, 1, bass.ds(t - 1, 1)], min_val=0, max_val=1))
                    for a in range(2):
                        pe.wait_ge(S["hidden_done"], times(t * 2 + a + 1))
                        pe.wait_ge(S["hT_lo_done"], times((t - 1) * 2 + a + 1))
                        for c in range(4):
                            ins = pe.transpose(ps_hT[:, a, P * c:P * c + P],
                                               hidden[:, HALF * a + P * c:HALF * a + P * c + P], ident[:, :])
                        ins.then_inc(S["h_turned"], 1)
            down(N_SLOT_TILE - 1, UNROLL - 1, pe.value_load(
                tile_tab[0:1, 1, N_SLOT_TILE - 1:N_SLOT_TILE], min_val=0, max_val=1))


_INS = ['x', 'ctx_1024', 'L0_xattn_W_proj', 'L0_xattn_b_proj', 'L0_ffn_Wg', 'L0_ffn_W1', 'L0_ffn_W3', 'L0_ffn_W2']


def kernel(**inputs):
    import numpy as _np
    import concourse.bacc as _bacc
    from concourse import mybir as _mybir
    from concourse.bass_utils import run_bass_kernel_spmd as _run

    nc = _bacc.Bacc("TRN2", target_bir_lowering=False, num_devices=1)
    arrays, args = {}, []
    for name in _INS:
        a = _np.ascontiguousarray(inputs[name])
        arrays[f"in_{name}_dram"] = a
        args.append(nc.dram_tensor(f"in_{name}_dram", a.shape, _mybir.dt.from_np(a.dtype), kind="ExternalInput").ap())
    rows = (N_TOK + PAD_ROWS, D)
    out = nc.dram_tensor("out_0_dram", rows, _mybir.dt.float32, kind="ExternalOutput").ap()
    xn_rows = nc.dram_tensor("xn_rows_dram", rows, _mybir.dt.float32, kind="Internal").ap()
    attention_and_experts(nc, *args, out, xn_rows)
    r = _run(nc, [arrays], core_ids=[0])
    return r.results[0]["out_0_dram"][:N_TOK].reshape(B, T, D)
```

```python
from contextlib import ExitStack

import concourse.bass as bass
from concourse import mybir

B, T, D = 8, 256, 256
P = 128
N_TOK = B * T
N_TILE = N_TOK // P
H, HD = 16, 16
WIN = 64
NKB = T // WIN
SPAN = 3 * WIN
NC = D // P
NPAIR = H // 2
E, F_DIM = 8, 1024
N_ASSIGN = 2 * N_TOK
N_CHOICE = 2 * N_TILE
N_SLOT_TILE = (N_ASSIGN + E * P - 1) // P
SLOT_COLS = N_SLOT_TILE + 1
NF = F_DIM // P
HALF = F_DIM // 2
MAT = 2 * 2 * F_DIM
UNROLL = 3
PAD_ROWS = P
HOT_CHUNK = 8
ATTENTION_CONSTS = 7
EPS = 1e-5
MASKED = -1e30
NIT = 4
SPT = 16
BASE = 64


def attention_and_experts(nc, x, ctx, w_proj, b_proj, wg, w1, w3, w2, out, xn_rows):
    F32, F32R, I32 = mybir.dt.float32, mybir.dt.float32r, mybir.dt.int32
    BF16, F16 = mybir.dt.bfloat16, mybir.dt.float16
    ALU, ACT, AX = mybir.AluOpType, mybir.ActivationFunctionType, mybir.AxisListType

    x_t = x.rearrange("b (q p) d -> (b q) p d", p=P)
    ctx_t = ctx.rearrange("b (q p) d -> (b q) p d", p=P)
    ctx_v = ctx.rearrange("b (j p) d -> b p j d", p=WIN)
    out_t = out.rearrange("(t p) d -> t p d", p=P)
    xn_t = xn_rows.rearrange("(t p) d -> t p d", p=P)

    with ExitStack() as stack:
        def sem(name):
            s = stack.enter_context(nc.semaphore(name))
            return s

        place = {"at": (nc.sbuf_base + 63) // 64 * 64}

        def sb(name, shape, dt):
            size = 1
            for n in shape[1:]:
                size *= n
            size *= 2 if dt in (BF16, F16) else 4
            t = nc.alloc_sbuf_tensor_at(name, shape, dt, offset=place["at"])
            place["at"] += (size + 63) // 64 * 64
            return t

        def pb(name, shape, dt):
            return stack.enter_context(nc.psum_tensor(name, shape, dt))

        ident = sb("ident", [P, P], F32)
        ident_bf = sb("ident_bf", [P, P], BF16)
        mask = sb("mask", [P, 2, SPAN], BF16)
        head_sel = sb("head_sel", [H, NC, P], F32)
        ones_row = sb("ones_row", [1, P], F32)
        bias_row = sb("bias_row", [1, D], F32)
        ones_r = sb("ones_r", [1, P], F32R)
        bias_parts = sb("bias_parts", [1, 2, D], F32R)
        neg_half = sb("neg_half", [P, 1], F32)
        w_nat = sb("w_nat", [P, NC, D], F32)
        w_T = sb("w_T", [P, NC, D], F32)
        wg_s = sb("wg_s", [P, NC, E], F32)
        logits = sb("logits", [P, N_TILE, E], F32)

        iota_e = sb("iota_e", [P, E], F32)
        iota_slot = sb("iota_slot", [P, P], F32)
        iota_tile = sb("iota_tile", [P, SLOT_COLS], F32)
        token_id = sb("token_id", [P, N_TILE], F32)
        part_id = sb("part_id", [P, 1], F32)
        before = sb("before", [P, P], F32)
        ones = sb("ones", [P, P], F32)

        slot_tok = sb("slot_tok", [P, SLOT_COLS], I32)
        slot_gate = sb("slot_gate", [P, SLOT_COLS], F32)
        tile_tab = sb("tile_tab", [P, 4, SLOT_COLS], I32)
        raw = [sb(f"raw{m}", [P, 2 * F_DIM], F32) for m in range(3)]
        wts = sb("wts", [P, 2, 3, MAT], F32R)
        behind_first = place["at"] - 3 * MAT * 4
        behind_wts = place["at"]

        place["at"] = behind_first
        k_in = [sb(f"k_in{q}", [P, D], F32) for q in range(2)]
        x_in = [sb(f"x_in{q}", [P, D], F32) for q in range(2)]
        v_in = sb("v_in", [P, NKB, D], F32)
        v_bd = [sb(f"v_bd{u}", [P, NKB, NPAIR, 2 * HD], F32) for u in range(2)]
        q_ln = [sb(f"q_ln{q}", [P, D], F32) for q in range(2)]
        k_parts = [sb(f"k_parts{q}", [P, H, 4, HD], F32) for q in range(2)]
        q_parts = [sb(f"q_parts{q}", [P, H, 4, HD], F32) for q in range(2)]
        kT = [sb(f"kT{u}", [P, NPAIR, T], F32R) for u in range(2)]
        qT = [sb(f"qT{u}", [P, NPAIR, T], F32R) for u in range(2)]
        neg_max = [sb(f"neg_max{g}", [P, 4], F32) for g in range(2)]
        probs = [sb(f"probs{g}", [P, 2, 3, 2, WIN], F32) for g in range(2)]
        probs_T = [sb(f"probs_T{g}", [P, 2, 3, P], F32) for g in range(2)]
        sums = [sb(f"sums{g}", [P, H], F32) for g in range(2)]
        rsum = sb("rsum", [P, H], F32)
        rsum_T = sb("rsum_T", [H, P], F32)
        y_raw = sb("y_raw", [P, NC, P], F32)
        y_norm = sb("y_norm", [P, NC, P], F32)
        x_res = [sb(f"x_res{q}", [P, D], F32) for q in range(2)]
        x2 = [sb(f"x2_{q}", [P, D], F32) for q in range(2)]
        xn = [sb(f"xn_{q}", [P, D], F32) for q in range(2)]
        xn_T = sb("xn_T", [P, NC, P], F32)
        zero_rows = sb("zero_rows", [P, D + E], F32)
        st1 = sb("st1", [P, 6], F32)
        mv1 = sb("mv1", [P, 2], F32)
        ve1 = sb("ve1", [P, 1], F32)
        rstd1 = sb("rstd1", [P, 1], F32)
        st2 = sb("st2", [P, 6], F32)
        mv2 = sb("mv2", [P, 2], F32)
        ve2 = sb("ve2", [P, 1], F32)
        rstd2 = sb("rstd2", [P, 1], F32)

        assert place["at"] <= nc.sbuf_usable_end

        place["at"] = behind_wts

        def table(name, *shape, dt=F32):
            return sb(name, [P, *shape], dt)

        best = table("best", 2, N_TILE)
        choice = table("choice", 2, N_TILE, E)
        same = table("same", N_TILE, E)
        cand = table("cand", N_TILE, E)
        first = table("first", N_TILE)
        rest = table("rest", N_TILE, E)
        chosen = table("chosen", N_TILE, E)
        total = table("total", N_TILE, E)
        upto = [table(f"upto{n}", N_TILE, E) for n in range(5)]
        earlier = table("earlier", N_TILE, E)
        place_e = table("place_e", N_TILE, E)
        picked = table("picked", 2, N_TILE, E)
        tiles_i = table("tiles_i", E, dt=I32)
        tiles_s = table("tiles_s", E, dt=I32)
        tiles_f = table("tiles_f", E)
        cum = [table(f"cum{n}", E) for n in range(4)]
        tile0 = table("tile0", E)
        pos = table("pos", N_CHOICE)
        pos_i = table("pos_i", N_CHOICE, dt=I32)
        row_i = table("row_i", N_CHOICE, dt=I32)
        til_i = table("til_i", N_CHOICE, dt=I32)
        row_f = table("row_f", N_CHOICE)
        til_f = table("til_f", N_CHOICE)
        diff = table("diff", N_TILE)
        ex = table("ex", N_TILE)
        gates = table("gates", N_CHOICE)
        gate_of = table("gate_of", 3, N_TILE, E)
        row_hot = table("row_hot", N_CHOICE, P, dt=F16)
        til_hot = table("til_hot", N_CHOICE, SLOT_COLS)
        slot_vals = table("slot_vals", N_CHOICE, SLOT_COLS, dt=F16)
        ge_tile = table("ge_tile", SLOT_COLS, E - 1)
        tile_e = table("tile_e", SLOT_COLS + 1)
        tile_new = table("tile_new", SLOT_COLS)
        pad_row = table("pad_row", SLOT_COLS)
        tab_f = table("tab_f", 4, SLOT_COLS)
        assert place["at"] <= nc.sbuf_usable_end

        behind_tables = place["at"]

        place["at"] = behind_wts
        xT = [table(f"xT{n}", 2, NC, P, dt=F32R) for n in range(UNROLL)]
        gated = table("gated", F_DIM)
        hidden = table("hidden", F_DIM)
        hT = [table(f"hT{n}", 2, NF, P, dt=F32R) for n in range(UNROLL)]
        y_small = table("y_small", D)
        y_out = [table(f"y_out{n}", D) for n in range(UNROLL)]
        place["at"] = max(place["at"], behind_tables)
        gather_row = [table(f"gather_row{n}", 1, dt=I32) for n in range(UNROLL)]
        add_row = [table(f"add_row{n}", 1, dt=I32) for n in range(UNROLL)]
        xg = [table(f"xg{n}", D + E) for n in range(UNROLL)]
        assert place["at"] <= nc.sbuf_usable_end

        ps = pb("ps", [P, 8, 512], F32)
        ps_s = ps[:, 0:4, :].rearrange("p (g e) c -> p g e c", g=2)
        ps_pt = ps[:, 4:6, :]
        ps_y = ps[:, 6, 0:D].rearrange("p (c t) -> p c t", c=NC)
        ps_m = ps[:, 7, :]
        ps_h = ps[:, 0:4, :].rearrange("p (m a) c -> p m a c", m=2)
        ps_hT = ps[:, 4:6, :]
        ps_out = ps[:, 6, :]
        ps_xT = ps[:, 7, :]

        PE_SEMS = ["scores_done", "ptrans_done", "pv_done", "parts_T_done", "rsum_T_done", "rbc_done",
                   "proj_done", "xn_T_ps_done", "logits_done", "w_T_ps_done",
                   "rank_done", "slots_done", "x_turned", "h1_done", "h3_done", "h_turned", "out_done"]
        DVE_SEMS = ["max_done", "pt0_copied", "partsT0_copied", "q_ln_done", "ln1_stats", "rsum_done",
                    "rsum_T_copied", "y_norm_done", "x2_done", "ln2_stats", "xn_done", "xn_T_copied", "logits_copied",
                    "w_T_copied", "bias_split", "route_link", "diff_done", "chosen_done", "hots_done", "gates_done", "tables_done",
                    "xT_lo_done", "hidden_done", "hT_lo_done", "y_done", "ln1_link", "ln2_link", "gate_taken", "dve_waited"]
        ACT_SEMS = ["exp_done", "pt1_copied", "partsT1_copied", "hi_done", "v_bd_done", "y_raw_done", "ex_done",
                    "silu_done", "xT_hi_done", "hT_hi_done", "y_small_done", "w_hi_done"]
        POOL_SEMS = ["lo_done", "rstd1_done", "rstd2_done", "consts_done", "pool_link", "w_lo_done",
                     "rows_read", "adds_landed", "pool_waited"]
        S = {n: sem(n) for n in PE_SEMS + DVE_SEMS + ACT_SEMS + POOL_SEMS}
        DMA_SEMS = ["k_in0", "k_in1", "x_in0", "x_in1", "v_in", "x_res0", "x_res1", "weights_in",
                    "x2_out0", "x2_out1", "xn_out0", "xn_out1", "zero_out", "gates_out",
                    "raw0", "raw1", "raw2"]
        POOL_DMA_SEMS = ["xg0", "xg1", "xg2", "added"]
        L = {n: sem("dma_" + n) for n in DMA_SEMS + POOL_DMA_SEMS}

        def start(eng, names):
            for n in names:
                eng.sem_inc(S[n], BASE)

        def times(count):
            return count + BASE

        def landed(count):
            return count * 16 + BASE

        def within(value, low, high):
            return nc.s_assert_within(value, low, high, skip_runtime_bounds_check_because=
                                      "the If around it leaves the loop's register in this range")

        def lagged(eng, i, s, lag, task):
            if s >= lag:
                task(i, s - lag)
            else:
                with eng.If(i > 0):
                    task(within(i - 1, 0, NIT - 2), s - lag + SPT)

        def last_of_tile(s, lag):
            return (s - lag) % 4 == 3

        def tile_of(i, s):
            return i * 4 + s // 4

        def turns(eng, step, depth):
            with eng.Fori(0, NIT) as i:
                for s in range(SPT):
                    step(i, s)
            for s in range(SPT, SPT + depth):
                step(None, s)

        def lag_task(eng, i, s, lag, task):
            if i is None:
                if s - lag < SPT:
                    task(NIT - 1, s - lag)
            else:
                lagged(eng, i, s, lag, task)

        DEPTH = 9

        def prep(eng, i, s, task, late=0):
            if i is None:
                return
            u, k = s // 8, s % 8
            if u == 0 and k <= late:
                with eng.If(i > 0):
                    task(i * 2, 8 + k, 0)
            elif k <= late:
                task(i * 2 + 1, 8 + k, 1)
            elif u == 0:
                task(i * 2 + 1, k, 1)
            else:
                with eng.If(i < NIT - 1):
                    task(within(i * 2 + 2, 2, B - 2), k, 0)

        def prep0(eng, i, s, task):
            if i is None:
                return
            u, k = s // 8, s % 8
            if u == 0:
                task(i * 2 + 1, k, 1)
            else:
                with eng.If(i < NIT - 1):
                    task(within(i * 2 + 2, 2, B - 2), k, 0)

        block = stack.enter_context(nc.Block())

        @block.sync
        def _(sp):
            for n in DMA_SEMS:
                sp.sem_inc(L[n], BASE)

            def load_item(b, m):
                if m < 2:
                    sp.wait_ge(S["lo_done"], times((b - 1) * 4 + m + 1))
                    sp.dma_start(k_in[m][:, :], ctx_t[b * 2 + m, :, :]).then_inc(L[f"k_in{m}"], 16)
                else:
                    sp.wait_ge(S["q_ln_done"], times((b - 1) * 2 + m - 1))
                    sp.dma_start(x_in[m - 2][:, :], x_t[b * 2 + m - 2, :, :]).then_inc(L[f"x_in{m - 2}"], 16)

            def load_v(b):
                sp.wait_ge(S["v_bd_done"], times(b * 2))
                for half in range(2):
                    sp.dma_start(v_in[WIN * half:WIN * half + WIN, :, :], ctx_v[b, :, :, :])\
                        .then_inc(L["v_in"], 16)

            for m in range(4):
                load_item(0, m)
            load_v(0)
            sp.dma_start(w_nat[:, :, :], w_proj.rearrange("(c p) d -> p c d", p=P)).then_inc(L["weights_in"], 16)
            sp.dma_start(bias_row[:, :], b_proj.rearrange("(a n) -> a n", a=1)).then_inc(L["weights_in"], 16)
            sp.dma_start(wg_s[:, :, :], wg.rearrange("(c p) e -> p c e", p=P)).then_inc(L["weights_in"], 16)
            for m in range(3):
                load_item(1, m)
            w_dram = [w1.rearrange("e (c p) f -> e p c f", p=P), w3.rearrange("e (c p) f -> e p c f", p=P),
                      w2.rearrange("e (c p) n -> e p c n", p=P)]

            def load_expert(e, m):
                c = NC if m < 2 else NF
                sp.dma_start(raw[m][:, :].rearrange("p (c n) -> p c n", c=c), w_dram[m][e, :, :, :])\
                    .then_inc(L[f"raw{m}"], 16)

            for m in range(3):
                load_expert(0, m)
            sp.wait_ge(S["consts_done"], times(ATTENTION_CONSTS))
            sp.dma_start(out_t[N_TILE, :, :], zero_rows[:, 0:D]).then_inc(L["zero_out"], 16)
            sp.dma_start(xn_t[N_TILE, :, :], zero_rows[:, :]).then_inc(L["zero_out"], 16)

            def store_x2(i, s):
                t, q = tile_of(i, s), (s // 4) % 2
                sp.wait_ge(S["x2_done"], times(t + 1))
                sp.dma_start(out_t[t, :, :], x2[q][:, :]).then_inc(L[f"x2_out{q}"], 16)

            def store_xn(i, s):
                t, q = tile_of(i, s), (s // 4) % 2
                sp.wait_ge(S["xn_done"], times(t + 1))
                sp.dma_start(xn_t[t, :, 0:D], xn[q][:, :]).then_inc(L[f"xn_out{q}"], 16)

            def step(i, s):
                if i is not None:
                    u, k = s // 8, s % 8
                    if k in (2, 4, 6):
                        with sp.If(i < NIT - 1):
                            load_item(within(i * 2 + (u + 2), u + 2, B - 2 + u), k // 2 - 1)
                    if k == 0:
                        if u == 0:
                            load_item(i * 2 + 1, 3)
                            load_v(i * 2 + 1)
                        else:
                            with sp.If(i < NIT - 1):
                                nxt = within(i * 2 + 2, 2, B - 2)
                                load_item(nxt, 3)
                                load_v(nxt)
                    if s % 4 == 3:
                        t, q = tile_of(i, s), (s // 4) % 2
                        sp.wait_ge(S["x2_done"], times(t - 1))
                        sp.dma_start(x_res[q][:, :], x_t[t, :, :]).then_inc(L[f"x_res{q}"], 16)
                if last_of_tile(s, 5):
                    lag_task(sp, i, s, 5, store_x2)
                if last_of_tile(s, 6):
                    lag_task(sp, i, s, 6, store_xn)

            turns(sp, step, DEPTH)
            sp.wait_ge(S["gates_done"], times(1))
            sp.dma_start(xn_rows.rearrange("(t p) d -> p t d", p=P)[:, 0:N_TILE, D:D + E], gate_of[:, 2, :, :])\
                .then_inc(L["gates_out"], 16)
            with sp.Fori(1, E) as e:
                for m in range(3):
                    sp.wait_ge(S["w_hi_done"], times((e - 1) * 3 + m + 1))
                    sp.wait_ge(S["w_lo_done"], times((e - 1) * 3 + m + 1))
                    load_expert(e, m)
            for n in ("x2_out0", "x2_out1", "xn_out0", "xn_out1"):
                sp.wait_ge(L[n], landed(N_TILE // 2))
            sp.wait_ge(L["zero_out"], landed(2))
            sp.wait_ge(L["added"], N_SLOT_TILE * 16)

        @block.gpsimd
        def _(pool):
            start(pool, POOL_SEMS)
            def rstd1_task(b, q):
                pool.wait_ge(S["ln1_stats"], times(b * 2 + q + 1))
                pool.tensor_tensor(rstd1[:, :], ve1[:, :], neg_half[:, :], ALU.pow).then_inc(S["rstd1_done"], 1)

            pool.memset(ident[:, :], 0.0).then_inc(S["pool_link"], 1)
            pool.memset(ident_bf[:, :], 0.0).then_inc(S["pool_link"], 1)
            pool.memset(mask[:, :, :], 0.0).then_inc(S["pool_link"], 1)
            pool.memset(neg_half[:, :], -0.5).then_inc(S["pool_link"], 1)
            pool.wait_ge(S["pool_link"], times(4))
            for m in (ident, ident_bf):
                pool.affine_select(out=m[:, :], in_=m[:, :], compare_op=ALU.not_equal, fill=1.0, base=0,
                                   pattern=[[-1, P]], channel_multiplier=1).then_inc(S["consts_done"], 1)
            for q in range(2):
                pool.affine_select(out=mask[:, q, :], in_=mask[:, q, :], compare_op=ALU.is_ge, fill=MASKED,
                                   base=WIN + WIN * q, pattern=[[-1, SPAN]], channel_multiplier=1)\
                    .then_inc(S["pool_link"], 1)
            rstd1_task(0, 0)
            pool.wait_ge(S["pool_link"], times(6))
            for q in range(2):
                pool.affine_select(out=mask[:, q, :], in_=mask[:, q, :], compare_op=ALU.is_ge, fill=MASKED,
                                   base=WIN - WIN * q, pattern=[[1, SPAN]], channel_multiplier=-1)\
                    .then_inc(S["consts_done"], 1)
            rstd1_task(0, 1)
            for u in range(2):
                pool.memset(v_bd[u][:, :, :, :], 0.0).then_inc(S["consts_done"], 1)
            pool.memset(ones_row[:, :], 1.0).then_inc(S["pool_link"], 1)
            pool.memset(zero_rows[:, :], 0.0).then_inc(S["pool_link"], 1)
            pool.memset(head_sel[:, :, :], 1.0).then_inc(S["pool_link"], 1)
            pool.wait_ge(S["pool_link"], times(9))
            pool.affine_select(out=head_sel[:, :, :], in_=head_sel[:, :, :], compare_op=ALU.is_ge, fill=0.0,
                               base=0, pattern=[[P, NC], [1, P]], channel_multiplier=-HD)\
                .then_inc(S["pool_link"], 1)
            pool.wait_ge(S["pool_link"], times(10))
            pool.affine_select(out=head_sel[:, :, :], in_=head_sel[:, :, :], compare_op=ALU.is_ge, fill=0.0,
                               base=HD - 1, pattern=[[-P, NC], [-1, P]], channel_multiplier=HD)\
                .then_inc(S["consts_done"], 1)

            def count(out, pattern, base, per_partition):
                pool.iota(out, pattern, base=base, channel_multiplier=per_partition,
                          allow_small_or_imprecise_dtypes=True).then_inc(S["pool_link"], 1)

            count(iota_e[:, :], [[1, E]], 0, 0)
            count(iota_slot[:, :], [[1, P]], 0, 0)
            count(iota_tile[:, :], [[1, SLOT_COLS]], 0, 0)
            count(token_id[:, :], [[P, N_TILE]], 1, 1)
            count(part_id[:, :], [[1, 1]], N_TOK + 1, 1)
            pool.memset(before[:, :], 1.0).then_inc(S["pool_link"], 1)
            pool.memset(ones[:, :], 1.0).then_inc(S["pool_link"], 1)
            pool.wait_ge(S["pool_link"], times(17))
            pool.affine_select(out=before[:, :], in_=before[:, :], compare_op=ALU.is_gt, fill=0.0, base=0,
                               pattern=[[1, P]], channel_multiplier=-1).then_inc(S["pool_link"], 1)
            pool.wait_ge(S["pool_link"], times(18))
            pool.nop().then_inc(S["consts_done"], 1)

            def lo_parts(b, m, u):
                q = m % 2
                pool.wait_ge(S["hi_done"], times(b * 4 + m + 1))
                if m < 2:
                    src, dst, sl, hi = k_in[q], k_parts[q], slice(1, 4, 2), 0
                else:
                    src, dst, sl, hi = q_ln[q], q_parts[q], slice(2, 4), 0
                for at in range(*sl.indices(4)):
                    ins = pool.tensor_tensor(dst[:, :, at, :].bitcast(F32R),
                                             src[:, :].rearrange("p (h d) -> p h d", h=H),
                                             dst[:, :, hi, :], ALU.subtract)
                ins.then_inc(S["lo_done"], 1)

            def rstd2_task(i, s):
                t = tile_of(i, s)
                pool.wait_ge(S["ln2_stats"], times(t + 1))
                pool.tensor_tensor(rstd2[:, :], ve2[:, :], neg_half[:, :], ALU.pow).then_inc(S["rstd2_done"], 1)

            pool.wait_ge(S["lo_done"], times(4))
            def step(i, s):
                def task(b, k, u):
                    lo_parts(b, k // 2, u)
                    if k in (2, 4):
                        rstd1_task(b, k // 2 - 1)
                if s % 2 == 0:
                    prep0(pool, i, s, task)
                if last_of_tile(s, 5):
                    lag_task(pool, i, s, 5, rstd2_task)

            turns(pool, step, DEPTH)

            def w_lo(e, slot, m):
                pool.wait_ge(S["w_hi_done"], times(e * 3 + m + 1))
                part = wts[:, slot, m, :]
                if m < 2:
                    hi, lo, src = part[:, 0:MAT // 2], part[:, MAT // 2:MAT], raw[m][:, :]
                else:
                    both = part.rearrange("p (c a n) -> p c a n", c=NF, a=2)
                    hi, lo = both[:, :, 0, :], both[:, :, 1, :]
                    src = raw[m][:, :].rearrange("p (c n) -> p c n", c=NF)
                pool.tensor_tensor(lo, src, hi.bitcast(F32), ALU.subtract).then_inc(S["w_lo_done"], 1)

            for m in range(3):
                w_lo(0, 0, m)
            pool.wait_ge(S["tables_done"], times(1))
            for n in range(2):
                pool.wait_ge(L[f"xn_out{n}"], landed(N_TILE // 2))
                pool.wait_ge(L[f"x2_out{n}"], landed(N_TILE // 2))
            pool.wait_ge(L["zero_out"], landed(2))
            pool.wait_ge(L["gates_out"], landed(1))

            def gather(t, n):
                pool.tensor_copy(gather_row[n][:, :], slot_tok[:, bass.ds(t, 1)]).then_inc(S["rows_read"], 1)
                pool.wait_ge(S["rows_read"], times(t + 1))
                pool.wait_ge(S["xT_lo_done"], times(t - 2))
                pool.nop().then_inc(S["pool_waited"], 1)
                pool.indirect_dma_start(xg[n][:, :], None, xn_rows, bass.IndirectOffsetOnAxis(gather_row[n][:, :], 0),
                                        bounds_check=N_TOK + PAD_ROWS - 1).then_inc(L[f"xg{n}"], 16)

            def add(t, n):
                pool.wait_ge(S["y_done"], times(t + 1))
                pool.nop().then_inc(S["adds_landed"], 1)
                pool.tensor_copy(add_row[n][:, :], slot_tok[:, bass.ds(t, 1)]).then_inc(S["pool_link"], 1)
                pool.wait_ge(S["pool_link"], times(t + 19))
                pool.nop().then_inc(S["pool_waited"], 1)
                pool.indirect_dma_start(out, bass.IndirectOffsetOnAxis(add_row[n][:, :], 0), y_out[n][:, :], None,
                                        bounds_check=N_TOK + PAD_ROWS - 1, compute_op=ALU.add)\
                    .then_inc(L["added"], 16)

            def convert(t):
                is_first = pool.value_load(tile_tab[0:1, 2, bass.ds(t, 1)], min_val=0, max_val=1)
                with pool.If(is_first > 0):
                    expert = pool.value_load(tile_tab[0:1, 0, bass.ds(t, 1)], min_val=0, max_val=E - 2)
                    to = pool.value_load(tile_tab[0:1, 3, bass.ds(t, 1)], min_val=0, max_val=1)
                    for m in range(3):
                        w_lo(expert + 1, to, m)

            for n in range(UNROLL):
                gather(n, n)
            convert(0)
            with pool.Fori(0, N_SLOT_TILE // UNROLL) as i:
                for n in range(UNROLL):
                    t = i * UNROLL + n
                    with pool.If(i < N_SLOT_TILE // UNROLL - 1):
                        gather(within(t + UNROLL, UNROLL, N_SLOT_TILE - 1), n)
                    if n < UNROLL - 1:
                        convert(t + 1)
                    else:
                        with pool.If(i < N_SLOT_TILE // UNROLL - 1):
                            convert(within(t + 1, UNROLL, N_SLOT_TILE - 1))
                    pool.wait_ge(L["added"], i * (UNROLL * 16) + 16 * n)
                    add(t, n)

        @block.scalar
        def _(act):
            start(act, ACT_SEMS)

            def hi_parts(b, m):
                q = m % 2
                act.wait_ge(S["parts_T_done"], times((b - 1) * 8 + 2 * m + 2))
                if m < 2:
                    act.wait_ge(L[f"k_in{q}"], landed(b + 1))
                    src, dst = k_in[q], k_parts[q][:, :, 0:4:2, :]
                else:
                    act.wait_ge(S["q_ln_done"], times(b * 2 + q + 1))
                    src, dst = q_ln[q], q_parts[q][:, :, 0:2, :]
                src = src[:, :].rearrange("p (h d) -> p h d", h=H).unsqueeze(2).broadcast_to([P, H, 2, HD])
                act.activation(dst.bitcast(F32R), src, ACT.Copy).then_inc(S["hi_done"], 1)

            def copy_parts_T(b, k, u, bank=ps_m):
                m, q = k // 2 - 1, (k // 2 - 1) % 2
                act.wait_ge(S["parts_T_done"], times(b * 8 + k))
                dst = (kT if m < 2 else qT)[u]
                act.activation(dst[:, 4:8, P * q:P * q + P], bank.rearrange("p (r t) -> p r t", r=4),
                               ACT.Copy).then_inc(S["partsT1_copied"], 1)

            def spread_v(b, u):
                act.wait_ge(L["v_in"], landed((b + 1) * 2))
                act.wait_ge(S["consts_done"], times(6))
                act.wait_ge(S["pv_done"], times((b - 1) * 8))
                for par in range(2):
                    lo = WIN * par
                    src = v_in[lo:lo + WIN, :, :].rearrange("p j (r e d) -> p j r e d", e=2, d=HD)
                    act.activation(v_bd[u][lo:lo + WIN, :, :, HD * par:HD * par + HD], src[:, :, :, par, :], ACT.Copy)\
                        .then_inc(S["v_bd_done"], 1)

            def exps(i, s):
                g, w = s % 2, (s // 4) % 2
                n = i * SPT + s
                act.wait_ge(S["max_done"], times(n + 1))
                if s % 4 == 0:
                    act.wait_ge(S["rsum_done"], times(tile_of(i, s) - 1))
                for par in range(2):
                    for r in range(2):
                        h = 2 * (2 * (s % 4) + r) + par
                        ins = act.activation(
                            probs[g][:, r, :, par, :],
                            ps_s[:, g, par, SPAN * r:SPAN * r + SPAN].rearrange("p (j c) -> p j c", j=3),
                            ACT.Exp, bias=neg_max[g][:, 2 * par + r:2 * par + r + 1],
                            accum_out=sums[w][:, h:h + 1])
                ins.then_inc(S["exp_done"], 1)

            def copy_pt1(i, s):
                g, n = s % 2, i * SPT + s
                act.wait_ge(S["ptrans_done"], times(n + 1))
                act.wait_ge(S["pv_done"], times(n - 1))
                act.activation(probs_T[g][:, 1, :, :], ps_pt[:, 1, 0:3 * P].rearrange("p (j q) -> p j q", j=3),
                               ACT.Copy).then_inc(S["pt1_copied"], 1)

            def copy_y(i, s):
                t = tile_of(i, s)
                act.wait_ge(S["pv_done"], times(i * SPT + s + 1))
                act.wait_ge(S["y_norm_done"], times(t))
                act.activation(y_raw[:, :, :], ps_y[:, :, :], ACT.Copy).then_inc(S["y_raw_done"], 1)

            hi_parts(0, 0)
            hi_parts(0, 1)
            copy_parts_T(0, 2, 0, ps[:, 1, :])
            hi_parts(0, 2)
            copy_parts_T(0, 4, 0, ps[:, 3, :])
            hi_parts(0, 3)
            copy_parts_T(0, 6, 0, ps[:, 1, :])
            copy_parts_T(0, 8, 0, ps[:, 3, :])
            spread_v(0, 0)

            def step(i, s):
                if s % 2 == 1:
                    prep(act, i, s, lambda b, k, u: copy_parts_T(b, k - 1, u), late=1)
                else:
                    prep0(act, i, s, lambda b, k, u: hi_parts(b, k // 2))
                lag_task(act, i, s, 2, copy_pt1)
                if i is not None:
                    exps(i, s)
                if last_of_tile(s, 3):
                    lag_task(act, i, s, 3, copy_y)
                if s % 8 == 7:
                    prep0(act, i, s, lambda b, k, u: spread_v(b, u))

            turns(act, step, DEPTH)

            def w_hi(e, slot, m):
                act.wait_ge(L[f"raw{m}"], landed(e + 1))
                part = wts[:, slot, m, :]
                if m < 2:
                    act.copy(part[:, 0:MAT // 2], raw[m][:, :]).then_inc(S["w_hi_done"], 1)
                else:
                    act.copy(part.rearrange("p (c a n) -> p c a n", c=NF, a=2)[:, :, 0, :],
                             raw[m][:, :].rearrange("p (c n) -> p c n", c=NF)).then_inc(S["w_hi_done"], 1)

            for m in range(3):
                w_hi(0, 0, m)
            act.wait_ge(S["diff_done"], times(1))
            act.activation(ex[:, :], diff[:, :], ACT.Exp).then_inc(S["ex_done"], 1)

            def x_hi(t, n):
                act.wait_ge(S["x_turned"], times(t + 1))
                act.wait_ge(S["h3_done"], times((t - 2) * 2))
                act.activation(xT[n][:, 0, :, :], ps_xT[:, 0:D].rearrange("p (c t) -> p c t", c=NC),
                               ACT.Copy).then_inc(S["xT_hi_done"], 1)

            def y_low(t):
                act.wait_ge(S["out_done"], times(t + 1))
                act.wait_ge(S["y_done"], times(t))
                act.activation(y_small[:, :], ps_out[:, D:2 * D], ACT.Copy, scale=slot_gate[:, bass.ds(t, 1)])\
                    .then_inc(S["y_small_done"], 1)

            def convert(t, m):
                is_first = act.value_load(tile_tab[0:1, 2, bass.ds(t, 1)], min_val=0, max_val=1)
                with act.If(is_first > 0):
                    expert = act.value_load(tile_tab[0:1, 0, bass.ds(t, 1)], min_val=0, max_val=E - 2)
                    to = act.value_load(tile_tab[0:1, 3, bass.ds(t, 1)], min_val=0, max_val=1)
                    if m < 2:
                        act.wait_ge(S["h3_done"], times(t * 2))
                    else:
                        act.wait_ge(S["out_done"], times(t))
                    w_hi(expert + 1, to, m)

            act.wait_ge(S["tables_done"], times(1))
            x_hi(0, 0)
            with act.Fori(0, N_SLOT_TILE // UNROLL) as i:
                for n in range(UNROLL):
                    t = i * UNROLL + n
                    for a in range(2):
                        act.wait_ge(S["h1_done"], times(t * 2 + a + 1))
                        act.wait_ge(S["hidden_done"], times((t - 1) * 2 + a + 1))
                        act.activation(gated[:, HALF * a:HALF * a + HALF], ps_h[:, 0, a, :], ACT.Silu)\
                            .then_inc(S["silu_done"], 1)
                        if a == 0:
                            convert(t, 0)
                    if n < UNROLL - 1:
                        x_hi(t + 1, n + 1)
                    else:
                        with act.If(i < N_SLOT_TILE // UNROLL - 1):
                            x_hi(t + 1, 0)
                    convert(t, 1)
                    if n == 0:
                        with act.If(i > 0):
                            y_low(within(t - 1, 2, N_SLOT_TILE - 2))
                    else:
                        y_low(t - 1)
                    for a in range(2):
                        act.wait_ge(S["h_turned"], times(t * 2 + a + 1))
                        act.wait_ge(S["out_done"], times(t - 2))
                        act.activation(hT[n][:, 0, 4 * a:4 * a + 4, :], ps_hT[:, a, :].rearrange("p (c t) -> p c t", c=4),
                                       ACT.Copy).then_inc(S["hT_hi_done"], 1)
                    convert(t, 2)
            y_low(N_SLOT_TILE - 1)

        @block.vector
        def _(dve):
            start(dve, DVE_SEMS)
            links = {"ln1": 0, "ln2": 0}

            def stats1(b, q):
                dve.wait_ge(L[f"x_in{q}"], landed(b + 1))
                dve.wait_ge(S["q_ln_done"], times(b * 2 + q))
                n = (b * 2 + q) * 2
                dve.bn_stats(st1[:, :], x_in[q][:, :]).then_inc(S["ln1_link"], 1)
                dve.wait_ge(S["ln1_link"], times(n + 1))
                dve.nop().then_inc(S["dve_waited"], 1)
                dve.bn_aggr(mv1[:, :], st1[:, :]).then_inc(S["ln1_link"], 1)
                dve.wait_ge(S["ln1_link"], times(n + 2))
                dve.tensor_scalar(ve1[:, :], mv1[:, 1:2], EPS, float(HD), ALU.add, ALU.mult)\
                    .then_inc(S["ln1_stats"], 1)

            def normalise(b, q):
                dve.wait_ge(S["rstd1_done"], times(b * 2 + q + 1))
                dve.wait_ge(S["lo_done"], times((b - 1) * 4 + 3 + q))
                dve.tensor_scalar(q_ln[q][:, :], x_in[q][:, :], mv1[:, 0:1], rstd1[:, 0:1],
                                  ALU.subtract, ALU.mult).then_inc(S["q_ln_done"], 1)

            def copy_parts_T(b, k, u, bank=ps_m):
                m, q = k // 2, (k // 2) % 2
                dve.wait_ge(S["parts_T_done"], times(b * 8 + k))
                dst = (kT if m < 2 else qT)[u]
                dve.tensor_copy(dst[:, 0:4, P * q:P * q + P], bank.rearrange("p (r t) -> p r t", r=4))\
                    .then_inc(S["partsT0_copied"], 1)

            def maxes(i, s):
                g, n = s % 2, i * SPT + s
                dve.wait_ge(S["scores_done"], times(n + 1))
                dve.tensor_reduce(neg_max[g][:, :].rearrange("p (e r) -> p e r", e=2),
                                  ps_s[:, g, :, 0:2 * SPAN].rearrange("p e (r c) -> p e r c", r=2),
                                  AX.X, ALU.max, negate=True).then_inc(S["max_done"], 1)

            def copy_pt0(i, s):
                g, n = s % 2, i * SPT + s
                dve.wait_ge(S["ptrans_done"], times(n + 1))
                dve.wait_ge(S["pv_done"], times(n - 1))
                dve.tensor_copy(probs_T[g][:, 0, :, :], ps_pt[:, 0, 0:3 * P].rearrange("p (j q) -> p j q", j=3))\
                    .then_inc(S["pt0_copied"], 1)

            def invert_sums(i, s):
                t, w = tile_of(i, s), (s // 4) % 2
                dve.wait_ge(S["exp_done"], times(i * SPT + s + 1))
                dve.wait_ge(S["rsum_T_done"], times(t))
                dve.reciprocal(rsum[:, :], sums[w][:, :]).then_inc(S["rsum_done"], 1)

            def copy_rsum_T(i, s):
                t = tile_of(i, s)
                dve.wait_ge(S["rsum_T_done"], times(t + 1))
                dve.wait_ge(S["rbc_done"], times(t))
                dve.tensor_copy(rsum_T[:, :], ps_m[0:H, D:D + P]).then_inc(S["rsum_T_copied"], 1)

            def copy_xn_T(i, s):
                t = tile_of(i, s)
                dve.wait_ge(S["xn_T_ps_done"], times(t + 1))
                dve.wait_ge(S["logits_done"], times(t))
                dve.tensor_copy(xn_T[:, :, :], ps_m[:, 0:D].rearrange("p (c t) -> p c t", c=NC))\
                    .then_inc(S["xn_T_copied"], 1)

            def norm_y(i, s):
                t = tile_of(i, s)
                dve.wait_ge(S["rbc_done"], times(t + 1))
                dve.wait_ge(S["y_raw_done"], times(t + 1))
                dve.wait_ge(S["proj_done"], times(t))
                dve.tensor_tensor(y_norm[:, :, :], ps_m[:, 0:D].rearrange("p (c t) -> p c t", c=NC),
                                  y_raw[:, :, :], ALU.mult).then_inc(S["y_norm_done"], 1)

            def residual(i, s):
                t, q = tile_of(i, s), (s // 4) % 2
                dve.wait_ge(S["proj_done"], times(t + 1))
                dve.wait_ge(L[f"x_res{q}"], (i * 2 + s // 8 + 1) * 16 + BASE)
                dve.wait_ge(L[f"x2_out{q}"], (i * 2 + s // 8) * 16 + BASE)
                dve.wait_ge(S["xn_done"], times(t))
                dve.tensor_tensor(x2[q][:, :], ps_m[:, 0:D], x_res[q][:, :], ALU.add).then_inc(S["x2_done"], 1)

            def stats2(i, s):
                t, q = tile_of(i, s), (s // 4) % 2
                dve.wait_ge(S["x2_done"], times(t + 1))
                dve.bn_stats(st2[:, :], x2[q][:, :]).then_inc(S["ln2_link"], 1)
                dve.wait_ge(S["ln2_link"], times(t * 2 + 1))
                dve.nop().then_inc(S["dve_waited"], 1)
                dve.bn_aggr(mv2[:, :], st2[:, :]).then_inc(S["ln2_link"], 1)
                dve.wait_ge(S["ln2_link"], times(t * 2 + 2))
                dve.tensor_scalar(ve2[:, :], mv2[:, 1:2], EPS, None, ALU.add).then_inc(S["ln2_stats"], 1)

            def norm_x2(i, s):
                t, q = tile_of(i, s), (s // 4) % 2
                dve.wait_ge(S["rstd2_done"], times(t + 1))
                dve.wait_ge(L[f"xn_out{q}"], (i * 2 + s // 8) * 16 + BASE)
                dve.wait_ge(S["xn_T_ps_done"], times(t - 1))
                dve.tensor_scalar(xn[q][:, :], x2[q][:, :], mv2[:, 0:1], rstd2[:, 0:1],
                                  ALU.subtract, ALU.mult).then_inc(S["xn_done"], 1)

            def copy_logits(i, s):
                t = tile_of(i, s)
                dve.wait_ge(S["logits_done"], times(t + 1))
                dve.tensor_copy(logits[:, t, :], ps_m[:, D:D + E]).then_inc(S["logits_copied"], 1)

            def first_lo_parts(m):
                q = m % 2
                dve.wait_ge(S["hi_done"], times(m + 1))
                src, dst, at = (k_in[q], k_parts[q], (1, 3)) if m < 2 else (q_ln[q], q_parts[q], (2, 3))
                for a in at:
                    ins = dve.tensor_tensor(dst[:, :, a, :].bitcast(F32R), src[:, :].rearrange("p (h d) -> p h d", h=H),
                                            dst[:, :, 0, :], ALU.subtract)
                ins.then_inc(S["lo_done"], 1)

            stats1(0, 0)
            first_lo_parts(0)
            normalise(0, 0)
            stats1(0, 1)
            first_lo_parts(1)
            normalise(0, 1)
            copy_parts_T(0, 1, 0, ps[:, 0, :])
            first_lo_parts(2)
            copy_parts_T(0, 3, 0, ps[:, 2, :])
            first_lo_parts(3)
            copy_parts_T(0, 5, 0, ps[:, 0, :])
            copy_parts_T(0, 7, 0, ps[:, 2, :])
            dve.wait_ge(S["w_T_ps_done"], times(1))
            dve.tensor_copy(w_T[:, :, :].rearrange("p c n -> p (c n)"), ps_m[:, :]).then_inc(S["w_T_copied"], 1)
            dve.wait_ge(S["consts_done"], times(ATTENTION_CONSTS))
            dve.tensor_copy(ones_r[:, :], ones_row[:, :]).then_inc(S["bias_split"], 1)
            dve.wait_ge(L["weights_in"], landed(3))
            dve.tensor_copy(bias_parts[:, 0, :], bias_row[:, :]).then_inc(S["bias_split"], 1)
            dve.wait_ge(S["bias_split"], times(2))
            dve.tensor_tensor(bias_parts[:, 1, :], bias_row[:, :], bias_parts[:, 0, :].bitcast(F32), ALU.subtract)\
                .then_inc(S["bias_split"], 1)

            def step(i, s):
                if s % 2 == 0:
                    prep(dve, i, s, lambda b, k, u: copy_parts_T(b, k - 1, u))
                if i is not None:
                    maxes(i, s)
                if s % 4 != 2:
                    lag_task(dve, i, s, 2, copy_pt0)
                for lag, task in ((3, copy_rsum_T), (7, copy_xn_T), (4, norm_y), (8, copy_logits), (5, residual)):
                    if last_of_tile(s, lag):
                        lag_task(dve, i, s, lag, task)
                if s % 4 == 2:
                    lag_task(dve, i, s, 2, copy_pt0)
                if last_of_tile(s, 2):
                    lag_task(dve, i, s, 2, invert_sums)
                if last_of_tile(s, 5):
                    lag_task(dve, i, s, 5, stats2)
                if last_of_tile(s, 6):
                    lag_task(dve, i, s, 6, norm_x2)
                if s % 8 in (2, 4):
                    prep0(dve, i, s, lambda b, k, u: stats1(b, k // 2 - 1))
                if s % 8 in (3, 5):
                    prep0(dve, i, s, lambda b, k, u: normalise(b, k // 2 - 1))

            turns(dve, step, DEPTH)

            links["route"] = 0

            def link(ins):
                links["route"] += 1
                ins.then_inc(S["route_link"], 1)
                dve.wait_ge(S["route_link"], times(links["route"]))

            def over(ap, *shape):
                return ap.broadcast_to([P, *shape])

            dve.wait_ge(S["logits_copied"], times(N_TILE))
            dve.wait_ge(S["consts_done"], times(ATTENTION_CONSTS + 1))
            for k in range(2):
                lg = logits if k == 0 else rest
                if k == 1:
                    link(dve.scalar_tensor_tensor(out=rest[:, :, :], in0=choice[:, 0, :, :], scalar=-3e38,
                                                  in1=logits[:, :, :], op0=ALU.mult, op1=ALU.add))
                link(dve.tensor_reduce(best[:, k, :], lg[:, :, :], AX.X, ALU.max))
                link(dve.tensor_tensor(same[:, :, :], lg[:, :, :], over(best[:, k, :].unsqueeze(2), N_TILE, E),
                                       ALU.is_equal))
                link(dve.scalar_tensor_tensor(out=cand[:, :, :], in0=same[:, :, :], scalar=-float(E),
                                              in1=over(iota_e[:, :].unsqueeze(1), N_TILE, E),
                                              op0=ALU.mult, op1=ALU.add))
                link(dve.tensor_reduce(first[:, :], cand[:, :, :], AX.X, ALU.min))
                link(dve.tensor_tensor(choice[:, k, :, :], cand[:, :, :], over(first[:, :].unsqueeze(2), N_TILE, E),
                                       ALU.is_equal))
            dve.tensor_tensor(diff[:, :], best[:, 1, :], best[:, 0, :], ALU.subtract).then_inc(S["diff_done"], 1)
            dve.tensor_tensor(chosen[:, :, :], choice[:, 0, :, :], choice[:, 1, :, :], ALU.add)\
                .then_inc(S["chosen_done"], 1)
            dve.wait_ge(S["ex_done"], times(1))
            link(dve.tensor_scalar(gates[:, N_TILE:], ex[:, :], 1.0, None, ALU.add))
            link(dve.reciprocal(gates[:, 0:N_TILE], gates[:, N_TILE:]))
            link(dve.tensor_tensor(gates[:, N_TILE:], gates[:, 0:N_TILE], ex[:, :], ALU.mult))
            for k in range(2):
                link(dve.tensor_tensor(gate_of[:, k, :, :], choice[:, k, :, :],
                                       over(gates[:, N_TILE * k:N_TILE * k + N_TILE].unsqueeze(2), N_TILE, E),
                                       ALU.mult))
            dve.tensor_tensor(gate_of[:, 2, :, :], gate_of[:, 0, :, :], gate_of[:, 1, :, :], ALU.add)\
                .then_inc(S["gates_done"], 1)
            dve.wait_ge(S["rank_done"], times(1))
            flat = "p t e -> p (t e)"
            link(dve.tensor_copy(total[:, :, :].rearrange(flat), ps[:, 1, 0:P]))
            src = total
            for n, sh in enumerate((1, 2, 4, 8)):
                link(dve.tensor_copy(upto[n][:, 0:sh, :], src[:, 0:sh, :]))
                link(dve.tensor_tensor(upto[n][:, sh:, :], src[:, sh:, :], src[:, :N_TILE - sh, :], ALU.add))
                src = upto[n]
            link(dve.tensor_tensor(upto[4][:, :, :], src[:, :, :], total[:, :, :], ALU.subtract))
            link(dve.tensor_tensor(earlier[:, :, :].rearrange(flat), ps[:, 0, 0:P], upto[4][:, :, :].rearrange(flat),
                                   ALU.add))
            link(dve.tensor_scalar(tiles_i[:, :], src[:, N_TILE - 1, :], float(P - 1), None, ALU.add))
            link(dve.tensor_scalar(tiles_s[:, :], tiles_i[:, :], 7, None, ALU.arith_shift_right))
            link(dve.tensor_scalar(tiles_f[:, :], tiles_s[:, :], 1.0, None, ALU.max))
            src = tiles_f
            for n, sh in enumerate((1, 2, 4)):
                link(dve.tensor_copy(cum[n][:, 0:sh], src[:, 0:sh]))
                link(dve.tensor_tensor(cum[n][:, sh:], src[:, sh:], src[:, :E - sh], ALU.add))
                src = cum[n]
            link(dve.tensor_tensor(tile0[:, :], src[:, :], tiles_f[:, :], ALU.subtract))
            link(dve.scalar_tensor_tensor(out=place_e[:, :, :], in0=over(tile0[:, :].unsqueeze(1), N_TILE, E),
                                          scalar=float(P), in1=earlier[:, :, :], op0=ALU.mult, op1=ALU.add))
            for k in range(2):
                link(dve.tensor_tensor(picked[:, k, :, :], choice[:, k, :, :], place_e[:, :, :], ALU.mult))
            link(dve.tensor_reduce(pos[:, :], picked[:, :, :, :].rearrange("p k t e -> p (k t) e"), AX.X, ALU.add))
            link(dve.tensor_copy(pos_i[:, :], pos[:, :]))
            link(dve.tensor_scalar(row_i[:, :], pos_i[:, :], P - 1, None, ALU.bitwise_and))
            link(dve.tensor_scalar(til_i[:, :], pos_i[:, :], 7, None, ALU.arith_shift_right))
            link(dve.tensor_copy(row_f[:, :], row_i[:, :]))
            link(dve.tensor_copy(til_f[:, :], til_i[:, :]))
            for n in range(2):
                dve.wait_ge(L[f"x2_out{n}"], landed(N_TILE // 2))
                dve.wait_ge(L[f"xn_out{n}"], landed(N_TILE // 2))
            link(dve.tensor_tensor(til_hot[:, :, :], over(iota_tile[:, :].unsqueeze(1), N_CHOICE, SLOT_COLS),
                                   over(til_f[:, :].unsqueeze(2), N_CHOICE, SLOT_COLS), ALU.is_equal))
            for k in range(2):
                at = slice(N_TILE * k, N_TILE * k + N_TILE)
                dve.tensor_tensor(slot_vals[:, at, :], til_hot[:, at, :],
                                  over(token_id[:, :].unsqueeze(2), N_TILE, SLOT_COLS), ALU.mult)\
                    .then_inc(S["route_link"], 1)
                links["route"] += 1
            for a in range(0, N_CHOICE, HOT_CHUNK):
                dve.tensor_tensor(row_hot[:, a:a + HOT_CHUNK, :], over(iota_slot[:, :].unsqueeze(1), HOT_CHUNK, P),
                                  over(row_f[:, a:a + HOT_CHUNK].unsqueeze(2), HOT_CHUNK, P), ALU.is_equal)\
                    .then_inc(S["hots_done"], 1)
            link(dve.tensor_tensor(ge_tile[:, :, :], over(iota_tile[:, :].unsqueeze(2), SLOT_COLS, E - 1),
                                   over(tile0[:, 1:].unsqueeze(1), SLOT_COLS, E - 1), ALU.is_ge))
            link(dve.memset(tile_e[:, 0:1], -1.0))
            link(dve.tensor_reduce(tile_e[:, 1:], ge_tile[:, :, :], AX.X, ALU.add))
            link(dve.tensor_copy(tab_f[:, 0, :], tile_e[:, 1:]))
            link(dve.tensor_tensor(tile_new[:, :], tile_e[:, 1:], tile_e[:, 0:SLOT_COLS], ALU.subtract))
            link(dve.scalar_tensor_tensor(out=tab_f[:, 2, :], in0=tile_e[:, 1:], scalar=float(E - 1),
                                          in1=tile_new[:, :], op0=ALU.is_lt, op1=ALU.mult))
            link(dve.tensor_copy(tile_tab[:, 0, :], tab_f[:, 0, :]))
            link(dve.tensor_copy(tile_tab[:, 2, :], tab_f[:, 2, :]))
            link(dve.tensor_scalar(tile_tab[:, 1, :], tile_tab[:, 0, :], 1, None, ALU.bitwise_and))
            link(dve.tensor_scalar(tile_tab[:, 3, :], tile_tab[:, 1, :], 1, None, ALU.bitwise_xor))
            dve.wait_ge(S["slots_done"], times(1))
            link(dve.scalar_tensor_tensor(out=pad_row[:, :], in0=ps[:, 2, 0:SLOT_COLS], scalar=0.0,
                                          in1=over(part_id[:, :], SLOT_COLS), op0=ALU.is_equal, op1=ALU.mult))
            link(dve.scalar_tensor_tensor(out=slot_tok[:, :], in0=ps[:, 2, 0:SLOT_COLS], scalar=1.0,
                                          in1=pad_row[:, :], op0=ALU.subtract, op1=ALU.add))
            dve.nop().then_inc(S["tables_done"], 1)

            def x_lo(t, n):
                expert = dve.value_load(tile_tab[0:1, 0, bass.ds(t, 1)], min_val=0, max_val=E - 1)
                dve.wait_ge(S["xT_hi_done"], times(t + 1))
                dve.wait_ge(S["h3_done"], times((t - 2) * 2))
                dve.tensor_copy(slot_gate[:, bass.ds(t, 1)], xg[n][:, bass.ds(expert + D, 1)])\
                    .then_inc(S["gate_taken"], 1)
                dve.tensor_tensor(xT[n][:, 1, :, :], ps_xT[:, 0:D].rearrange("p (c t) -> p c t", c=NC),
                                  xT[n][:, 0, :, :].bitcast(F32), ALU.subtract).then_inc(S["xT_lo_done"], 1)

            def y_final(t, n):
                dve.wait_ge(S["y_small_done"], times(t + 1))
                dve.wait_ge(S["adds_landed"], times(t - 1))
                dve.scalar_tensor_tensor(out=y_out[n][:, :], in0=ps_out[:, 0:D], scalar=slot_gate[:, bass.ds(t, 1)],
                                         in1=y_small[:, :], op0=ALU.mult, op1=ALU.add).then_inc(S["y_done"], 1)

            x_lo(0, 0)
            with dve.Fori(0, N_SLOT_TILE // UNROLL) as i:
                for n in range(UNROLL):
                    t = i * UNROLL + n
                    for a in range(2):
                        dve.wait_ge(S["h3_done"], times(t * 2 + a + 1))
                        dve.wait_ge(S["silu_done"], times(t * 2 + a + 1))
                        dve.wait_ge(S["h_turned"], times((t - 1) * 2 + a + 1))
                        dve.tensor_tensor(hidden[:, HALF * a:HALF * a + HALF], ps_h[:, 1, a, :],
                                          gated[:, HALF * a:HALF * a + HALF], ALU.mult).then_inc(S["hidden_done"], 1)
                    if n < UNROLL - 1:
                        x_lo(t + 1, n + 1)
                    else:
                        with dve.If(i < N_SLOT_TILE // UNROLL - 1):
                            x_lo(t + 1, 0)
                    if n == 0:
                        with dve.If(i > 0):
                            y_final(within(t - 1, 2, N_SLOT_TILE - 2), UNROLL - 1)
                    else:
                        y_final(t - 1, n - 1)
                    for a in range(2):
                        dve.wait_ge(S["hT_hi_done"], times(t * 2 + a + 1))
                        dve.wait_ge(S["out_done"], times(t - 2))
                        dve.tensor_tensor(hT[n][:, 1, 4 * a:4 * a + 4, :],
                                          ps_hT[:, a, :].rearrange("p (c t) -> p c t", c=4),
                                          hT[n][:, 0, 4 * a:4 * a + 4, :].bitcast(F32), ALU.subtract)\
                            .then_inc(S["hT_lo_done"], 1)
            y_final(N_SLOT_TILE - 1, UNROLL - 1)

        @block.tensor
        def _(pe):
            start(pe, PE_SEMS)

            def parts_round(b, k, u, misc_free, bank=ps_m):
                m, half = (k - 1) // 2, (k - 1) % 2
                q = m % 2
                pe.wait_ge(S["lo_done"], times(b * 4 + m + 1))
                misc_free()
                src = (k_parts if m < 2 else q_parts)[q]
                for r in range(4):
                    pair = 4 * half + r
                    ins = pe.transpose(bank[:, P * r:P * r + P],
                                       src[:, 2 * pair:2 * pair + 2, :, :].rearrange("p h a d -> p (h a d)"),
                                       ident[:, :])
                ins.then_inc(S["parts_T_done"], 1)

            def parts_copied(b, k):
                pe.wait_ge(S["partsT0_copied"], times(b * 4 + (k + 1) // 2))
                pe.wait_ge(S["partsT1_copied"], times(b * 4 + k // 2))

            def scores(i, s):
                n, g, u, q = i * SPT + s, s % 2, s // 8, (s // 4) % 2
                b = i * 2 + u
                pe.wait_ge(S["exp_done"], times(n - 1))
                if s % 8 == 0:
                    parts_copied(b, 6)
                if s % 8 == 4:
                    parts_copied(b, 8)
                for par in range(2):
                    pe.matmul(ps_s[:, g, par, 0:2 * SPAN], ident_bf[:, :],
                              mask[:, q, :].unsqueeze(1).broadcast_to([P, 2, SPAN]), start=True, stop=False)
                    for r in range(2):
                        pair = 2 * (s % 4) + r
                        rows = slice(64 * par, 64 * par + 64)
                        ins = pe.matmul(ps_s[:, g, par, SPAN * r:SPAN * r + SPAN],
                                        qT[u][rows, pair, P * q:P * q + P],
                                        kT[u][rows, pair, WIN * q:WIN * q + SPAN], start=False, stop=(r == 1))
                ins.then_inc(S["scores_done"], 1)

            def prob_transposes(i, s):
                n, g = i * SPT + s, s % 2
                pe.wait_ge(S["exp_done"], times(n + 1))
                pe.wait_ge(S["pt0_copied"], times(n))
                pe.wait_ge(S["pt1_copied"], times(n))
                for r in range(2):
                    for j in range(3):
                        ins = pe.transpose(ps_pt[:, r, P * j:P * j + P],
                                           probs[g][:, r, j, :, :].rearrange("p e c -> p (e c)"), ident[:, :])
                ins.then_inc(S["ptrans_done"], 1)

            def values(i, s):
                n, g, u, q = i * SPT + s, s % 2, s // 8, (s // 4) % 2
                pe.wait_ge(S["pt0_copied"], times(n + 1))
                pe.wait_ge(S["pt1_copied"], times(n + 1))
                if s % 4 == 0:
                    pe.wait_ge(S["y_raw_done"], times(tile_of(i, s)))
                if s % 8 == 0:
                    pe.wait_ge(S["v_bd_done"], times((i * 2 + u) * 2 + 2))
                for r in range(2):
                    pair = 2 * (s % 4) + r
                    c, row = pair // 4, 32 * (pair % 4)
                    for j in range(3):
                        ins = pe.matmul(ps_y[row:row + 32, c, :], v_bd[u][:, q + j, pair, :],
                                        probs_T[g][:, r, j, :], start=(j == 0), stop=(j == 2))
                ins.then_inc(S["pv_done"], 1)

            def tail_sums(i, s):
                t = tile_of(i, s)
                pe.wait_ge(S["rsum_done"], times(t + 1))
                pe.transpose(ps_m[0:H, D:D + P], rsum[:, :], ident[:, :]).then_inc(S["rsum_T_done"], 1)

            def tail_broadcast(i, s):
                t = tile_of(i, s)
                pe.wait_ge(S["rsum_T_copied"], times(t + 1))
                pe.wait_ge(S["consts_done"], times(ATTENTION_CONSTS))
                for c in range(NC):
                    ins = pe.matmul(ps_m[:, P * c:P * c + P], head_sel[:, c, :], rsum_T[:, :],
                                    start=True, stop=True)
                ins.then_inc(S["rbc_done"], 1)

            def tail_project(i, s):
                t = tile_of(i, s)
                pe.wait_ge(S["y_norm_done"], times(t + 1))
                pe.wait_ge(S["bias_split"], times(3))
                for part in range(2):
                    pe.matmul(ps_m[:, 0:D], ones_r[:, :], bias_parts[:, part, :], start=(part == 0), stop=False)
                for c in range(NC):
                    ins = pe.matmul(ps_m[:, 0:D], y_norm[:, c, :], w_T[:, c, :], start=False, stop=(c == NC - 1))
                ins.then_inc(S["proj_done"], 1)

            def tail_turn(i, s):
                t, q = tile_of(i, s), (s // 4) % 2
                pe.wait_ge(S["xn_done"], times(t + 1))
                for c in range(NC):
                    ins = pe.transpose(ps_m[:, P * c:P * c + P], xn[q][:, P * c:P * c + P], ident[:, :])
                ins.then_inc(S["xn_T_ps_done"], 1)

            def tail_logits(i, s):
                t = tile_of(i, s)
                pe.wait_ge(S["xn_T_copied"], times(t + 1))
                for c in range(NC):
                    ins = pe.matmul(ps_m[:, D:D + E], xn_T[:, c, :], wg_s[:, c, :], start=(c == 0), stop=(c == NC - 1))
                ins.then_inc(S["logits_done"], 1)

            TAIL = {2: ((7, tail_turn, "xn_T_copied"), (3, tail_sums, "rsum_T_copied")),
                    3: ((8, tail_logits, "logits_copied"), (4, tail_broadcast, "y_norm_done")),
                    0: ((5, tail_project, "x2_done"),)}

            def tail_emptied(i, s):
                for lag, _, copied in TAIL[s % 4]:
                    if i is None:
                        pe.wait_ge(S[copied], times(min((NIT - 1) * 4 + (s - lag) // 4 + 1, N_TILE)))
                    else:
                        pe.wait_ge(S[copied], times(i * 4 + ((s - lag) // 4 + 1)))

            pe.wait_ge(S["consts_done"], times(1))
            for k in range(1, 9):
                parts_round(0, k, 0, lambda: parts_copied(0, k - 4), ps[:, (k - 1) % 4, :])
            pe.wait_ge(L["weights_in"], landed(3))
            for c in range(NC):
                for r in range(NC):
                    ins = pe.transpose(ps_m[:, D * c + P * r:D * c + P * r + P], w_nat[:, r, P * c:P * c + P],
                                       ident[:, :])
            ins.then_inc(S["w_T_ps_done"], 1)
            parts_copied(0, 8)
            pe.wait_ge(S["consts_done"], times(4))

            def step(i, s):
                if i is not None:
                    scores(i, s)
                lag_task(pe, i, s, 2, prob_transposes)
                if s % 4 in TAIL and (i is not None or any(s - lag < SPT for lag, _, _ in TAIL[s % 4])):
                    if i is not None:
                        b, k = i * 2 + s // 8, s % 8
                        if k == 0:
                            parts_copied(b, 7)
                        elif s < 8:
                            parts_copied(b + 1, k - 1)
                        else:
                            if k == 2:
                                parts_copied(b, 8)
                            with pe.If(i < NIT - 1):
                                parts_copied(b + 1, k - 1)
                    tail_emptied(i, s - 2 if s % 4 == 2 else s - 1)
                    for lag, task, _ in TAIL[s % 4]:
                        lag_task(pe, i, s, lag, task)
                lag_task(pe, i, s, 3, values)

                def bank_free(b, k):
                    if s == 1:
                        pe.wait_ge(S["w_T_copied"], times(1))
                    if s % 4 in TAIL:
                        tail_emptied(i, s)
                    if s % 4 == 1 or s <= 4:
                        parts_copied(b, k - 1)

                prep(pe, i, s, lambda b, k, u: parts_round(b, k, u, lambda: bank_free(b, k)))

            turns(pe, step, DEPTH)

            pe.wait_ge(S["chosen_done"], times(1))
            flat = chosen[:, :, :].rearrange("p t e -> p (t e)")
            pe.matmul(ps[:, 0, 0:P], before[:, :], flat, start=True, stop=True)
            pe.matmul(ps[:, 1, 0:P], ones[:, :], flat, start=True, stop=True).then_inc(S["rank_done"], 1)
            for a in range(N_CHOICE):
                if a % HOT_CHUNK == 0:
                    pe.wait_ge(S["hots_done"], times(a // HOT_CHUNK + 1))
                ins = pe.matmul(ps[:, 2, 0:SLOT_COLS], row_hot[:, a, :], slot_vals[:, a, :],
                                start=(a == 0), stop=(a == N_CHOICE - 1))
            ins.then_inc(S["slots_done"], 1)
            pe.wait_ge(S["tables_done"], times(1))

            def turn_x(t, n, landed):
                pe.wait_ge(L[f"xg{n}"], landed * 16)
                pe.wait_ge(S["xT_lo_done"], times(t))
                for c in range(NC):
                    ins = pe.transpose(ps_xT[:, P * c:P * c + P], xg[n][:, P * c:P * c + P], ident[:, :])
                ins.then_inc(S["x_turned"], 1)

            def down(t, n, slot):
                pe.wait_ge(S["hT_lo_done"], times(t * 2 + 2))
                pe.wait_ge(S["y_done"], times(t))
                w = wts[:, slot, 2, :].rearrange("p (c a n) -> p c a n", c=NF, a=2)
                for c in range(NF):
                    pe.matmul(ps_out[:, :], hT[n][:, 0, c, :], w[:, c, :, :].rearrange("p a n -> p (a n)"),
                              start=(c == 0), stop=False)
                    ins = pe.matmul(ps_out[:, 0:D], hT[n][:, 1, c, :], w[:, c, 0, :],
                                    start=False, stop=(c == NF - 1))
                ins.then_inc(S["out_done"], 1)

            turn_x(0, 0, 1)
            with pe.Fori(0, N_SLOT_TILE // UNROLL) as i:
                for n in range(UNROLL):
                    t = i * UNROLL + n
                    expert = pe.value_load(tile_tab[0:1, 0, bass.ds(t, 1)], min_val=0, max_val=E - 1)
                    slot = pe.value_load(tile_tab[0:1, 1, bass.ds(t, 1)], min_val=0, max_val=1)
                    pe.wait_ge(S["xT_lo_done"], times(t + 1))
                    pe.wait_ge(S["w_lo_done"], times(expert * 3 + 3))
                    for a in range(2):
                        for m in range(2):
                            pe.wait_ge(S["silu_done" if m == 0 else "hidden_done"], times((t - 1) * 2 + a + 1))
                            w = wts[:, slot, m, :].rearrange("p (a c f) -> p a c f", a=2, c=NC)
                            for c in range(NC):
                                for part, x_part in ((0, 0), (1, 0), (0, 1)):
                                    ins = pe.matmul(ps_h[:, m, a, :], xT[n][:, x_part, c, :],
                                                    w[:, part, c, HALF * a:HALF * a + HALF],
                                                    start=(c == 0 and part + x_part == 0),
                                                    stop=(c == NC - 1 and x_part == 1))
                            ins.then_inc(S["h1_done" if m == 0 else "h3_done"], 1)
                    if n < UNROLL - 1:
                        turn_x(t + 1, n + 1, i + 1)
                    else:
                        with pe.If(i < N_SLOT_TILE // UNROLL - 1):
                            turn_x(t + 1, 0, i + 2)
                    if n == 0:
                        with pe.If(i > 0):
                            down(t - 1, UNROLL - 1, pe.value_load(
                                tile_tab[0:1, 1, bass.ds(within(t - 1, 2, N_SLOT_TILE - 2), 1)], min_val=0, max_val=1))
                    else:
                        down(t - 1, n - 1, pe.value_load(tile_tab[0:1, 1, bass.ds(t - 1, 1)], min_val=0, max_val=1))
                    for a in range(2):
                        pe.wait_ge(S["hidden_done"], times(t * 2 + a + 1))
                        pe.wait_ge(S["hT_lo_done"], times((t - 1) * 2 + a + 1))
                        for c in range(4):
                            ins = pe.transpose(ps_hT[:, a, P * c:P * c + P],
                                               hidden[:, HALF * a + P * c:HALF * a + P * c + P], ident[:, :])
                        ins.then_inc(S["h_turned"], 1)
            down(N_SLOT_TILE - 1, UNROLL - 1, pe.value_load(
                tile_tab[0:1, 1, N_SLOT_TILE - 1:N_SLOT_TILE], min_val=0, max_val=1))


_INS = ['x', 'ctx_1024', 'L0_xattn_W_proj', 'L0_xattn_b_proj', 'L0_ffn_Wg', 'L0_ffn_W1', 'L0_ffn_W3', 'L0_ffn_W2']


def kernel(**inputs):
    import numpy as _np
    import concourse.bacc as _bacc
    from concourse import mybir as _mybir
    from concourse.bass_utils import run_bass_kernel_spmd as _run

    nc = _bacc.Bacc("TRN2", target_bir_lowering=False, num_devices=1)
    arrays, args = {}, []
    for name in _INS:
        a = _np.ascontiguousarray(inputs[name])
        arrays[f"in_{name}_dram"] = a
        args.append(nc.dram_tensor(f"in_{name}_dram", a.shape, _mybir.dt.from_np(a.dtype), kind="ExternalInput").ap())
    out = nc.dram_tensor("out_0_dram", (N_TOK + PAD_ROWS, D), _mybir.dt.float32, kind="ExternalOutput").ap()
    xn_rows = nc.dram_tensor("xn_rows_dram", (N_TOK + PAD_ROWS, D + E), _mybir.dt.float32, kind="Internal").ap()
    attention_and_experts(nc, *args, out, xn_rows)
    r = _run(nc, [arrays], core_ids=[0])
    return r.results[0]["out_0_dram"][:N_TOK].reshape(B, T, D)
```

```python
from contextlib import ExitStack

import concourse.bass as bass
from concourse import mybir

B, T, D = 8, 256, 256
P = 128
N_TOK = B * T
N_TILE = N_TOK // P
H, HD = 16, 16
WIN = 64
NKB = T // WIN
SPAN = 3 * WIN
NC = D // P
NPAIR = H // 2
E, F_DIM = 8, 1024
N_ASSIGN = 2 * N_TOK
N_CHOICE = 2 * N_TILE
N_SLOT_TILE = (N_ASSIGN + E * P - 1) // P
SLOT_COLS = N_SLOT_TILE + 1
NF = F_DIM // P
HALF = F_DIM // 2
MAT = 2 * 2 * F_DIM
UNROLL = 3
PAD_ROWS = P
HOT_CHUNK = 8
WARM_UP = (16, 4)
PAD_T = 8
ATTENTION_CONSTS = 7
EPS = 1e-5
MASKED = -1e30
NIT = 4
SPT = 16
BASE = 64


def attention_and_experts(nc, x, ctx, w_proj, b_proj, wg, w1, w3, w2, out, xn_rows):
    F32, F32R, I32 = mybir.dt.float32, mybir.dt.float32r, mybir.dt.int32
    BF16, F16 = mybir.dt.bfloat16, mybir.dt.float16
    ALU, ACT, AX = mybir.AluOpType, mybir.ActivationFunctionType, mybir.AxisListType

    x_t = x.rearrange("b (q p) d -> (b q) p d", p=P)
    ctx_t = ctx.rearrange("b (q p) d -> (b q) p d", p=P)
    ctx_v = ctx.rearrange("b (j p) d -> b p j d", p=WIN)
    out_t = out.rearrange("(t p) d -> t p d", p=P)
    xn_t = xn_rows.rearrange("(t p) d -> t p d", p=P)

    with ExitStack() as stack:
        def sem(name):
            s = stack.enter_context(nc.semaphore(name))
            return s

        place = {"at": (nc.sbuf_base + 63) // 64 * 64}

        def sb(name, shape, dt):
            size = 1
            for n in shape[1:]:
                size *= n
            size *= 2 if dt in (BF16, F16) else 4
            t = nc.alloc_sbuf_tensor_at(name, shape, dt, offset=place["at"])
            place["at"] += (size + 63) // 64 * 64
            return t

        def pb(name, shape, dt):
            return stack.enter_context(nc.psum_tensor(name, shape, dt))

        ident = sb("ident", [P, P], F32)
        ident_bf = sb("ident_bf", [P, P], BF16)
        mask = sb("mask", [P, 2, SPAN], BF16)
        head_sel = sb("head_sel", [H, NC, P], F32)
        ones_row = sb("ones_row", [1, P], F32)
        bias_row = sb("bias_row", [1, D], F32)
        ones_r = sb("ones_r", [1, P], F32R)
        bias_parts = sb("bias_parts", [1, 2, D], F32R)
        neg_half = sb("neg_half", [P, 1], F32)
        w_nat = sb("w_nat", [P, NC, D], F32)
        w_T = sb("w_T", [P, NC, D], F32)
        wg_s = sb("wg_s", [P, NC, E], F32)
        logits = sb("logits", [P, N_TILE, E], F32)

        iota_e = sb("iota_e", [P, E], F32)
        iota_slot = sb("iota_slot", [P, P], F32)
        iota_tile = sb("iota_tile", [P, SLOT_COLS], F32)
        token_id = sb("token_id", [P, N_TILE], F32)
        part_id = sb("part_id", [P, 1], F32)
        before = sb("before", [P, P], F32)
        ones = sb("ones", [P, P], F32)

        slot_tok = sb("slot_tok", [P, SLOT_COLS], I32)
        slot_gate = sb("slot_gate", [P, SLOT_COLS], F32)
        tile_tab = sb("tile_tab", [P, 5, SLOT_COLS], I32)
        raw = [sb(f"raw{m}", [P, 2 * F_DIM], F32) for m in range(3)]
        wts = sb("wts", [P, 2, 3, MAT], F32R)
        behind_first = place["at"] - 3 * MAT * 4
        behind_wts = place["at"]

        place["at"] = behind_first
        k_in = [sb(f"k_in{q}", [P, D], F32) for q in range(2)]
        x_in = [sb(f"x_in{q}", [P, D], F32) for q in range(2)]
        v_in = sb("v_in", [P, NKB, D], F32)
        v_bd = [sb(f"v_bd{u}", [P, NKB, NPAIR, 2 * HD], F32) for u in range(2)]
        q_ln = [sb(f"q_ln{q}", [P, D], F32) for q in range(2)]
        k_parts = [sb(f"k_parts{q}", [P, H, 4, HD], F32) for q in range(2)]
        q_parts = [sb(f"q_parts{q}", [P, H, 4, HD], F32) for q in range(2)]
        kT = [sb(f"kT{u}", [P, NPAIR, T], F32R) for u in range(2)]
        qT = [sb(f"qT{u}", [P, NPAIR, T], F32R) for u in range(2)]
        neg_max = [sb(f"neg_max{g}", [P, 4], F32) for g in range(2)]
        probs = [sb(f"probs{g}", [P, 2, 3, 2, WIN], F32) for g in range(2)]
        probs_T = [sb(f"probs_T{g}", [P, 6, P], F32) for g in range(2)]
        sums = [sb(f"sums{g}", [P, H], F32) for g in range(2)]
        rsum = sb("rsum", [P, H], F32)
        rsum_T = sb("rsum_T", [H, P], F32)
        y_raw = sb("y_raw", [P, NC, P], F32)
        y_norm = sb("y_norm", [P, NC, P], F32)
        x_res = [sb(f"x_res{q}", [P, D], F32) for q in range(2)]
        x2 = [sb(f"x2_{q}", [P, D], F32) for q in range(2)]
        xn = [sb(f"xn_{q}", [P, D], F32) for q in range(2)]
        xn_T = sb("xn_T", [P, NC, P], F32)
        zero_rows = sb("zero_rows", [P, D + E], F32)
        st1 = sb("st1", [P, 6], F32)
        mv1 = sb("mv1", [P, 2], F32)
        ve1 = sb("ve1", [P, 1], F32)
        rstd1 = sb("rstd1", [P, 1], F32)
        st2 = sb("st2", [P, 6], F32)
        mv2 = sb("mv2", [P, 2], F32)
        ve2 = sb("ve2", [P, 1], F32)
        rstd2 = sb("rstd2", [P, 1], F32)

        assert place["at"] <= nc.sbuf_usable_end

        place["at"] = behind_wts

        def table(name, *shape, dt=F32):
            return sb(name, [P, *shape], dt)

        best = table("best", 2, N_TILE)
        choice = table("choice", 2, N_TILE, E)
        same = table("same", N_TILE, E)
        cand = table("cand", N_TILE, E)
        first = table("first", N_TILE)
        rest = table("rest", N_TILE, E)
        chosen = table("chosen", N_TILE, E)
        upto = table("upto", 5, PAD_T + N_TILE, E)
        earlier = table("earlier", N_TILE, E)
        place_e = table("place_e", N_TILE, E)
        picked = table("picked", 2, N_TILE, E)
        tiles_i = table("tiles_i", E, dt=I32)
        tiles_s = table("tiles_s", E, dt=I32)
        cum = table("cum", 4, PAD_T + E)
        tile0 = table("tile0", E)
        pos = table("pos", N_CHOICE)
        pos_i = table("pos_i", N_CHOICE, dt=I32)
        row_i = table("row_i", N_CHOICE, dt=I32)
        til_i = table("til_i", N_CHOICE, dt=I32)
        row_f = table("row_f", N_CHOICE)
        til_f = table("til_f", N_CHOICE)
        diff = table("diff", N_TILE)
        ex = table("ex", N_TILE)
        gates = table("gates", N_CHOICE)
        gates_2nd = table("gates_2nd", N_TILE)
        gate_of = table("gate_of", 3, N_TILE, E)
        row_hot = table("row_hot", N_CHOICE, P, dt=F16)
        til_hot = table("til_hot", N_CHOICE, SLOT_COLS)
        slot_vals = table("slot_vals", N_CHOICE, SLOT_COLS, dt=F16)
        ge_tile = table("ge_tile", SLOT_COLS, E - 1)
        tile_e = table("tile_e", SLOT_COLS + 1)
        tile_new = table("tile_new", SLOT_COLS)
        pad_row = table("pad_row", SLOT_COLS)
        tab_f = table("tab_f", 4, SLOT_COLS)
        assert place["at"] <= nc.sbuf_usable_end

        behind_tables = place["at"]

        place["at"] = behind_wts
        xT = [table(f"xT{n}", 2, NC, P, dt=F32R) for n in range(UNROLL)]
        gated = table("gated", F_DIM)
        hidden = table("hidden", F_DIM)
        hT = [table(f"hT{n}", 2, NF, P, dt=F32R) for n in range(UNROLL)]
        y_small = table("y_small", D)
        y_out = [table(f"y_out{n}", D) for n in range(UNROLL)]
        place["at"] = max(place["at"], behind_tables)
        gather_row = [table(f"gather_row{n}", 1, dt=I32) for n in range(UNROLL)]
        add_row = [table(f"add_row{n}", 1, dt=I32) for n in range(UNROLL)]
        xg = [table(f"xg{n}", D + E) for n in range(UNROLL)]
        assert place["at"] <= nc.sbuf_usable_end

        ps = pb("ps", [P, 8, 512], F32)
        ps_s = ps[:, 0:4, :].rearrange("p (g e) c -> p g e c", g=2)
        ps_pt = ps[:, 4:6, :]
        ps_tail = ps[:, 5, 2 * P:4 * P]
        ps_y = ps[:, 6, 0:D].rearrange("p (c t) -> p c t", c=NC)
        ps_m = ps[:, 7, :]
        ps_h = ps[:, 0:4, :].rearrange("p (m a) c -> p m a c", m=2)
        ps_hT = ps[:, 4:6, :]
        ps_out = ps[:, 6, :]
        ps_xT = ps[:, 7, :]

        PE_SEMS = ["scores_done", "ptrans_done", "pv_done", "parts_T_done", "rsum_T_done", "rbc_done",
                   "proj_done", "xn_T_ps_done", "logits_done", "w_T_ps_done",
                   "rank_done", "slots_done", "x_turned", "h1_done", "h3_done", "h_turned", "out_done"]
        DVE_SEMS = ["max_done", "pt1_copied", "partsT0_copied", "v_bd_done", "q_ln_done", "ln1_stats", "rsum_done",
                    "rsum_T_copied", "y_norm_done", "x2_done", "ln2_stats", "xn_done", "xn_T_copied", "logits_copied",
                    "w_T_copied", "bias_split", "route_link", "diff_done", "chosen_done", "hots_done",
                    "first_gates_done", "til_hot_done",
                    "slots_read", "tables_done",
                    "xT_lo_done", "hidden_done", "hT_lo_done", "y_done", "ln1_link", "ln2_link", "gate_taken",
                    "dve_waited"]
        ACT_SEMS = ["exp_done", "pt0_copied", "partsT1_copied", "hi_done", "y_raw_done", "ex_done",
                    "silu_done", "xT_hi_done", "hT_hi_done", "y_small_done", "w_hi_done"]
        POOL_SEMS = ["lo_done", "rstd1_done", "rstd2_done", "consts_done", "pool_link", "w_lo_done", "w3_lo_done",
                     "gate_link", "gates_done", "slot_vals_done",
                     "rows_read", "adds_landed", "pool_waited"]
        SP_SEMS = ["sp_waited"]
        S = {n: sem(n) for n in PE_SEMS + DVE_SEMS + ACT_SEMS + POOL_SEMS + SP_SEMS}
        DMA_SEMS = ["k_in0", "k_in1", "x_in0", "x_in1", "v_in", "x_res0", "x_res1", "weights_in",
                    "x2_out0", "x2_out1", "xn_out0", "xn_out1", "zero_out", "gates_out",
                    "raw0", "raw1", "raw2"]
        POOL_DMA_SEMS = ["xg0", "xg1", "xg2", "added"]
        L = {n: sem("dma_" + n) for n in DMA_SEMS + POOL_DMA_SEMS}

        def start(eng, names):
            for n in names:
                eng.sem_inc(S[n], BASE)

        def times(count):
            return count + BASE

        def landed(count):
            return count * 16 + BASE

        def within(value, low, high):
            return nc.s_assert_within(value, low, high, skip_runtime_bounds_check_because=
                                      "the If around it leaves the loop's register in this range")

        def lagged(eng, i, s, lag, task):
            if s >= lag:
                task(i, s - lag)
            else:
                with eng.If(i > 0):
                    task(within(i - 1, 0, NIT - 2), s - lag + SPT)

        def last_of_tile(s, lag):
            return (s - lag) % 4 == 3

        def tile_of(i, s):
            return i * 4 + s // 4

        def turns(eng, step, depth):
            with eng.Fori(0, NIT) as i:
                for s in range(SPT):
                    step(i, s)
            for s in range(SPT, SPT + depth):
                step(None, s)

        def lag_task(eng, i, s, lag, task):
            if i is None:
                if s - lag < SPT:
                    task(NIT - 1, s - lag)
            else:
                lagged(eng, i, s, lag, task)

        DEPTH = 11

        def prep(eng, i, s, task, late=0):
            if i is None:
                return
            u, k = s // 8, s % 8
            if u == 0 and k <= late:
                with eng.If(i > 0):
                    task(i * 2, 8 + k, 0)
            elif k <= late:
                task(i * 2 + 1, 8 + k, 1)
            elif u == 0:
                task(i * 2 + 1, k, 1)
            else:
                with eng.If(i < NIT - 1):
                    task(within(i * 2 + 2, 2, B - 2), k, 0)

        def prep0(eng, i, s, task):
            if i is None:
                return
            u, k = s // 8, s % 8
            if u == 0:
                task(i * 2 + 1, k, 1)
            else:
                with eng.If(i < NIT - 1):
                    task(within(i * 2 + 2, 2, B - 2), k, 0)

        block = stack.enter_context(nc.Block())

        @block.sync
        def _(sp):
            for n in DMA_SEMS:
                sp.sem_inc(L[n], BASE)
            start(sp, SP_SEMS)

            def load_item(b, m):
                if m < 2:
                    sp.wait_ge(S["lo_done"], times((b - 1) * 4 + m + 1))
                    sp.dma_start(k_in[m][:, :], ctx_t[b * 2 + m, :, :]).then_inc(L[f"k_in{m}"], 16)
                else:
                    sp.wait_ge(S["q_ln_done"], times((b - 1) * 2 + m - 1))
                    sp.dma_start(x_in[m - 2][:, :], x_t[b * 2 + m - 2, :, :]).then_inc(L[f"x_in{m - 2}"], 16)

            def load_v(b):
                sp.wait_ge(S["v_bd_done"], times(b * 2))
                for half in range(2):
                    sp.dma_start(v_in[WIN * half:WIN * half + WIN, :, :], ctx_v[b, :, :, :])\
                        .then_inc(L["v_in"], 16)

            for m in range(4):
                load_item(0, m)
            load_v(0)
            sp.dma_start(w_nat[:, :, :], w_proj.rearrange("(c p) d -> p c d", p=P)).then_inc(L["weights_in"], 16)
            sp.dma_start(bias_row[:, :], b_proj.rearrange("(a n) -> a n", a=1)).then_inc(L["weights_in"], 16)
            sp.dma_start(wg_s[:, :, :], wg.rearrange("(c p) e -> p c e", p=P)).then_inc(L["weights_in"], 16)
            for m in range(3):
                load_item(1, m)
            w_dram = [w1.rearrange("e (c p) f -> e p c f", p=P), w3.rearrange("e (c p) f -> e p c f", p=P),
                      w2.rearrange("e (c p) n -> e p c n", p=P)]

            def load_expert(e, m):
                c = NC if m < 2 else NF
                sp.dma_start(raw[m][:, :].rearrange("p (c n) -> p c n", c=c), w_dram[m][e, :, :, :])\
                    .then_inc(L[f"raw{m}"], 16)

            for m in range(3):
                load_expert(0, m)
            sp.wait_ge(S["consts_done"], times(ATTENTION_CONSTS))
            sp.dma_start(out_t[N_TILE, :, :], zero_rows[:, 0:D]).then_inc(L["zero_out"], 16)
            sp.dma_start(xn_t[N_TILE, :, :], zero_rows[:, :]).then_inc(L["zero_out"], 16)

            def store_x2(i, s):
                t, q = tile_of(i, s), (s // 4) % 2
                sp.wait_ge(S["x2_done"], times(t + 1))
                sp.dma_start(out_t[t, :, :], x2[q][:, :]).then_inc(L[f"x2_out{q}"], 16)

            def store_xn(i, s):
                t, q = tile_of(i, s), (s // 4) % 2
                sp.wait_ge(S["xn_done"], times(t + 1))
                sp.dma_start(xn_t[t, :, 0:D], xn[q][:, :]).then_inc(L[f"xn_out{q}"], 16)

            def step(i, s):
                if i is not None:
                    u, k = s // 8, s % 8
                    if k in (2, 4, 6):
                        with sp.If(i < NIT - 1):
                            load_item(within(i * 2 + (u + 2), u + 2, B - 2 + u), k // 2 - 1)
                    if k == 0:
                        if u == 0:
                            load_item(i * 2 + 1, 3)
                            load_v(i * 2 + 1)
                        else:
                            with sp.If(i < NIT - 1):
                                nxt = within(i * 2 + 2, 2, B - 2)
                                load_item(nxt, 3)
                                load_v(nxt)
                    if s % 4 == 3:
                        t, q = tile_of(i, s), (s // 4) % 2
                        sp.wait_ge(S["x2_done"], times(t - 1))
                        sp.dma_start(x_res[q][:, :], x_t[t, :, :]).then_inc(L[f"x_res{q}"], 16)
                if last_of_tile(s, 5):
                    lag_task(sp, i, s, 5, store_x2)
                if last_of_tile(s, 6):
                    lag_task(sp, i, s, 6, store_xn)

            turns(sp, step, DEPTH)
            sp.wait_ge(S["gates_done"], times(1))
            sp.dma_start(xn_rows.rearrange("(t p) d -> p t d", p=P)[:, 0:N_TILE, D:D + E], gate_of[:, 2, :, :])\
                .then_inc(L["gates_out"], 16)
            with sp.Fori(1, E) as e:
                for m in range(3):
                    if m == 1:
                        sp.wait_ge(S["w3_lo_done"], times(e))
                    else:
                        sp.wait_ge(S["w_lo_done"], times((e - 1) * 2 + m // 2 + 1))
                    sp.nop().then_inc(S["sp_waited"], 1)
                    load_expert(e, m)
            for n in ("x2_out0", "x2_out1", "xn_out0", "xn_out1"):
                sp.wait_ge(L[n], landed(N_TILE // 2))
            sp.wait_ge(L["zero_out"], landed(2))
            sp.wait_ge(L["added"], N_SLOT_TILE * 16)

        @block.gpsimd
        def _(pool):
            start(pool, POOL_SEMS)
            def rstd1_task(b, q):
                pool.wait_ge(S["ln1_stats"], times(b * 2 + q + 1))
                pool.tensor_tensor(rstd1[:, :], ve1[:, :], neg_half[:, :], ALU.pow).then_inc(S["rstd1_done"], 1)

            pool.memset(ident[:, :], 0.0).then_inc(S["pool_link"], 1)
            pool.memset(ident_bf[:, :], 0.0).then_inc(S["pool_link"], 1)
            pool.memset(mask[:, :, :], 0.0).then_inc(S["pool_link"], 1)
            pool.memset(neg_half[:, :], -0.5).then_inc(S["pool_link"], 1)
            pool.wait_ge(S["pool_link"], times(4))
            for m in (ident, ident_bf):
                pool.affine_select(out=m[:, :], in_=m[:, :], compare_op=ALU.not_equal, fill=1.0, base=0,
                                   pattern=[[-1, P]], channel_multiplier=1).then_inc(S["consts_done"], 1)
            for q in range(2):
                pool.affine_select(out=mask[:, q, :], in_=mask[:, q, :], compare_op=ALU.is_ge, fill=MASKED,
                                   base=WIN + WIN * q, pattern=[[-1, SPAN]], channel_multiplier=1)\
                    .then_inc(S["pool_link"], 1)
            rstd1_task(0, 0)
            pool.wait_ge(S["pool_link"], times(6))
            for q in range(2):
                pool.affine_select(out=mask[:, q, :], in_=mask[:, q, :], compare_op=ALU.is_ge, fill=MASKED,
                                   base=WIN - WIN * q, pattern=[[1, SPAN]], channel_multiplier=-1)\
                    .then_inc(S["consts_done"], 1)
            rstd1_task(0, 1)
            for u in range(2):
                pool.memset(v_bd[u][:, :, :, :], 0.0).then_inc(S["consts_done"], 1)
            pool.memset(ones_row[:, :], 1.0).then_inc(S["pool_link"], 1)
            pool.memset(zero_rows[:, :], 0.0).then_inc(S["pool_link"], 1)
            pool.memset(head_sel[:, :, :], 1.0).then_inc(S["pool_link"], 1)
            pool.wait_ge(S["pool_link"], times(9))
            pool.affine_select(out=head_sel[:, :, :], in_=head_sel[:, :, :], compare_op=ALU.is_ge, fill=0.0,
                               base=0, pattern=[[P, NC], [1, P]], channel_multiplier=-HD)\
                .then_inc(S["pool_link"], 1)
            pool.wait_ge(S["pool_link"], times(10))
            pool.affine_select(out=head_sel[:, :, :], in_=head_sel[:, :, :], compare_op=ALU.is_ge, fill=0.0,
                               base=HD - 1, pattern=[[-P, NC], [-1, P]], channel_multiplier=HD)\
                .then_inc(S["consts_done"], 1)

            def count(out, pattern, base, per_partition):
                pool.iota(out, pattern, base=base, channel_multiplier=per_partition,
                          allow_small_or_imprecise_dtypes=True).then_inc(S["pool_link"], 1)

            count(iota_e[:, :], [[1, E]], 0, 0)
            count(iota_slot[:, :], [[1, P]], 0, 0)
            count(iota_tile[:, :], [[1, SLOT_COLS]], 0, 0)
            count(token_id[:, :], [[P, N_TILE]], 1, 1)
            count(part_id[:, :], [[1, 1]], N_TOK + 1, 1)
            pool.memset(before[:, :], 0.0).then_inc(S["pool_link"], 1)
            pool.memset(ones[:, :], 1.0).then_inc(S["pool_link"], 1)
            pool.wait_ge(S["pool_link"], times(17))
            pool.affine_select(out=before[:, :], in_=before[:, :], compare_op=ALU.is_gt, fill=-1.0, base=0,
                               pattern=[[1, P]], channel_multiplier=-1).then_inc(S["pool_link"], 1)
            pool.wait_ge(S["pool_link"], times(18))
            pool.nop().then_inc(S["consts_done"], 1)

            def hi_parts(b, m):
                q = m % 2
                pool.wait_ge(S["parts_T_done"], times((b - 1) * 8 + 2 * m + 2))
                if m < 2:
                    pool.wait_ge(L[f"k_in{q}"], landed(b + 1))
                    src, dst = k_in[q], k_parts[q][:, :, 0:4:2, :]
                else:
                    pool.wait_ge(S["q_ln_done"], times(b * 2 + q + 1))
                    src, dst = q_ln[q], q_parts[q][:, :, 0:2, :]
                pool.nop().then_inc(S["pool_waited"], 1)
                src = src[:, :].rearrange("p (h d) -> p h d", h=H).unsqueeze(2).broadcast_to([P, H, 2, HD])
                pool.tensor_copy(dst.bitcast(F32R), src).then_inc(S["hi_done"], 1)

            def lo_parts(b, m, u):
                q = m % 2
                pool.wait_ge(S["hi_done"], times(b * 4 + m + 1))
                if m < 2:
                    src, dst, sl, hi = k_in[q], k_parts[q], slice(1, 4, 2), 0
                else:
                    src, dst, sl, hi = q_ln[q], q_parts[q], slice(2, 4), 0
                for at in range(*sl.indices(4)):
                    ins = pool.tensor_tensor(dst[:, :, at, :].bitcast(F32R),
                                             src[:, :].rearrange("p (h d) -> p h d", h=H),
                                             dst[:, :, hi, :], ALU.subtract)
                ins.then_inc(S["lo_done"], 1)

            def rstd2_task(i, s):
                t = tile_of(i, s)
                pool.wait_ge(S["ln2_stats"], times(t + 1))
                pool.tensor_tensor(rstd2[:, :], ve2[:, :], neg_half[:, :], ALU.pow).then_inc(S["rstd2_done"], 1)

            pool.wait_ge(S["lo_done"], times(4))
            def step(i, s):
                def task(b, k, u):
                    hi_parts(b, k // 2)
                    lo_parts(b, k // 2, u)
                    if k in (2, 4):
                        rstd1_task(b, k // 2 - 1)
                if s % 2 == 0:
                    prep0(pool, i, s, task)
                if last_of_tile(s, 5):
                    lag_task(pool, i, s, 5, rstd2_task)

            turns(pool, step, DEPTH)

            def w_lo(e, slot, m):
                pool.wait_ge(S["w_hi_done"], times(e * 3 + m + 1))
                part = wts[:, slot, m, :]
                if m < 2:
                    hi, lo, src = part[:, 0:MAT // 2], part[:, MAT // 2:MAT], raw[m][:, :]
                else:
                    both = part.rearrange("p (c a n) -> p c a n", c=NF, a=2)
                    hi, lo = both[:, :, 0, :], both[:, :, 1, :]
                    src = raw[m][:, :].rearrange("p (c n) -> p c n", c=NF)
                pool.tensor_tensor(lo, src, hi.bitcast(F32), ALU.subtract)\
                    .then_inc(S["w3_lo_done" if m == 1 else "w_lo_done"], 1)

            for m in range(3):
                w_lo(0, 0, m)

            pool.wait_ge(S["first_gates_done"], times(1))
            pool.tensor_tensor(gates_2nd[:, :], gates[:, 0:N_TILE], ex[:, :], ALU.mult).then_inc(S["gate_link"], 1)
            pool.tensor_tensor(gate_of[:, 0, :, :], choice[:, 0, :, :],
                               gates[:, 0:N_TILE].unsqueeze(2).broadcast_to([P, N_TILE, E]), ALU.mult)\
                .then_inc(S["gate_link"], 1)
            pool.wait_ge(S["gate_link"], times(1))
            pool.tensor_tensor(gate_of[:, 1, :, :], choice[:, 1, :, :],
                               gates_2nd[:, :].unsqueeze(2).broadcast_to([P, N_TILE, E]), ALU.mult)\
                .then_inc(S["gate_link"], 1)
            pool.wait_ge(S["gate_link"], times(3))
            pool.tensor_tensor(gate_of[:, 2, :, :], gate_of[:, 0, :, :], gate_of[:, 1, :, :], ALU.add)\
                .then_inc(S["gates_done"], 1)

            pool.wait_ge(S["til_hot_done"], times(1))
            for k in range(2):
                at = slice(N_TILE * k, N_TILE * k + N_TILE)
                pool.tensor_tensor(slot_vals[:, at, :], til_hot[:, at, :],
                                   token_id[:, :].unsqueeze(2).broadcast_to([P, N_TILE, SLOT_COLS]), ALU.mult)\
                    .then_inc(S["slot_vals_done"], 1)
            pool.wait_ge(S["slots_read"], times(1))
            for n in range(2):
                pool.wait_ge(L[f"xn_out{n}"], landed(N_TILE // 2))
                pool.wait_ge(L[f"x2_out{n}"], landed(N_TILE // 2))
            pool.wait_ge(L["zero_out"], landed(2))
            pool.wait_ge(L["gates_out"], landed(1))

            def gather(t, n):
                pool.tensor_copy(gather_row[n][:, :], slot_tok[:, bass.ds(t, 1)]).then_inc(S["rows_read"], 1)
                pool.wait_ge(S["rows_read"], times(t + 1))
                pool.wait_ge(S["xT_lo_done"], times(t - 2))
                pool.nop().then_inc(S["pool_waited"], 1)
                pool.indirect_dma_start(xg[n][:, :], None, xn_rows, bass.IndirectOffsetOnAxis(gather_row[n][:, :], 0),
                                        bounds_check=N_TOK + PAD_ROWS - 1).then_inc(L[f"xg{n}"], 16)

            def add(t, n):
                pool.wait_ge(S["y_done"], times(t + 1))
                pool.nop().then_inc(S["adds_landed"], 1)
                pool.tensor_copy(add_row[n][:, :], slot_tok[:, bass.ds(t, 1)]).then_inc(S["pool_link"], 1)
                pool.wait_ge(S["pool_link"], times(t + 19))
                pool.nop().then_inc(S["pool_waited"], 1)
                pool.indirect_dma_start(out, bass.IndirectOffsetOnAxis(add_row[n][:, :], 0), y_out[n][:, :], None,
                                        bounds_check=N_TOK + PAD_ROWS - 1, compute_op=ALU.add)\
                    .then_inc(L["added"], 16)

            def convert(t, m):
                is_first = pool.value_load(tile_tab[0:1, 2, bass.ds(t, 1)], min_val=0, max_val=1)
                with pool.If(is_first > 0):
                    expert = pool.value_load(tile_tab[0:1, 0, bass.ds(t, 1)], min_val=0, max_val=E - 2)
                    to = pool.value_load(tile_tab[0:1, 3, bass.ds(t, 1)], min_val=0, max_val=1)
                    w_lo(expert + 1, to, m)

            for n in range(UNROLL):
                gather(n, n)
            pool.wait_ge(S["tables_done"], times(1))
            convert(0, 0)
            gather(UNROLL, 0)
            convert(0, 2)
            with pool.Fori(0, N_SLOT_TILE // UNROLL) as i:
                for n in range(UNROLL):
                    t = i * UNROLL + n
                    if n < UNROLL - 1:
                        convert(t + 1, 0)
                        with pool.If(i < N_SLOT_TILE // UNROLL - 1):
                            gather(within(t + UNROLL + 1, UNROLL + 1, N_SLOT_TILE - 1), n + 1)
                        convert(t + 1, 2)
                    else:
                        with pool.If(i < N_SLOT_TILE // UNROLL - 1):
                            convert(within(t + 1, UNROLL, N_SLOT_TILE - 1), 0)
                        with pool.If(i < N_SLOT_TILE // UNROLL - 2):
                            gather(within(t + UNROLL + 1, 2 * UNROLL, N_SLOT_TILE - 1), 0)
                        with pool.If(i < N_SLOT_TILE // UNROLL - 1):
                            convert(within(t + 1, UNROLL, N_SLOT_TILE - 1), 2)
                    pool.wait_ge(L["added"], i * (UNROLL * 16) + 16 * n)
                    add(t, n)

        @block.scalar
        def _(act):
            start(act, ACT_SEMS)

            def hi_parts(b, m):
                q = m % 2
                act.wait_ge(S["parts_T_done"], times((b - 1) * 8 + 2 * m + 2))
                if m < 2:
                    act.wait_ge(L[f"k_in{q}"], landed(b + 1))
                    src, dst = k_in[q], k_parts[q][:, :, 0:4:2, :]
                else:
                    act.wait_ge(S["q_ln_done"], times(b * 2 + q + 1))
                    src, dst = q_ln[q], q_parts[q][:, :, 0:2, :]
                src = src[:, :].rearrange("p (h d) -> p h d", h=H).unsqueeze(2).broadcast_to([P, H, 2, HD])
                act.activation(dst.bitcast(F32R), src, ACT.Copy).then_inc(S["hi_done"], 1)

            def copy_parts_T(b, k, u, bank=ps_m):
                m, q = k // 2 - 1, (k // 2 - 1) % 2
                act.wait_ge(S["parts_T_done"], times(b * 8 + k))
                dst = (kT if m < 2 else qT)[u]
                act.activation(dst[:, 4:8, P * q:P * q + P], bank.rearrange("p (r t) -> p r t", r=4),
                               ACT.Copy).then_inc(S["partsT1_copied"], 1)

            def exps(i, s):
                g, w = s % 2, (s // 4) % 2
                n = i * SPT + s
                act.wait_ge(S["max_done"], times(n + 1))
                if s % 4 == 0:
                    act.wait_ge(S["rsum_done"], times(tile_of(i, s) - 1))
                for par in range(2):
                    for r in range(2):
                        h = 2 * (2 * (s % 4) + r) + par
                        ins = act.activation(
                            probs[g][:, r, :, par, :],
                            ps_s[:, g, par, SPAN * r:SPAN * r + SPAN].rearrange("p (j c) -> p j c", j=3),
                            ACT.Exp, bias=neg_max[g][:, 2 * par + r:2 * par + r + 1],
                            accum_out=sums[w][:, h:h + 1])
                ins.then_inc(S["exp_done"], 1)

            def copy_ptA(i, s):
                g, n = s % 2, i * SPT + s
                act.wait_ge(S["ptrans_done"], times(n + 1))
                act.wait_ge(S["pv_done"], times(n - 1))
                act.activation(probs_T[g][:, 0:4, :], ps_pt[:, 0, :].rearrange("p (j q) -> p j q", j=4),
                               ACT.Copy).then_inc(S["pt0_copied"], 1)

            def copy_y(i, s):
                t = tile_of(i, s)
                act.wait_ge(S["pv_done"], times(i * SPT + s + 1))
                act.wait_ge(S["y_norm_done"], times(t))
                act.activation(y_raw[:, :, :], ps_y[:, :, :], ACT.Copy).then_inc(S["y_raw_done"], 1)

            hi_parts(0, 0)
            hi_parts(0, 1)
            copy_parts_T(0, 2, 0, ps[:, 1, :])
            hi_parts(0, 2)
            copy_parts_T(0, 4, 0, ps[:, 3, :])
            hi_parts(0, 3)
            copy_parts_T(0, 6, 0, ps[:, 1, :])
            copy_parts_T(0, 8, 0, ps[:, 3, :])

            def step(i, s):
                if s % 2 == 1:
                    prep(act, i, s, lambda b, k, u: copy_parts_T(b, k - 1, u), late=1)
                lag_task(act, i, s, 2, copy_ptA)
                if i is not None:
                    exps(i, s)
                if last_of_tile(s, 3):
                    lag_task(act, i, s, 3, copy_y)
            turns(act, step, DEPTH)

            def w_hi(e, slot, m):
                act.wait_ge(L[f"raw{m}"], landed(e + 1))
                part = wts[:, slot, m, :]
                if m < 2:
                    act.copy(part[:, 0:MAT // 2], raw[m][:, :]).then_inc(S["w_hi_done"], 1)
                else:
                    act.copy(part.rearrange("p (c a n) -> p c a n", c=NF, a=2)[:, :, 0, :],
                             raw[m][:, :].rearrange("p (c n) -> p c n", c=NF)).then_inc(S["w_hi_done"], 1)

            for m in range(3):
                w_hi(0, 0, m)
            act.wait_ge(S["diff_done"], times(1))
            act.activation(ex[:, :], diff[:, :], ACT.Exp).then_inc(S["ex_done"], 1)

            def x_hi(t, n):
                act.wait_ge(S["x_turned"], times(t + 1))
                act.wait_ge(S["h3_done"], times((t - 2) * 2))
                act.activation(xT[n][:, 0, :, :], ps_xT[:, 0:D].rearrange("p (c t) -> p c t", c=NC),
                               ACT.Copy).then_inc(S["xT_hi_done"], 1)

            def y_low(t):
                act.wait_ge(S["out_done"], times(t + 1))
                act.wait_ge(S["y_done"], times(t))
                act.activation(y_small[:, :], ps_out[:, D:2 * D], ACT.Copy, scale=slot_gate[:, bass.ds(t, 1)])\
                    .then_inc(S["y_small_done"], 1)

            def convert(t, m):
                is_first = act.value_load(tile_tab[0:1, 2, bass.ds(t, 1)], min_val=0, max_val=1)
                with act.If(is_first > 0):
                    expert = act.value_load(tile_tab[0:1, 0, bass.ds(t, 1)], min_val=0, max_val=E - 2)
                    to = act.value_load(tile_tab[0:1, 3, bass.ds(t, 1)], min_val=0, max_val=1)
                    if m < 2:
                        act.wait_ge(S["h3_done"], times(t * 2))
                    else:
                        act.wait_ge(S["out_done"], times(t))
                    w_hi(expert + 1, to, m)

            act.wait_ge(S["tables_done"], times(1))
            x_hi(0, 0)
            with act.Fori(0, N_SLOT_TILE // UNROLL) as i:
                for n in range(UNROLL):
                    t = i * UNROLL + n
                    for a in range(2):
                        act.wait_ge(S["h1_done"], times(t * 2 + a + 1))
                        act.wait_ge(S["hidden_done"], times((t - 1) * 2 + a + 1))
                        act.activation(gated[:, HALF * a:HALF * a + HALF], ps_h[:, 0, a, :], ACT.Silu)\
                            .then_inc(S["silu_done"], 1)
                        if a == 0:
                            convert(t, 0)
                    if n < UNROLL - 1:
                        x_hi(t + 1, n + 1)
                    else:
                        with act.If(i < N_SLOT_TILE // UNROLL - 1):
                            x_hi(t + 1, 0)
                    convert(t, 1)
                    if n == 0:
                        with act.If(i > 0):
                            y_low(within(t - 1, 2, N_SLOT_TILE - 2))
                    else:
                        y_low(t - 1)
                    for a in range(2):
                        act.wait_ge(S["h_turned"], times(t * 2 + a + 1))
                        act.wait_ge(S["out_done"], times(t - 2))
                        act.activation(hT[n][:, 0, 4 * a:4 * a + 4, :], ps_hT[:, a, :].rearrange("p (c t) -> p c t", c=4),
                                       ACT.Copy).then_inc(S["hT_hi_done"], 1)
                    convert(t, 2)
            y_low(N_SLOT_TILE - 1)

        @block.vector
        def _(dve):
            start(dve, DVE_SEMS)
            links = {"ln1": 0, "ln2": 0}

            def stats1(b, q):
                dve.wait_ge(L[f"x_in{q}"], landed(b + 1))
                dve.wait_ge(S["q_ln_done"], times(b * 2 + q))
                n = (b * 2 + q) * 2
                dve.bn_stats(st1[:, :], x_in[q][:, :]).then_inc(S["ln1_link"], 1)
                dve.wait_ge(S["ln1_link"], times(n + 1))
                dve.nop().then_inc(S["dve_waited"], 1)
                dve.bn_aggr(mv1[:, :], st1[:, :]).then_inc(S["ln1_link"], 1)
                dve.wait_ge(S["ln1_link"], times(n + 2))
                dve.tensor_scalar(ve1[:, :], mv1[:, 1:2], EPS, float(HD), ALU.add, ALU.mult)\
                    .then_inc(S["ln1_stats"], 1)

            def normalise(b, q):
                dve.wait_ge(S["rstd1_done"], times(b * 2 + q + 1))
                dve.wait_ge(S["lo_done"], times((b - 1) * 4 + 3 + q))
                dve.tensor_scalar(q_ln[q][:, :], x_in[q][:, :], mv1[:, 0:1], rstd1[:, 0:1],
                                  ALU.subtract, ALU.mult).then_inc(S["q_ln_done"], 1)

            def copy_parts_T(b, k, u, bank=ps_m):
                m, q = k // 2, (k // 2) % 2
                dve.wait_ge(S["parts_T_done"], times(b * 8 + k))
                dst = (kT if m < 2 else qT)[u]
                dve.tensor_copy(dst[:, 0:4, P * q:P * q + P], bank.rearrange("p (r t) -> p r t", r=4))\
                    .then_inc(S["partsT0_copied"], 1)

            def spread_v(b, u):
                dve.wait_ge(L["v_in"], landed((b + 1) * 2))
                dve.wait_ge(S["consts_done"], times(6))
                dve.wait_ge(S["pv_done"], times((b - 1) * 8))
                for par in range(2):
                    lo = WIN * par
                    src = v_in[lo:lo + WIN, :, :].rearrange("p j (r e d) -> p j r e d", e=2, d=HD)
                    dve.tensor_copy(v_bd[u][lo:lo + WIN, :, :, HD * par:HD * par + HD], src[:, :, :, par, :])\
                        .then_inc(S["v_bd_done"], 1)

            def maxes(i, s):
                g, n = s % 2, i * SPT + s
                dve.wait_ge(S["scores_done"], times(n + 1))
                dve.tensor_reduce(neg_max[g][:, :].rearrange("p (e r) -> p e r", e=2),
                                  ps_s[:, g, :, 0:2 * SPAN].rearrange("p e (r c) -> p e r c", r=2),
                                  AX.X, ALU.max, negate=True).then_inc(S["max_done"], 1)

            def probs_turned(i, s):
                dve.wait_ge(S["ptrans_done"], times(i * SPT + s + 1))

            def probs_turned_apart(i, s):
                dve.wait_ge(S["ptrans_done"], times(i * SPT + s + 1))
                dve.nop().then_inc(S["dve_waited"], 1)

            def copy_ptB(i, s):
                g, n = s % 2, i * SPT + s
                dve.wait_ge(S["pv_done"], times(n - 1))
                dve.tensor_copy(probs_T[g][:, 4:6, :], ps_pt[:, 1, 0:2 * P].rearrange("p (j q) -> p j q", j=2))\
                    .then_inc(S["pt1_copied"], 1)

            def invert_sums(i, s):
                t, w = tile_of(i, s), (s // 4) % 2
                dve.wait_ge(S["exp_done"], times(i * SPT + s + 1))
                dve.wait_ge(S["rsum_T_done"], times(t))
                dve.reciprocal(rsum[:, :], sums[w][:, :]).then_inc(S["rsum_done"], 1)

            def copy_rsum_T(i, s):
                t = tile_of(i, s)
                dve.wait_ge(S["rsum_T_done"], times(t + 1))
                dve.wait_ge(S["rbc_done"], times(t))
                dve.tensor_copy(rsum_T[:, :], ps_tail[0:H, 0:P]).then_inc(S["rsum_T_copied"], 1)

            def copy_xn_T(i, s):
                t = tile_of(i, s)
                dve.wait_ge(S["xn_T_ps_done"], times(t + 1))
                dve.wait_ge(S["logits_done"], times(t))
                dve.tensor_copy(xn_T[:, :, :], ps_tail.rearrange("p (c t) -> p c t", c=NC))\
                    .then_inc(S["xn_T_copied"], 1)

            def norm_y(i, s):
                t = tile_of(i, s)
                dve.wait_ge(S["rbc_done"], times(t + 1))
                dve.wait_ge(S["y_raw_done"], times(t + 1))
                dve.wait_ge(S["proj_done"], times(t))
                dve.tensor_tensor(y_norm[:, :, :], ps_tail.rearrange("p (c t) -> p c t", c=NC),
                                  y_raw[:, :, :], ALU.mult).then_inc(S["y_norm_done"], 1)

            def residual(i, s):
                t, q = tile_of(i, s), (s // 4) % 2
                dve.wait_ge(S["proj_done"], times(t + 1))
                dve.wait_ge(L[f"x_res{q}"], (i * 2 + s // 8 + 1) * 16 + BASE)
                dve.wait_ge(L[f"x2_out{q}"], (i * 2 + s // 8) * 16 + BASE)
                dve.wait_ge(S["xn_done"], times(t))
                dve.tensor_tensor(x2[q][:, :], ps_tail, x_res[q][:, :], ALU.add).then_inc(S["x2_done"], 1)

            def stats2(i, s):
                t, q = tile_of(i, s), (s // 4) % 2
                dve.wait_ge(S["x2_done"], times(t + 1))
                dve.bn_stats(st2[:, :], x2[q][:, :]).then_inc(S["ln2_link"], 1)
                dve.wait_ge(S["ln2_link"], times(t * 2 + 1))
                dve.nop().then_inc(S["dve_waited"], 1)
                dve.bn_aggr(mv2[:, :], st2[:, :]).then_inc(S["ln2_link"], 1)
                dve.wait_ge(S["ln2_link"], times(t * 2 + 2))
                dve.tensor_scalar(ve2[:, :], mv2[:, 1:2], EPS, None, ALU.add).then_inc(S["ln2_stats"], 1)

            def norm_x2(i, s):
                t, q = tile_of(i, s), (s // 4) % 2
                dve.wait_ge(S["rstd2_done"], times(t + 1))
                dve.wait_ge(L[f"xn_out{q}"], (i * 2 + s // 8) * 16 + BASE)
                dve.wait_ge(S["xn_T_ps_done"], times(t - 1))
                dve.tensor_scalar(xn[q][:, :], x2[q][:, :], mv2[:, 0:1], rstd2[:, 0:1],
                                  ALU.subtract, ALU.mult).then_inc(S["xn_done"], 1)

            def copy_logits(i, s):
                t = tile_of(i, s)
                dve.wait_ge(S["logits_done"], times(t + 1))
                dve.tensor_copy(logits[:, t, :], ps_tail[:, P:P + E]).then_inc(S["logits_copied"], 1)

            def first_lo_parts(m):
                q = m % 2
                dve.wait_ge(S["hi_done"], times(m + 1))
                src, dst, at = (k_in[q], k_parts[q], (1, 3)) if m < 2 else (q_ln[q], q_parts[q], (2, 3))
                for a in at:
                    ins = dve.tensor_tensor(dst[:, :, a, :].bitcast(F32R), src[:, :].rearrange("p (h d) -> p h d", h=H),
                                            dst[:, :, 0, :], ALU.subtract)
                ins.then_inc(S["lo_done"], 1)

            stats1(0, 0)
            first_lo_parts(0)
            normalise(0, 0)
            stats1(0, 1)
            first_lo_parts(1)
            normalise(0, 1)
            copy_parts_T(0, 1, 0, ps[:, 0, :])
            first_lo_parts(2)
            copy_parts_T(0, 3, 0, ps[:, 2, :])
            first_lo_parts(3)
            copy_parts_T(0, 5, 0, ps[:, 0, :])
            copy_parts_T(0, 7, 0, ps[:, 2, :])
            spread_v(0, 0)
            dve.wait_ge(S["w_T_ps_done"], times(1))
            dve.tensor_copy(w_T[:, :, :].rearrange("p c n -> p (c n)"), ps_m[:, :]).then_inc(S["w_T_copied"], 1)
            dve.wait_ge(S["consts_done"], times(ATTENTION_CONSTS))
            dve.tensor_copy(ones_r[:, :], ones_row[:, :]).then_inc(S["bias_split"], 1)
            dve.wait_ge(L["weights_in"], landed(3))
            dve.tensor_copy(bias_parts[:, 0, :], bias_row[:, :]).then_inc(S["bias_split"], 1)
            dve.wait_ge(S["bias_split"], times(2))
            dve.tensor_tensor(bias_parts[:, 1, :], bias_row[:, :], bias_parts[:, 0, :].bitcast(F32), ALU.subtract)\
                .then_inc(S["bias_split"], 1)

            def step(i, s):
                if s % 2 == 0:
                    prep(dve, i, s, lambda b, k, u: copy_parts_T(b, k - 1, u))
                if i is not None:
                    maxes(i, s)
                lag_task(dve, i, s, 2, probs_turned_apart if s <= 6 else probs_turned)
                for lag, task in ((2, copy_rsum_T), (10, copy_logits), (7, copy_xn_T), (4, norm_y), (5, residual)):
                    if last_of_tile(s, lag):
                        lag_task(dve, i, s, lag, task)
                lag_task(dve, i, s, 2, copy_ptB)
                if last_of_tile(s, 1):
                    lag_task(dve, i, s, 1, invert_sums)
                if s % 8 in (2, 4):
                    prep0(dve, i, s, lambda b, k, u: stats1(b, k // 2 - 1))
                if last_of_tile(s, 5):
                    lag_task(dve, i, s, 5, stats2)
                if last_of_tile(s, 6):
                    lag_task(dve, i, s, 6, norm_x2)
                if s % 8 == 7:
                    prep0(dve, i, s, lambda b, k, u: spread_v(b, u))
                if s % 8 in (3, 5):
                    prep0(dve, i, s, lambda b, k, u: normalise(b, k // 2 - 1))


            turns(dve, step, DEPTH)

            links["route"] = 0

            def link(ins):
                links["route"] += 1
                ins.then_inc(S["route_link"], 1)
                dve.wait_ge(S["route_link"], times(links["route"]))

            def over(ap, *shape):
                return ap.broadcast_to([P, *shape])

            dve.wait_ge(S["logits_copied"], times(N_TILE))
            dve.wait_ge(S["consts_done"], times(ATTENTION_CONSTS + 1))
            for k in range(2):
                lg = logits if k == 0 else rest
                if k == 1:
                    link(dve.scalar_tensor_tensor(out=rest[:, :, :], in0=choice[:, 0, :, :], scalar=-3e38,
                                                  in1=logits[:, :, :], op0=ALU.mult, op1=ALU.add))
                link(dve.tensor_reduce(best[:, k, :], lg[:, :, :], AX.X, ALU.max))
                link(dve.tensor_tensor(same[:, :, :], lg[:, :, :], over(best[:, k, :].unsqueeze(2), N_TILE, E),
                                       ALU.is_equal))
                link(dve.scalar_tensor_tensor(out=cand[:, :, :], in0=same[:, :, :], scalar=-float(E),
                                              in1=over(iota_e[:, :].unsqueeze(1), N_TILE, E),
                                              op0=ALU.mult, op1=ALU.add))
                link(dve.tensor_reduce(first[:, :], cand[:, :, :], AX.X, ALU.min))
                link(dve.tensor_tensor(choice[:, k, :, :], cand[:, :, :], over(first[:, :].unsqueeze(2), N_TILE, E),
                                       ALU.is_equal))
            dve.tensor_tensor(diff[:, :], best[:, 1, :], best[:, 0, :], ALU.subtract).then_inc(S["diff_done"], 1)
            dve.tensor_tensor(chosen[:, :, :], choice[:, 0, :, :], choice[:, 1, :, :], ALU.add)\
                .then_inc(S["chosen_done"], 1)
            dve.wait_ge(S["ex_done"], times(1))
            link(dve.tensor_scalar(gates[:, N_TILE:], ex[:, :], 1.0, None, ALU.add))
            dve.reciprocal(gates[:, 0:N_TILE], gates[:, N_TILE:]).then_inc(S["first_gates_done"], 1)
            dve.memset(upto[:, :, 0:PAD_T, :], 0.0).then_inc(S["route_link"], 1)
            dve.memset(cum[:, :, 0:PAD_T], 0.0).then_inc(S["route_link"], 1)
            links["route"] += 2
            dve.wait_ge(S["rank_done"], times(1))
            flat = "p t e -> p (t e)"
            link(dve.tensor_copy(upto[:, 0, PAD_T:, :].rearrange(flat), ps[:, 1, 0:P]))
            for n, sh in enumerate((1, 2, 4, 8)):
                link(dve.tensor_tensor(upto[:, n + 1, PAD_T:, :], upto[:, n, PAD_T:, :],
                                       upto[:, n, PAD_T - sh:PAD_T + N_TILE - sh, :], ALU.add))
            link(dve.tensor_tensor(earlier[:, :, :].rearrange(flat), ps[:, 0, 0:P],
                                   upto[:, 4, PAD_T:, :].rearrange(flat), ALU.add))
            link(dve.tensor_scalar(tiles_i[:, :], upto[:, 4, PAD_T + N_TILE - 1, :], float(P - 1), None, ALU.add))
            link(dve.tensor_scalar(tiles_s[:, :], tiles_i[:, :], 7, None, ALU.arith_shift_right))
            link(dve.tensor_scalar(cum[:, 0, PAD_T:], tiles_s[:, :], 1.0, None, ALU.max))
            for n, sh in enumerate((1, 2, 4)):
                link(dve.tensor_tensor(cum[:, n + 1, PAD_T:], cum[:, n, PAD_T:], cum[:, n, PAD_T - sh:PAD_T + E - sh],
                                       ALU.add))
            link(dve.tensor_tensor(tile0[:, :], cum[:, 3, PAD_T:], cum[:, 0, PAD_T:], ALU.subtract))
            link(dve.scalar_tensor_tensor(out=place_e[:, :, :], in0=over(tile0[:, :].unsqueeze(1), N_TILE, E),
                                          scalar=float(P), in1=earlier[:, :, :], op0=ALU.mult, op1=ALU.add))
            for k in range(2):
                link(dve.tensor_tensor(picked[:, k, :, :], choice[:, k, :, :], place_e[:, :, :], ALU.mult))
            link(dve.tensor_reduce(pos[:, :], picked[:, :, :, :].rearrange("p k t e -> p (k t) e"), AX.X, ALU.add))
            link(dve.tensor_copy(pos_i[:, :], pos[:, :]))
            link(dve.tensor_scalar(til_i[:, :], pos_i[:, :], 7, None, ALU.arith_shift_right))
            link(dve.tensor_copy(til_f[:, :], til_i[:, :]))
            for n in range(2):
                dve.wait_ge(L[f"x2_out{n}"], landed(N_TILE // 2))
                dve.wait_ge(L[f"xn_out{n}"], landed(N_TILE // 2))
            dve.tensor_tensor(til_hot[:, :, :], over(iota_tile[:, :].unsqueeze(1), N_CHOICE, SLOT_COLS),
                              over(til_f[:, :].unsqueeze(2), N_CHOICE, SLOT_COLS), ALU.is_equal)\
                .then_inc(S["til_hot_done"], 1)
            link(dve.tensor_scalar(row_i[:, :], pos_i[:, :], P - 1, None, ALU.bitwise_and))
            link(dve.tensor_copy(row_f[:, :], row_i[:, :]))
            for a in range(0, N_CHOICE, HOT_CHUNK):
                dve.tensor_tensor(row_hot[:, a:a + HOT_CHUNK, :], over(iota_slot[:, :].unsqueeze(1), HOT_CHUNK, P),
                                  over(row_f[:, a:a + HOT_CHUNK].unsqueeze(2), HOT_CHUNK, P), ALU.is_equal)\
                    .then_inc(S["hots_done"], 1)
            dve.wait_ge(S["slots_done"], times(1))
            link(dve.scalar_tensor_tensor(out=pad_row[:, :], in0=ps[:, 2, 0:SLOT_COLS], scalar=0.0,
                                          in1=over(part_id[:, :], SLOT_COLS), op0=ALU.is_equal, op1=ALU.mult))
            link(dve.scalar_tensor_tensor(out=slot_tok[:, :], in0=ps[:, 2, 0:SLOT_COLS], scalar=1.0,
                                          in1=pad_row[:, :], op0=ALU.subtract, op1=ALU.add))
            dve.nop().then_inc(S["slots_read"], 1)
            link(dve.tensor_tensor(ge_tile[:, :, :], over(iota_tile[:, :].unsqueeze(2), SLOT_COLS, E - 1),
                                   over(tile0[:, 1:].unsqueeze(1), SLOT_COLS, E - 1), ALU.is_ge))
            link(dve.memset(tile_e[:, 0:1], -1.0))
            link(dve.tensor_reduce(tile_e[:, 1:], ge_tile[:, :, :], AX.X, ALU.add))
            link(dve.tensor_copy(tab_f[:, 0, :], tile_e[:, 1:]))
            link(dve.tensor_tensor(tile_new[:, :], tile_e[:, 1:], tile_e[:, 0:SLOT_COLS], ALU.subtract))
            link(dve.scalar_tensor_tensor(out=tab_f[:, 2, :], in0=tile_e[:, 1:], scalar=float(E - 1),
                                          in1=tile_new[:, :], op0=ALU.is_lt, op1=ALU.mult))
            link(dve.tensor_copy(tile_tab[:, 0, :], tab_f[:, 0, :]))
            link(dve.tensor_copy(tile_tab[:, 2, :], tab_f[:, 2, :]))
            link(dve.tensor_scalar(tile_tab[:, 1, :], tile_tab[:, 0, :], 1, None, ALU.bitwise_and))
            link(dve.tensor_scalar(tile_tab[:, 3, :], tile_tab[:, 1, :], 1, None, ALU.bitwise_xor))
            link(dve.tensor_tensor(tab_f[:, 1, :], over(cum[:, 3, PAD_T + E - 1:], SLOT_COLS), iota_tile[:, :],
                                   ALU.is_gt))
            link(dve.tensor_copy(tab_f[:, 3, :], tile_tab[:, 1, :]))
            for k in (3, 0):
                link(dve.scalar_tensor_tensor(out=tab_f[:, 1, :], in0=tab_f[:, k, :], scalar=2.0 if k == 3 else 4.0,
                                              in1=tab_f[:, 1, :], op0=ALU.mult, op1=ALU.add))
            link(dve.tensor_copy(tile_tab[:, 4, :], tab_f[:, 1, :]))
            dve.nop().then_inc(S["tables_done"], 1)

            def x_lo(t, n):
                expert = dve.value_load(tile_tab[0:1, 0, bass.ds(t, 1)], min_val=0, max_val=E - 1)
                dve.wait_ge(S["xT_hi_done"], times(t + 1))
                dve.wait_ge(S["h3_done"], times((t - 2) * 2))
                dve.tensor_copy(slot_gate[:, bass.ds(t, 1)], xg[n][:, bass.ds(expert + D, 1)])\
                    .then_inc(S["gate_taken"], 1)
                dve.tensor_tensor(xT[n][:, 1, :, :], ps_xT[:, 0:D].rearrange("p (c t) -> p c t", c=NC),
                                  xT[n][:, 0, :, :].bitcast(F32), ALU.subtract).then_inc(S["xT_lo_done"], 1)

            def y_final(t, n):
                dve.wait_ge(S["y_small_done"], times(t + 1))
                dve.wait_ge(S["adds_landed"], times(t - 1))
                dve.scalar_tensor_tensor(out=y_out[n][:, :], in0=ps_out[:, 0:D], scalar=slot_gate[:, bass.ds(t, 1)],
                                         in1=y_small[:, :], op0=ALU.mult, op1=ALU.add).then_inc(S["y_done"], 1)

            def convert(t):
                is_first = dve.value_load(tile_tab[0:1, 2, bass.ds(t, 1)], min_val=0, max_val=1)
                with dve.If(is_first > 0):
                    expert = dve.value_load(tile_tab[0:1, 0, bass.ds(t, 1)], min_val=0, max_val=E - 2)
                    to = dve.value_load(tile_tab[0:1, 3, bass.ds(t, 1)], min_val=0, max_val=1)
                    dve.wait_ge(S["w_hi_done"], times(expert * 3 + 5))
                    dve.tensor_tensor(wts[:, to, 1, MAT // 2:MAT], raw[1][:, :],
                                      wts[:, to, 1, 0:MAT // 2].bitcast(F32), ALU.subtract)\
                        .then_inc(S["w3_lo_done"], 1)

            dve.wait_ge(S["w3_lo_done"], times(1))
            x_lo(0, 0)
            with dve.Fori(0, N_SLOT_TILE // UNROLL) as i:
                for n in range(UNROLL):
                    t = i * UNROLL + n
                    for a in range(2):
                        dve.wait_ge(S["h3_done"], times(t * 2 + a + 1))
                        dve.wait_ge(S["silu_done"], times(t * 2 + a + 1))
                        dve.wait_ge(S["h_turned"], times((t - 1) * 2 + a + 1))
                        dve.tensor_tensor(hidden[:, HALF * a:HALF * a + HALF], ps_h[:, 1, a, :],
                                          gated[:, HALF * a:HALF * a + HALF], ALU.mult).then_inc(S["hidden_done"], 1)
                    if n < UNROLL - 1:
                        x_lo(t + 1, n + 1)
                    else:
                        with dve.If(i < N_SLOT_TILE // UNROLL - 1):
                            x_lo(t + 1, 0)
                    if n == 0:
                        with dve.If(i > 0):
                            y_final(within(t - 1, 2, N_SLOT_TILE - 2), UNROLL - 1)
                    else:
                        y_final(t - 1, n - 1)
                    for a in range(2):
                        dve.wait_ge(S["hT_hi_done"], times(t * 2 + a + 1))
                        dve.wait_ge(S["out_done"], times(t - 2))
                        dve.tensor_tensor(hT[n][:, 1, 4 * a:4 * a + 4, :],
                                          ps_hT[:, a, :].rearrange("p (c t) -> p c t", c=4),
                                          hT[n][:, 0, 4 * a:4 * a + 4, :].bitcast(F32), ALU.subtract)\
                            .then_inc(S["hT_lo_done"], 1)
                    convert(t)
            y_final(N_SLOT_TILE - 1, UNROLL - 1)

        @block.tensor
        def _(pe):
            start(pe, PE_SEMS)

            def parts_round(b, k, u, misc_free, bank=ps_m):
                m, half = (k - 1) // 2, (k - 1) % 2
                q = m % 2
                pe.wait_ge(S["lo_done"], times(b * 4 + m + 1))
                misc_free()
                src = (k_parts if m < 2 else q_parts)[q]
                for r in range(4):
                    pair = 4 * half + r
                    ins = pe.transpose(bank[:, P * r:P * r + P],
                                       src[:, 2 * pair:2 * pair + 2, :, :].rearrange("p h a d -> p (h a d)"),
                                       ident[:, :])
                ins.then_inc(S["parts_T_done"], 1)

            def parts_copied(b, k):
                pe.wait_ge(S["partsT0_copied"], times(b * 4 + (k + 1) // 2))
                pe.wait_ge(S["partsT1_copied"], times(b * 4 + k // 2))

            def scores(i, s):
                n, g, u, q = i * SPT + s, s % 2, s // 8, (s // 4) % 2
                b = i * 2 + u
                pe.wait_ge(S["exp_done"], times(n - 1))
                if s % 8 == 0:
                    parts_copied(b, 6)
                if s % 8 == 4:
                    parts_copied(b, 8)
                for par in range(2):
                    pe.matmul(ps_s[:, g, par, 0:2 * SPAN], ident_bf[:, :],
                              mask[:, q, :].unsqueeze(1).broadcast_to([P, 2, SPAN]), start=True, stop=False)
                    for r in range(2):
                        pair = 2 * (s % 4) + r
                        rows = slice(64 * par, 64 * par + 64)
                        ins = pe.matmul(ps_s[:, g, par, SPAN * r:SPAN * r + SPAN],
                                        qT[u][rows, pair, P * q:P * q + P],
                                        kT[u][rows, pair, WIN * q:WIN * q + SPAN], start=False, stop=(r == 1))
                ins.then_inc(S["scores_done"], 1)

            def prob_transposes(i, s):
                n, g = i * SPT + s, s % 2
                pe.wait_ge(S["exp_done"], times(n + 1))
                pe.wait_ge(S["pt0_copied"], times(n))
                pe.wait_ge(S["pt1_copied"], times(n))
                for r in range(2):
                    for j in range(3):
                        half, at = divmod(3 * r + j, 4)
                        ins = pe.transpose(ps_pt[:, half, P * at:P * at + P],
                                           probs[g][:, r, j, :, :].rearrange("p e c -> p (e c)"), ident[:, :])
                ins.then_inc(S["ptrans_done"], 1)

            def values(i, s):
                n, g, u, q = i * SPT + s, s % 2, s // 8, (s // 4) % 2
                pe.wait_ge(S["pt0_copied"], times(n + 1))
                pe.wait_ge(S["pt1_copied"], times(n + 1))
                if s % 4 == 0:
                    pe.wait_ge(S["y_raw_done"], times(tile_of(i, s)))
                if s % 8 == 0:
                    pe.wait_ge(S["v_bd_done"], times((i * 2 + u) * 2 + 2))
                for r in range(2):
                    pair = 2 * (s % 4) + r
                    c, row = pair // 4, 32 * (pair % 4)
                    for j in range(3):
                        ins = pe.matmul(ps_y[row:row + 32, c, :], v_bd[u][:, q + j, pair, :],
                                        probs_T[g][:, 3 * r + j, :], start=(j == 0), stop=(j == 2))
                ins.then_inc(S["pv_done"], 1)

            def tail_sums(i, s):
                t = tile_of(i, s)
                pe.wait_ge(S["rsum_done"], times(t + 1))
                pe.transpose(ps_tail[0:H, 0:P], rsum[:, :], ident[:, :]).then_inc(S["rsum_T_done"], 1)

            def tail_broadcast(i, s):
                t = tile_of(i, s)
                pe.wait_ge(S["rsum_T_copied"], times(t + 1))
                pe.wait_ge(S["consts_done"], times(ATTENTION_CONSTS))
                for c in range(NC):
                    ins = pe.matmul(ps_tail[:, P * c:P * c + P], head_sel[:, c, :], rsum_T[:, :],
                                    start=True, stop=True)
                ins.then_inc(S["rbc_done"], 1)

            def tail_project(i, s):
                t = tile_of(i, s)
                pe.wait_ge(S["y_norm_done"], times(t + 1))
                pe.wait_ge(S["bias_split"], times(3))
                for part in range(2):
                    pe.matmul(ps_tail, ones_r[:, :], bias_parts[:, part, :], start=(part == 0), stop=False)
                for c in range(NC):
                    ins = pe.matmul(ps_tail, y_norm[:, c, :], w_T[:, c, :], start=False, stop=(c == NC - 1))
                ins.then_inc(S["proj_done"], 1)

            def tail_turn(i, s):
                t, q = tile_of(i, s), (s // 4) % 2
                pe.wait_ge(S["xn_done"], times(t + 1))
                for c in range(NC):
                    ins = pe.transpose(ps_tail[:, P * c:P * c + P], xn[q][:, P * c:P * c + P], ident[:, :])
                ins.then_inc(S["xn_T_ps_done"], 1)

            def tail_logits(i, s):
                t = tile_of(i, s)
                pe.wait_ge(S["xn_T_copied"], times(t + 1))
                for c in range(NC):
                    ins = pe.matmul(ps_tail[:, P:P + E], xn_T[:, c, :], wg_s[:, c, :], start=(c == 0), stop=(c == NC - 1))
                ins.then_inc(S["logits_done"], 1)

            TAIL = {1: ((10, tail_logits, "logits_copied"), (2, tail_sums, "rsum_T_copied")),
                    2: ((7, tail_turn, "xn_T_copied"),),
                    3: ((4, tail_broadcast, "y_norm_done"),),
                    0: ((5, tail_project, "x2_done"),)}

            def tail_emptied(s):
                for lag, _, copied in TAIL[s % 4]:
                    pe.wait_ge(S[copied], times(min((NIT - 1) * 4 + (s - lag) // 4 + 1, N_TILE)))

            pe.wait_ge(S["consts_done"], times(1))
            for k in range(1, 9):
                parts_round(0, k, 0, lambda: parts_copied(0, k - 4), ps[:, (k - 1) % 4, :])
            pe.wait_ge(L["weights_in"], landed(3))
            for c in range(NC):
                for r in range(NC):
                    ins = pe.transpose(ps_m[:, D * c + P * r:D * c + P * r + P], w_nat[:, r, P * c:P * c + P],
                                       ident[:, :])
            ins.then_inc(S["w_T_ps_done"], 1)
            parts_copied(0, 8)
            pe.wait_ge(S["consts_done"], times(4))

            def step(i, s):
                if i is not None:
                    scores(i, s)
                lag_task(pe, i, s, 2, prob_transposes)
                if i is not None or any(s - lag < SPT for lag, _, _ in TAIL[s % 4]):
                    if i is None:
                        pe.wait_ge(S["pt1_copied"], times(min((NIT - 1) * SPT + s - 2, NIT * SPT)))
                        tail_emptied(s - 1)
                    else:
                        pe.wait_ge(S["pt1_copied"], times(i * SPT + s - 2))
                    for lag, task, _ in TAIL[s % 4]:
                        lag_task(pe, i, s, lag, task)
                lag_task(pe, i, s, 3, values)

                def bank_free(b, k):
                    if s == 1:
                        pe.wait_ge(S["w_T_copied"], times(1))
                    parts_copied(b, k - 1)

                prep(pe, i, s, lambda b, k, u: parts_round(b, k, u, lambda: bank_free(b, k)))

            turns(pe, step, DEPTH)

            pe.wait_ge(S["chosen_done"], times(1))
            flat = chosen[:, :, :].rearrange("p t e -> p (t e)")
            pe.matmul(ps[:, 0, 0:P], before[:, :], flat, start=True, stop=True)
            pe.matmul(ps[:, 1, 0:P], ones[:, :], flat, start=True, stop=True).then_inc(S["rank_done"], 1)
            for a in range(N_CHOICE):
                if a % N_TILE == 0:
                    pe.wait_ge(S["slot_vals_done"], times(a // N_TILE + 1))
                if a % HOT_CHUNK == 0:
                    pe.wait_ge(S["hots_done"], times(a // HOT_CHUNK + 1))
                ins = pe.matmul(ps[:, 2, 0:SLOT_COLS], row_hot[:, a, :], slot_vals[:, a, :],
                                start=(a == 0), stop=(a == N_CHOICE - 1))
            ins.then_inc(S["slots_done"], 1)

            def keep_warm(count):
                for _ in range(count):
                    pe.matmul(ps_hT[:, 0, 0:P], before[:, :], ones[:, :], start=True, stop=True)

            keep_warm(WARM_UP[0])
            pe.wait_ge(S["tables_done"], times(1))

            def turn_x(t, n, landed):
                pe.wait_ge(L[f"xg{n}"], landed * 16)
                pe.wait_ge(S["xT_lo_done"], times(t))
                for c in range(NC):
                    ins = pe.transpose(ps_xT[:, P * c:P * c + P], xg[n][:, P * c:P * c + P], ident[:, :])
                ins.then_inc(S["x_turned"], 1)

            def tile_values(t):
                if not isinstance(t, int):
                    t = bass.ds(t, 1)
                packed = pe.value_load(tile_tab[0:1, 4, t], min_val=0, max_val=4 * E - 1)
                return packed // 4, pe.snap(packed // 2 % 2, min_val=0, max_val=1), packed % 2

            def up(t, n, slot, whole):
                for a in range(2):
                    for m in range(2):
                        pe.wait_ge(S["silu_done" if m == 0 else "hidden_done"], times((t - 1) * 2 + a + 1))
                        w = wts[:, slot, m, :].rearrange("p (a c f) -> p a c f", a=2, c=NC)
                        for c in range(NC):
                            for part, x_part in ((0, 0), (1, 0), (0, 1)):
                                first = c == 0 and part + x_part == 0
                                last = c == NC - 1 and x_part == 1
                                if whole or last:
                                    ins = pe.matmul(ps_h[:, m, a, :], xT[n][:, x_part, c, :],
                                                    w[:, part, c, HALF * a:HALF * a + HALF],
                                                    start=first or not whole, stop=last)
                        ins.then_inc(S["h1_done" if m == 0 else "h3_done"], 1)

            def down(t, n, slot, used):
                pe.wait_ge(S["hT_lo_done"], times(t * 2 + 2))
                pe.wait_ge(S["y_done"], times(t))
                w = wts[:, slot, 2, :].rearrange("p (c a n) -> p c a n", c=NF, a=2)

                def chunks(cs):
                    for c in cs:
                        pe.matmul(ps_out[:, :], hT[n][:, 0, c, :], w[:, c, :, :].rearrange("p a n -> p (a n)"),
                                  start=(c == cs[0]), stop=False)
                        ins = pe.matmul(ps_out[:, 0:D], hT[n][:, 1, c, :], w[:, c, 0, :],
                                        start=False, stop=(c == NF - 1))
                    ins.then_inc(S["out_done"], 1)

                with pe.If(used > 0):
                    chunks(range(NF))
                with pe.Else():
                    chunks(range(NF - 1, NF))

            turn_x(0, 0, 1)
            keep_warm(WARM_UP[1])
            with pe.Fori(0, N_SLOT_TILE // UNROLL) as i:
                for n in range(UNROLL):
                    t = i * UNROLL + n
                    if n == 0:
                        expert, slot, used = tile_values(t)
                    pe.wait_ge(S["xT_lo_done"], times(t + 1))
                    pe.wait_ge(S["w_lo_done"], times(expert * 2 + 2))
                    pe.wait_ge(S["w3_lo_done"], times(expert + 1))
                    with pe.If(used > 0):
                        up(t, n, slot, True)
                    with pe.Else():
                        up(t, n, slot, False)
                    if n < UNROLL - 1:
                        turn_x(t + 1, n + 1, i + 1)
                    else:
                        with pe.If(i < N_SLOT_TILE // UNROLL - 1):
                            turn_x(t + 1, 0, i + 2)
                    if n == 0:
                        with pe.If(i > 0):
                            last_turns = within(t - 1, 2, N_SLOT_TILE - 2)
                            _, slot_before, used_before = tile_values(last_turns)
                            down(last_turns, UNROLL - 1, slot_before, used_before)
                    else:
                        down(t - 1, n - 1, slot_before, used_before)
                    slot_before, used_before = slot, used
                    if n < UNROLL - 1:
                        expert, slot, used = tile_values(t + 1)
                    for a in range(2):
                        pe.wait_ge(S["hidden_done"], times(t * 2 + a + 1))
                        pe.wait_ge(S["hT_lo_done"], times((t - 1) * 2 + a + 1))
                        for c in range(4):
                            ins = pe.transpose(ps_hT[:, a, P * c:P * c + P],
                                               hidden[:, HALF * a + P * c:HALF * a + P * c + P], ident[:, :])
                        ins.then_inc(S["h_turned"], 1)
            down(N_SLOT_TILE - 1, UNROLL - 1, slot_before, used_before)


_INS = ['x', 'ctx_1024', 'L0_xattn_W_proj', 'L0_xattn_b_proj', 'L0_ffn_Wg', 'L0_ffn_W1', 'L0_ffn_W3', 'L0_ffn_W2']


def kernel(**inputs):
    import numpy as _np
    import concourse.bacc as _bacc
    from concourse import mybir as _mybir
    from concourse.bass_utils import run_bass_kernel_spmd as _run

    nc = _bacc.Bacc("TRN2", target_bir_lowering=False, num_devices=1)
    arrays, args = {}, []
    for name in _INS:
        a = _np.ascontiguousarray(inputs[name])
        arrays[f"in_{name}_dram"] = a
        args.append(nc.dram_tensor(f"in_{name}_dram", a.shape, _mybir.dt.from_np(a.dtype), kind="ExternalInput").ap())
    out = nc.dram_tensor("out_0_dram", (N_TOK + PAD_ROWS, D), _mybir.dt.float32, kind="ExternalOutput").ap()
    xn_rows = nc.dram_tensor("xn_rows_dram", (N_TOK + PAD_ROWS, D + E), _mybir.dt.float32, kind="Internal").ap()
    attention_and_experts(nc, *args, out, xn_rows)
    r = _run(nc, [arrays], core_ids=[0])
    return r.results[0]["out_0_dram"][:N_TOK].reshape(B, T, D)
```
